# Optimizing a Trainium2 kernel written in Bass

```python
import numpy as np
import jax
import jax.numpy as jnp

def _softmax(x, axis=-1):
    return jax.nn.softmax(x, axis=axis)

def _gelu(x):
    return jax.nn.gelu(x, approximate=True)

def _silu(x):
    return jax.nn.silu(x)

def _sigmoid(x):
    return jax.nn.sigmoid(x)

def _layernorm(x, axis=-1, eps=1e-05):
    m = jnp.mean(x, axis=axis, keepdims=True)
    v = jnp.var(x, axis=axis, keepdims=True)
    return (x - m) / jnp.sqrt(v + eps)

def _scatter_add(tgt, idx, src, axis=0):
    return tgt.at[idx].add(src)

def _segment_sum(src, seg, n):
    return jax.ops.segment_sum(src, seg, n)
kernel_name = 'mk_lm_tower_d1_tok_ids512_r4_f72d2a'

def setup_inputs(seed: int=0):
    np.random.seed(seed)
    _w = jnp.asarray

    def _rec_inputs():
        import jax
        import jax.numpy as jnp
        _rk = jax.random.key(seed)
        x = jax.random.randint(jax.random.fold_in(_rk, 1), (32, 128), 0, 12564, jnp.int32)
        return x
    x = _rec_inputs()

    def _L0_tok_setup():
        import jax, jax.numpy as jnp
        import numpy as np
        EMBED_P = 0.1
        key = jax.random.key(seed)
        k1, k2, k3 = jax.random.split(key, 3)
        V, D, B, S = (50257, 128, 32, 128)
        words = jax.random.randint(k1, (B, S), 0, V, dtype=jnp.int64 if jax.config.jax_enable_x64 else jnp.int32)
        weight = jax.random.normal(k2, (V, D), dtype=jnp.float32)
        mask_u = jax.random.uniform(k3, (V, 1), dtype=jnp.float32)
        return {'words': words, 'weight': weight, 'mask_u': mask_u}
    _L0_tok_all = _L0_tok_setup()
    _L0_tok_in = {k: v for k, v in _L0_tok_all.items() if k in ('weight', 'mask_u')}
    del _L0_tok_all

    def _L0_attn_setup():
        import jax, jax.numpy as jnp
        import numpy as np
        H, KVH, HD, DN, DR = (8, 2, 64, 32, 32)
        EPS = 1e-06
        ROPE_BASE = 500000.0

        def _rms(x, w):
            return w * (x * jax.lax.rsqrt(jnp.mean(x * x, axis=-1, keepdims=True) + EPS))

        def _rope_tables(T):
            inv_freq = 1.0 / ROPE_BASE ** (np.arange(0, DR, 2, dtype=np.float32) / DR)
            freqs = np.outer(np.arange(T, dtype=np.float32), inv_freq)
            emb = np.concatenate([freqs, freqs], axis=-1)
            return (jnp.asarray(np.cos(emb)), jnp.asarray(np.sin(emb)))

        def _apply_rope(x, cos, sin):
            x1, x2 = jnp.split(x, 2, axis=-1)
            rot = jnp.concatenate([-x2, x1], axis=-1)
            return x * cos[None, None] + rot * sin[None, None]
        key = jax.random.key(seed)
        ks = jax.random.split(key, 10)
        std = 0.02
        mup = (256.0 / 512.0) ** 0.5
        return {'x': jax.random.normal(ks[0], (4, 512, 128), jnp.float32), 'W_DQ': jax.random.normal(ks[1], (128, 64), jnp.float32) * std, 'W_UQ': jax.random.normal(ks[2], (64, H * DN), jnp.float32) * std, 'W_QR': jax.random.normal(ks[3], (64, H * DR), jnp.float32) * std, 'W_DKV': jax.random.normal(ks[4], (128, 128), jnp.float32) * std, 'W_UK': jax.random.normal(ks[5], (128, KVH * DN), jnp.float32) * std, 'W_UV': jax.random.normal(ks[6], (128, KVH * HD), jnp.float32) * std, 'W_KR': jax.random.normal(ks[7], (128, KVH * DR), jnp.float32) * std, 'W_VR': jax.random.normal(ks[8], (128, H * HD), jnp.float32) * std * mup, 'W_O': jax.random.normal(ks[9], (H * HD, 128), jnp.float32) * std * mup, 'q_ln_w': jnp.ones((64,), jnp.float32), 'kv_ln_w': jnp.ones((128,), jnp.float32), 'q_head_norm_w': jnp.ones((HD,), jnp.float32), 'k_head_norm_w': jnp.ones((HD,), jnp.float32)}
    _L0_attn_all = _L0_attn_setup()
    _L0_attn_in = {k: v for k, v in _L0_attn_all.items() if k in ('W_DQ', 'W_UQ', 'W_QR', 'W_DKV', 'W_UK', 'W_UV', 'W_KR', 'W_VR', 'W_O', 'q_ln_w', 'kv_ln_w', 'q_head_norm_w', 'k_head_norm_w')}
    del _L0_attn_all

    def _L0_ffn_setup():
        import jax, jax.numpy as jnp
        import numpy as np
        D = 128
        E = 8
        K = 2
        EXP = 4
        LN_EPS = 1e-05
        key = jax.random.key(seed)
        ks = jax.random.split(key, 8)
        B, T = (8, 512)
        Dh = D * EXP
        x = jax.random.normal(ks[0], (B, T, D), dtype=jnp.float32)
        ln_g = jnp.ones((D,), dtype=jnp.float32)
        ln_b = jnp.zeros((D,), dtype=jnp.float32)
        lim_r = np.sqrt(6.0 / (D + E)).astype(np.float32)
        w_r = jax.random.uniform(ks[1], (E, D), dtype=jnp.float32, minval=-lim_r, maxval=lim_r)
        b_r = jnp.zeros((E,), dtype=jnp.float32)
        lim1 = np.sqrt(6.0 / (D + Dh)).astype(np.float32)
        W1 = jax.random.uniform(ks[2], (E, D, Dh), dtype=jnp.float32, minval=-lim1, maxval=lim1)
        b1 = jnp.zeros((E, Dh), dtype=jnp.float32)
        W2 = jax.random.uniform(ks[3], (E, Dh, D), dtype=jnp.float32, minval=-lim1, maxval=lim1)
        b2 = jnp.zeros((E, D), dtype=jnp.float32)
        return {'x': x, 'ln_g': ln_g, 'ln_b': ln_b, 'w_r': w_r, 'b_r': b_r, 'W1': W1, 'b1': b1, 'W2': W2, 'b2': b2}
    _L0_ffn_all = _L0_ffn_setup()
    _L0_ffn_in = {k: v for k, v in _L0_ffn_all.items() if k in ('ln_g', 'ln_b', 'w_r', 'b_r', 'W1', 'b1', 'W2', 'b2')}
    del _L0_ffn_all
    return {'x': x, 'L0_tok_weight': _L0_tok_in['weight'], 'L0_tok_mask_u': _L0_tok_in['mask_u'], 'L0_attn_W_DQ': _L0_attn_in['W_DQ'], 'L0_attn_W_UQ': _L0_attn_in['W_UQ'], 'L0_attn_W_QR': _L0_attn_in['W_QR'], 'L0_attn_W_DKV': _L0_attn_in['W_DKV'], 'L0_attn_W_UK': _L0_attn_in['W_UK'], 'L0_attn_W_UV': _L0_attn_in['W_UV'], 'L0_attn_W_KR': _L0_attn_in['W_KR'], 'L0_attn_W_VR': _L0_attn_in['W_VR'], 'L0_attn_W_O': _L0_attn_in['W_O'], 'L0_attn_q_ln_w': _L0_attn_in['q_ln_w'], 'L0_attn_kv_ln_w': _L0_attn_in['kv_ln_w'], 'L0_attn_q_head_norm_w': _L0_attn_in['q_head_norm_w'], 'L0_attn_k_head_norm_w': _L0_attn_in['k_head_norm_w'], 'L0_ffn_ln_g': _L0_ffn_in['ln_g'], 'L0_ffn_ln_b': _L0_ffn_in['ln_b'], 'L0_ffn_w_r': _L0_ffn_in['w_r'], 'L0_ffn_b_r': _L0_ffn_in['b_r'], 'L0_ffn_W1': _L0_ffn_in['W1'], 'L0_ffn_b1': _L0_ffn_in['b1'], 'L0_ffn_W2': _L0_ffn_in['W2'], 'L0_ffn_b2': _L0_ffn_in['b2']}

def reference(x, L0_tok_weight, L0_tok_mask_u, L0_attn_W_DQ, L0_attn_W_UQ, L0_attn_W_QR, L0_attn_W_DKV, L0_attn_W_UK, L0_attn_W_UV, L0_attn_W_KR, L0_attn_W_VR, L0_attn_W_O, L0_attn_q_ln_w, L0_attn_kv_ln_w, L0_attn_q_head_norm_w, L0_attn_k_head_norm_w, L0_ffn_ln_g, L0_ffn_ln_b, L0_ffn_w_r, L0_ffn_b_r, L0_ffn_W1, L0_ffn_b1, L0_ffn_W2, L0_ffn_b2):
    import jax
    import jax.numpy as jnp

    def _L0_tok_ref(words, weight, mask_u):
        import jax, jax.numpy as jnp
        import numpy as np
        EMBED_P = 0.1
        keep = (mask_u < 1.0 - EMBED_P).astype(weight.dtype)
        mask = keep / jnp.asarray(1.0 - EMBED_P, dtype=weight.dtype)
        masked_embed = weight * mask
        out = jnp.take(masked_embed, words, axis=0)
        return out

    def _L0_attn_ref(x, W_DQ, W_UQ, W_QR, W_DKV, W_UK, W_UV, W_KR, W_VR, W_O, q_ln_w, kv_ln_w, q_head_norm_w, k_head_norm_w):
        import jax, jax.numpy as jnp
        import numpy as np
        H, KVH, HD, DN, DR = (8, 2, 64, 32, 32)
        EPS = 1e-06
        ROPE_BASE = 500000.0

        def _rms(x, w):
            return w * (x * jax.lax.rsqrt(jnp.mean(x * x, axis=-1, keepdims=True) + EPS))

        def _rope_tables(T):
            inv_freq = 1.0 / ROPE_BASE ** (np.arange(0, DR, 2, dtype=np.float32) / DR)
            freqs = np.outer(np.arange(T, dtype=np.float32), inv_freq)
            emb = np.concatenate([freqs, freqs], axis=-1)
            return (jnp.asarray(np.cos(emb)), jnp.asarray(np.sin(emb)))

        def _apply_rope(x, cos, sin):
            x1, x2 = jnp.split(x, 2, axis=-1)
            rot = jnp.concatenate([-x2, x1], axis=-1)
            return x * cos[None, None] + rot * sin[None, None]
        B, T, D = x.shape
        cos, sin = _rope_tables(T)
        c_q = _rms(x @ W_DQ, q_ln_w)
        q_nope = (c_q @ W_UQ).reshape(B, T, H, DN).transpose(0, 2, 1, 3)
        q_rope = (c_q @ W_QR).reshape(B, T, H, DR).transpose(0, 2, 1, 3)
        c_kv = _rms(x @ W_DKV, kv_ln_w)
        k_nope = (c_kv @ W_UK).reshape(B, T, KVH, DN).transpose(0, 2, 1, 3)
        v = (c_kv @ W_UV).reshape(B, T, KVH, HD).transpose(0, 2, 1, 3)
        k_rope = (x @ W_KR).reshape(B, T, KVH, DR).transpose(0, 2, 1, 3)
        q_rope = _apply_rope(q_rope, cos, sin)
        k_rope = _apply_rope(k_rope, cos, sin)
        q = jnp.concatenate([q_nope, q_rope], axis=-1)
        k = jnp.concatenate([k_nope, k_rope], axis=-1)
        q = _rms(q, q_head_norm_w)
        k = _rms(k, k_head_norm_w)
        g = H // KVH
        k = jnp.repeat(k, g, axis=1)
        v = jnp.repeat(v, g, axis=1)
        scores = jnp.einsum('bhqd,bhkd->bhqk', q, k) * HD ** (-0.5)
        mask = jnp.tril(jnp.ones((T, T), dtype=bool))
        scores = jnp.where(mask, scores, -jnp.inf)
        attn_w = jax.nn.softmax(scores.astype(jnp.float32), axis=-1).astype(q.dtype)
        attn_out = jnp.einsum('bhqk,bhkd->bhqd', attn_w, v)
        v_res = (x @ W_VR).reshape(B, T, H, HD).transpose(0, 2, 1, 3)
        attn_out = attn_out + v_res
        out = attn_out.transpose(0, 2, 1, 3).reshape(B, T, H * HD)
        return out @ W_O

    def _L0_ffn_ref(x, ln_g, ln_b, w_r, b_r, W1, b1, W2, b2):
        import jax, jax.numpy as jnp
        import numpy as np
        D = 128
        E = 8
        K = 2
        EXP = 4
        LN_EPS = 1e-05
        B, T, d = x.shape
        mu = jnp.mean(x, axis=-1, keepdims=True)
        var = jnp.mean(jnp.square(x - mu), axis=-1, keepdims=True)
        h = (x - mu) * jax.lax.rsqrt(var + LN_EPS) * ln_g + ln_b
        logits = jnp.einsum('btd,ed->bte', h, w_r) + b_r
        topk_vals, topk_idx = jax.lax.top_k(logits, K)
        gates = jax.nn.softmax(topk_vals, axis=-1)
        hf = h.reshape(B * T, d)
        hid = jax.nn.gelu(jnp.einsum('nd,edf->nef', hf, W1) + b1, approximate=False)
        expert_stack = jnp.einsum('nef,efd->ned', hid, W2) + b2
        idx_flat = topk_idx.reshape(B * T, K)
        gates_flat = gates.reshape(B * T, K)
        gathered = jnp.take_along_axis(expert_stack, idx_flat[:, :, None], axis=1)
        mixed = jnp.sum(gathered * gates_flat[:, :, None], axis=1).reshape(B, T, d)
        return x + mixed
    h = _L0_tok_ref(x, L0_tok_weight, L0_tok_mask_u)
    h = h + _L0_attn_ref(_layernorm(h, axis=-1), L0_attn_W_DQ, L0_attn_W_UQ, L0_attn_W_QR, L0_attn_W_DKV, L0_attn_W_UK, L0_attn_W_UV, L0_attn_W_KR, L0_attn_W_VR, L0_attn_W_O, L0_attn_q_ln_w, L0_attn_kv_ln_w, L0_attn_q_head_norm_w, L0_attn_k_head_norm_w)
    h = h + _L0_ffn_ref(_layernorm(h, axis=-1), L0_ffn_ln_g, L0_ffn_ln_b, L0_ffn_w_r, L0_ffn_b_r, L0_ffn_W1, L0_ffn_b1, L0_ffn_W2, L0_ffn_b2)
    return h

_drawn_inputs = setup_inputs


def setup_inputs(seed=0):
    import zlib

    import numpy as np

    out = dict(_drawn_inputs(seed))
    spreads = {'L0_attn_q_ln_w': (1.0, 0.6),
     'L0_attn_kv_ln_w': (1.0, 0.2),
     'L0_attn_q_head_norm_w': (1.0, 0.6),
     'L0_attn_k_head_norm_w': (1.0, 0.6),
     'L0_ffn_ln_g': (1.0, 0.2),
     'L0_ffn_ln_b': (0.0, 0.1),
     'L0_ffn_b_r': (0.0, 0.1),
     'L0_ffn_b1': (0.0, 0.269),
     'L0_ffn_b2': (0.0, 0.1)}
    factors = {'L0_attn_W_DQ': 2.899,
     'L0_attn_W_UQ': 3.36,
     'L0_attn_W_QR': 3.568,
     'L0_attn_W_UK': 3.345,
     'L0_attn_W_KR': 4.027}
    for name, (base, spread) in spreads.items():
        noise = np.random.default_rng([zlib.crc32(name.encode()), seed]).standard_normal(out[name].shape)
        drawn = base * np.exp(spread * noise) if base else spread * noise
        out[name] = jnp.asarray(drawn.astype(out[name].dtype))
    for name, factor in factors.items():
        out[name] = (out[name] * factor).astype(out[name].dtype)
    return out
```

```python
from contextlib import ExitStack, contextmanager

import numpy as np

import concourse.bass as bass
from concourse import mybir

F32 = mybir.dt.float32
BF16 = mybir.dt.bfloat16
I32 = mybir.dt.int32
U32 = mybir.dt.uint32
ALU = mybir.AluOpType
ACT = mybir.ActivationFunctionType
AX = mybir.AxisListType

P = 128
H, KVH, HD, DN, DR = 8, 2, 64, 32, 32
HK = H + KVH
G = H // KVH
RMS_EPS = 1e-6
LN_EPS = 1e-5
KEEP = 0.9
MASKED = -1e30
E = 8
UNROLL = 4

TILE_SEMS = (
    "keep", "h0", "h0_kept", "ln1_stats", "ln1_mv", "ln1_x", "ln1_log", "ln1_exp", "ln1_n1", "ln1_n2",
    "rstd1", "xn", "xnT_ps", "xnT", "proj", "squares", "kv_x", "q_sum", "k_sum", "head_x", "head_log", "head_exp",
    "head_n1", "head_n2", "head_rs", "kn_scale", "q_nope", "k_nope", "rope_hi", "rope", "q_rope", "v", "qT_ps",
    "qT", "kT_ps", "kT", "scores", "neg_max", "probs", "inv_sum", "probs_half", "probs_n", "pT_ps", "pT", "oT_ps",
    "oT", "attn", "h1", "ln2_stats", "ln2_mv", "ln2_v", "ln2_inv", "ln2_x", "ln2_log", "ln2_exp", "ln2_n1",
    "ln2_n2", "rstd2", "xn2", "hn_t", "hn", "res", "hnT_ps", "hnT", "logits_ps", "logits", "top", "top_idx",
    "top_f", "pick", "gap", "mix1", "mixed", "out",
)
BLOCK_SEMS = ("xsT_ps", "xsT", "w1_copy", "hid_ps", "hid", "y_ps", "y")
OTHER_SEMS = (
    "words_in", "latent_in", "up_in", "cols_in", "wo_in", "rows_in", "vec_in", "vec2_in", "w1_in", "w2_in", "b2_in",
    "ones", "ident0", "ident", "const0", "consts", "zeroed", "words_f", "wordsT_ps", "words_i", "prep_pe", "prep_v",
    "route_pick", "route_pe", "route_v", "sort0", "sort1", "pos", "scattered0", "scattered1", "gate_exp", "gate1", "gate2", "gates",
)
PREP_LATENT, PREP_WVR, PREP_ALL = 6, 9, 13


def attention_and_experts_kernel(nc, x, emb, mask_u, W_DQ, W_UQ, W_QR, W_DKV, W_UK, W_UV, W_KR, W_VR, W_O,
                                 q_ln_w, kv_ln_w, q_hn_w, k_hn_w, ln_g, ln_b, w_r, b_r, W1, b1, W2, b2,
                                 rope_table, out):
    NT, T = x.shape
    D = emb.shape[1]
    F = W1.shape[2]
    FC = F // P
    RQ = W_DQ.shape[1]
    assert T == P and D == P and RQ == HD and W_DKV.shape[1] == P
    PARTS = (24, NT - 24)
    FIRST_TILE = (0, PARTS[0])
    BLOCKS = tuple(-(-(2 * n + E - 1) // UNROLL) * UNROLL for n in PARTS)
    FIRST_BLOCK = (0, BLOCKS[0])
    NB = sum(BLOCKS)
    ZROWS = 8 * P
    ZEROING = NB * P // ZROWS
    assert all(n * P % ZROWS == 0 for n in BLOCKS)

    C_V = HK * HD
    C_CQ = C_V + P
    C_CKV = C_CQ + RQ
    C_END = C_CKV + P

    sorted_x = [nc.dram_tensor(f"sorted_x{k}", (n * P, D), F32).ap() for k, n in enumerate(BLOCKS)]
    sorted_y = [nc.dram_tensor(f"sorted_y{k}", (n * P, D), F32).ap() for k, n in enumerate(BLOCKS)]

    with ExitStack() as ctx:
        def sb(name, shape, dt=F32):
            return ctx.enter_context(nc.sbuf_tensor(name, shape, dt))

        def ps(name, cols):
            return ctx.enter_context(nc.psum_tensor(name, [P, cols], F32))

        s = {name: ctx.enter_context(nc.semaphore(name)) for name in TILE_SEMS + BLOCK_SEMS + OTHER_SEMS}
        row_in = [ctx.enter_context(nc.semaphore(f"row_in{k}")) for k in range(UNROLL)]
        u_in = [ctx.enter_context(nc.semaphore(f"u_in{k}")) for k in range(UNROLL)]
        xs_in = [ctx.enter_context(nc.semaphore(f"xs_in{k}")) for k in range(UNROLL)]
        y_out = [ctx.enter_context(nc.semaphore(f"y_out{k}")) for k in range(UNROLL)]
        y1_in = [ctx.enter_context(nc.semaphore(f"y1_in{k}")) for k in range(UNROLL)]
        y2_in = [ctx.enter_context(nc.semaphore(f"y2_in{k}")) for k in range(UNROLL)]

        pj = ps("pj", 1024)
        sc = ps("sc", 1024)
        pt = ps("pt", 1024)
        qo = ps("qo", 512)
        ms = ps("ms", 512)

        ident = sb("ident_f", [P, P])
        ident_b = sb("ident_b", [P, P], BF16)
        causal = sb("causal", [P, G * P], BF16)
        before = sb("before", [P, P], BF16)
        ones_b = sb("ones_b", [P, P], BF16)
        iota_e = sb("iota_e", [P, E])
        iota_b = sb("iota_b", [P, BLOCKS[0]])
        ones_f = sb("ones_f", [P, E * PARTS[0]])
        zero = sb("zero", [P, ZROWS // P * D])
        rope_sb = sb("rope_sb", [P, 2 * DR])
        cos = rope_sb[:, 0:DR]
        sin = rope_sb[:, DR:2 * DR]
        w_proj = sb("w_proj", [P, C_END])
        w_res = sb("w_res", [P, P])
        wo = sb("wo", [P, G, P])
        wr = sb("wr", [P, P])
        qk_w = sb("qk_w", [P, 1])
        g_col = sb("g_col", [P, 1])
        b_col = sb("b_col", [P, 1])
        br_bc = sb("br_bc", [P, E])
        w1 = sb("w1", [P, E * F])
        w2 = sb("w2", [P, E * FC * P])
        b1c = sb("b1c", [P, E * FC])
        b2_bc = sb("b2_bc", [P, E * D])
        words = sb("words", [NT, P], I32)
        words_f = sb("words_f32", [NT, P])
        words_T = sb("words_T", [P, NT], U32)

        res = sb("res_all", [P, NT, D])
        hn = sb("hn_all", [P, NT, D])
        pick = sb("pick_all", [P, 2, E, NT])
        gap = sb("gap_all", [P, NT])
        gate_e = sb("gate_e", [P, NT])
        gates = sb("gates_all", [P, 2, NT])
        pos = sb("pos_all", [P, 2, NT], U32)
        block_e = sb("block_e", [1, NB], I32)

        U = UNROLL
        row = sb("row", [P, U, D])
        uval = sb("uval", [P, U])
        keep = sb("keep_b", [P, U])
        st1 = sb("st1", [P, U, 6])
        mv1 = sb("mv1", [P, U, 2])
        x1 = sb("x1", [P, U, 1])
        h0 = sb("h0_b", [P, U, D])
        rs1 = sb("rs1", [P, U, 5])
        xn = sb("xn_b", [P, U, D])
        xnT = sb("xnT_b", [P, U, P])
        sq = sb("sq", [P, 2, C_V])
        sq_lat = sb("sq_lat", [P, 2, P])
        sq_latq = sb("sq_latq", [P, 2, RQ])
        ss_lat = sb("ss_lat", [P, 2, 2])
        ss = sb("ss", [P, 2, 2 * HK])
        hx = sb("hx", [P, 2, HK + 1])
        hw = sb("hw", [P, 2, 5, HK + 1])
        small = sb("small", [P, 2, 16])
        rope_a = sb("rope_a", [P, 2, HK, DR])
        rope_b = sb("rope_bb", [P, 2, HK, DR])
        rope_c = sb("rope_cc", [P, 2, HK, DR])
        qh = sb("qh", [P, 2, HK, HD])
        vt = sb("vt", [P, U, P])
        qT = sb("qT_b", [P, 2, G, P])
        kT = sb("kT_b", [P, 2, P])
        nmax = sb("nmax", [P, 2, H])
        lsum = sb("lsum", [P, 2, H])
        linv = sb("linv", [P, 2, H])
        prob = sb("prob", [P, 2, H * P])
        probn = sb("probn", [P, 2, H * P])
        pT = sb("pT_b", [P, 2, H * P])
        oT = sb("oT_b", [P, 2, G, P])
        h1 = sb("h1_b", [P, 2, D])
        st2 = sb("st2", [P, 2, 6])
        mv2 = sb("mv2", [P, 2, 2])
        x2 = sb("x2", [P, 2, 4])
        rs2 = sb("rs2", [P, 2, 5, 2])
        xn2 = sb("xn2_b", [P, 2, D])
        hn_t = sb("hn_t", [P, 2, D])
        hnT = sb("hnT_b", [P, 2, P])
        logit = sb("logit", [P, 2, E])
        top = sb("top_b", [P, 2, E])
        top_i = sb("top_i", [P, 2, E], U32)
        top_f = sb("top_fb", [P, 2, 2])

        xs = sb("xs", [P, U, D])
        xsT = sb("xsT_b", [P, 2, P])
        w1s = sb("w1s", [P, 2, F])
        b1s = sb("b1s", [P, 2, FC])
        hid = sb("hid_b", [P, 2, FC, P])
        ysb = sb("ysb", [P, U, D])
        y1 = sb("y1", [P, U, D])
        y2 = sb("y2", [P, U, D])

        wdq = sb("wdq", [P, RQ])
        wdkv = sb("wdkv", [P, P])
        wuq = sb("wuq", [RQ, 2, H * DN])
        wukv = sb("wukv", [P, KVH * DN + KVH * HD])
        wvr = sb("wvr", [P, G, KVH, HD])
        wvrT = sb("wvrT", [P, G, P])
        wdqT = sb("wdqT", [RQ, P])
        wdkvT = sb("wdkvT", [P, P])
        wuq_s = sb("wuq_s", [RQ, H, HD])
        wukv_s = sb("wukv_s", [P, KVH * DN + KVH * HD])
        qln = sb("qln", [RQ, 1])
        kvln = sb("kvln", [P, 1])
        hn_w = sb("hn_w", [P, 2])
        wr_rows = sb("wr_rows", [E, P])
        b1_rows = sb("b1_rows", [E * FC, P])

        NR = E * PARTS[0]
        r_pick = sb("r_pick", [P, NR], BF16)
        r_cnt = sb("r_cnt", [P, NR])
        r_run = sb("r_run", [P, NR])
        r_rank = sb("r_rank", [P, NR])
        r_pos = sb("r_pos", [P, NR])
        r_sel = sb("r_sel", [P, 2, NR])
        r_posf = sb("r_posf", [P, 2, PARTS[0]])
        r_small = sb("r_small", [P, 8, E])
        r_int = sb("r_int", [P, 2, E], I32)
        r_cmp = sb("r_cmp", [P, BLOCKS[0], E])
        r_blk = sb("r_blk", [P, 2, BLOCKS[0]])

        def heads(ap):
            return ap.rearrange("p (h d) -> p h d", d=HD)

        def bc(ap, n):
            k = ap.shape[-1]
            return ap.unsqueeze(2).to_broadcast([P, k, n])

        def over_heads(ap, n):
            k = ap.shape[-1]
            return ap.unsqueeze(1).to_broadcast([P, n, k])

        def reused(eng, sem, i, depth=2):
            if not (isinstance(i, int) and i < depth):
                eng.wait_ge(s[sem], i - (depth - 1))

        def active(step, lag):
            return not isinstance(step, int) or 0 <= step - lag < NT

        def apart(eng):
            eng.wait_ge(s["ident"], 1)

        LN1, PROJ, SCORE, SOFT, OUT, FIN, ROUTE = range(7)
        AHEAD = 2
        LOOP_A = (8, 28)
        STEPS_A = NT + ROUTE
        SORT0 = PARTS[0] + ROUTE

        @contextmanager
        def groups(eng, first, end):
            with eng.Fori(0, (end - first) // U) as k:
                yield eng.snap(k * U + first)

        def active(st, lag):
            return not isinstance(st, int) or 0 <= st - lag < NT

        def steps_a(eng, body, sort):
            for st in range(LOOP_A[0]):
                body(st, st % U)
            with groups(eng, LOOP_A[0], LOOP_A[1]) as st:
                for u in range(U):
                    body(st + u, u)
            for st in range(LOOP_A[1], STEPS_A):
                if st == SORT0:
                    sort(0)
                body(st, st % U)
            sort(1)

        FFN1, FFN2 = 1, 2
        STEPS_C = NB + FFN2
        MIX0 = FIRST_BLOCK[1] + U

        def within(t, lag):
            return not isinstance(t, int) or 0 <= t - lag < NB

        def turn(t, u):
            return 16 * (t // U) if isinstance(t, int) else (t - u) * (16 // U)

        block = ctx.enter_context(nc.Block())

        @block.gpsimd
        def _(pool):
            pool.memset(ident[:], 0.0).then_inc(s["ident0"], 1)
            pool.wait_ge(s["ident0"], 1)
            pool.affine_select(out=ident[:], in_=ident[:], compare_op=ALU.not_equal, fill=1.0, base=0,
                               pattern=[[-1, P]], channel_multiplier=1).then_inc(s["ident"], 1)

            def gather(i, u):
                reused(pool, "h0", i, U)
                pool.indirect_dma_start(row[:, u, :], None, emb, bass.IndirectOffsetOnAxis(
                    ap=words_T[:, i:i + 1], axis=0)).then_inc(row_in[u], 16)
                pool.indirect_dma_start(uval[:, u:u + 1], None, mask_u, bass.IndirectOffsetOnAxis(
                    ap=words_T[:, i:i + 1], axis=0)).then_inc(u_in[u], 16)

            pool.wait_ge(s["words_i"], 1)
            for i in range(AHEAD):
                gather(i, i % U)

            pool.memset(ident_b[:], 0.0).then_inc(s["const0"], 1)
            pool.memset(causal[:], 0.0).then_inc(s["const0"], 1)
            pool.memset(before[:], 1.0).then_inc(s["const0"], 1)
            pool.wait_ge(s["const0"], 3)
            pool.affine_select(out=ident_b[:], in_=ident_b[:], compare_op=ALU.not_equal, fill=1.0, base=0,
                               pattern=[[-1, P]], channel_multiplier=1).then_inc(s["consts"], 1)
            pool.affine_select(out=causal[:].rearrange("p (g k) -> p g k", g=G),
                               in_=causal[:].rearrange("p (g k) -> p g k", g=G), compare_op=ALU.is_ge, fill=MASKED,
                               base=0, pattern=[[0, G], [-1, P]], channel_multiplier=1).then_inc(s["consts"], 1)
            pool.affine_select(out=before[:], in_=before[:], compare_op=ALU.is_gt, fill=0.0, base=0,
                               pattern=[[1, P]], channel_multiplier=-1).then_inc(s["consts"], 1)
            pool.iota(iota_e[:], pattern=[[1, E]], base=0, channel_multiplier=0,
                      allow_small_or_imprecise_dtypes=True).then_inc(s["consts"], 1)
            pool.iota(iota_b[:], pattern=[[1, BLOCKS[0]]], base=0, channel_multiplier=0,
                      allow_small_or_imprecise_dtypes=True).then_inc(s["consts"], 1)

            def scatter(part, lo, hi):
                pool.wait_ge(s["pos"], part + 1)
                pool.wait_ge(s["zeroed"], 16 * ZEROING)
                pool.wait_ge(s["hn"], FIRST_TILE[part] + PARTS[part])
                for i in range(lo, hi):
                    for k in range(2):
                        pool.indirect_dma_start(sorted_x[part], bass.IndirectOffsetOnAxis(ap=pos[:, k, i:i + 1], axis=0),
                                                hn[:, i, :], None).then_inc(s[f"scattered{part}"], 16)

            per_step = -(-PARTS[0] // (STEPS_A - SORT0))

            def step(st, u):
                if st + AHEAD < NT:
                    gather(st + AHEAD, (u + AHEAD) % U)
                if active(st, SOFT):
                    i, b = st - SOFT, (u - SOFT) % 2
                    pool.wait_ge(s["inv_sum"], i + 1)
                    reused(pool, "pT_ps", i)
                    for half, done in ((0, "probs_half"), (1, "probs_n")):
                        c = slice(half * G * P, (half + 1) * G * P)
                        pool.tensor_tensor(probn[:, b, c].rearrange("p (h k) -> p h k", k=P),
                                           prob[:, b, c].rearrange("p (h k) -> p h k", k=P),
                                           bc(linv[:, b, half * G:(half + 1) * G], P), ALU.mult).then_inc(s[done], 1)
                if active(st, FIN):
                    i, b = st - FIN, (u - FIN) % 2
                    pool.wait_ge(s["xn2"], i + 1)
                    pool.tensor_tensor(res[:, bass.ds(i, 1), :], h1[:, b:b + 1, :], xn2[:, b:b + 1, :],
                                       ALU.add).then_inc(s["res"], 1)
                if active(st, PROJ):
                    i, b = st - PROJ, (u - PROJ) % 2
                    pool.wait_ge(s["rope_hi"], i + 1)
                    pool.tensor_tensor(rope_c[:, b], rope_a[:, b], rope_b[:, b], ALU.add).then_inc(s["rope"], 1)
                    pool.wait_ge(s["rope"], i + 1)
                    pool.wait_ge(s["head_rs"], i + 1)
                    reused(pool, "kT_ps", i)
                    pool.tensor_tensor(qh[:, b, :, DN:HD], rope_c[:, b], bc(hw[:, b, 4, 0:HK], DR),
                                       ALU.mult).then_inc(s["q_rope"], 1)
                if st >= SORT0:
                    d = st - SORT0
                    scatter(0, d * per_step, min((d + 1) * per_step, PARTS[0]))

            for st in range(STEPS_A):
                step(st, st % U)
            scatter(1, FIRST_TILE[1], NT)

            def fetch(part, i, u):
                reused(pool, "mixed", i, U)
                pool.indirect_dma_start(y1[:, u, :], None, sorted_y[part], bass.IndirectOffsetOnAxis(
                    ap=pos[:, 0, i:i + 1], axis=0)).then_inc(y1_in[u], 16)
                pool.indirect_dma_start(y2[:, u, :], None, sorted_y[part], bass.IndirectOffsetOnAxis(
                    ap=pos[:, 1, i:i + 1], axis=0)).then_inc(y2_in[u], 16)

            for part in range(2):
                for u in range(U):
                    pool.wait_ge(y_out[u], 16 * (FIRST_BLOCK[part] + BLOCKS[part]) // U)
                for i in range(FIRST_TILE[part], FIRST_TILE[part] + PARTS[part]):
                    fetch(part, i, i % U)

        @block.sync
        def _(sp):
            sp.dma_start(words[:], x).then_inc(s["words_in"], 16)
            sp.dma_start(wdq[:], W_DQ).then_inc(s["latent_in"], 16)
            sp.dma_start(wdkv[:], W_DKV).then_inc(s["latent_in"], 16)
            sp.dma_start(wuq[:, 0, :], W_UQ).then_inc(s["up_in"], 16)
            sp.dma_start(wuq[:, 1, :], W_QR).then_inc(s["up_in"], 16)
            sp.dma_start(wukv[:, 0:KVH * DN], W_UK).then_inc(s["up_in"], 16)
            sp.dma_start(wukv[:, KVH * DN:], W_UV).then_inc(s["up_in"], 16)
            for g in range(KVH):
                sp.dma_start(w_proj[:, (H + g) * HD + DN:(H + g + 1) * HD],
                             W_KR[:, g * DR:(g + 1) * DR]).then_inc(s["cols_in"], 16)
            sp.dma_start(w_proj[:, C_CQ:C_CKV], W_DQ).then_inc(s["cols_in"], 16)
            sp.dma_start(w_proj[:, C_CKV:C_END], W_DKV).then_inc(s["cols_in"], 16)
            for g in range(KVH):
                sp.dma_start(wvr[:, :, g, :],
                             W_VR[:, g * G * HD:(g + 1) * G * HD].rearrange("k (c d) -> k c d", c=G)
                             ).then_inc(s["wo_in"], 16)
                sp.dma_start(wo[g * HD:(g + 1) * HD],
                             W_O[g * G * HD:(g + 1) * G * HD, :].rearrange("(c d) n -> d c n", c=G)
                             ).then_inc(s["wo_in"], 16)
            sp.dma_start(w1[:].rearrange("p (e f) -> p e f", e=E), W1.rearrange("e d f -> d e f")).then_inc(s["w1_in"], 16)
            sp.dma_start(w2[:].rearrange("p (e c d) -> p e c d", e=E, c=FC),
                         W2.rearrange("e (c p) d -> p e c d", p=P)).then_inc(s["w2_in"], 16)
            sp.dma_start(b2_bc[:], b2.rearrange("e d -> (e d)").partition_broadcast(P)).then_inc(s["b2_in"], 16)

            sp.wait_ge(s["ones"], 1)
            for part in range(2):
                with sp.Fori(0, BLOCKS[part] * P // ZROWS) as z:
                    sp.dma_start(sorted_x[part][bass.ds(z * ZROWS, ZROWS), :].rearrange("(p r) d -> p (r d)", p=P),
                                 zero[:]).then_inc(s["zeroed"], 16)

            STORE = 6
            PUT = MIX0 + 2 * U

            def put(i):
                sp.wait_ge(s["mixed"], i + 1)
                sp.dma_start(out[bass.ds(i, 1)].rearrange("a t d -> t a d"),
                             res[:, bass.ds(i, 1), :]).then_inc(s["out"], 16)

            def rows(buffers, part, n):
                return buffers[part][bass.ds((n - FIRST_BLOCK[part]) * P, P), :]

            def step(t, u, part=None):
                if within(t, 0):
                    reused(sp, "xsT_ps", t, U)
                    k = part if part is not None else int(t >= FIRST_BLOCK[1])
                    sp.dma_start(xs[:, u, :], rows(sorted_x, k, t)).then_inc(xs_in[u], 16)
                if within(t, STORE):
                    n, b4 = t - STORE, (u - STORE) % U
                    sp.wait_ge(s["y"], n + 1)
                    k = part if part is not None else int(n >= FIRST_BLOCK[1])
                    sp.dma_start(rows(sorted_y, k, n), ysb[:, b4, :]).then_inc(y_out[b4], 16)

            sp.wait_ge(s["scattered0"], 16 * 2 * PARTS[0])
            for t in range(2 * U):
                step(t, t % U)
            with groups(sp, 2 * U, FIRST_BLOCK[1]) as t:
                for u in range(U):
                    step(t + u, u, 0)
            sp.wait_ge(s["scattered1"], 16 * 2 * PARTS[1])
            for t in range(FIRST_BLOCK[1], PUT):
                step(t, t % U)
            with groups(sp, PUT, NB) as t:
                for u in range(U):
                    step(t + u, u, 1)
                    put(t + (u - PUT))
            for t in range(NB, NB + STORE):
                step(t, t % U)
            with sp.Fori(NB - PUT, NT) as i:
                put(i)
            sp.wait_ge(s["out"], 16 * NT)

        @block.tensor
        def _(pe):
            pe.wait_ge(s["ident"], 1)
            pe.wait_ge(s["words_f"], 1)
            pe.transpose(ms[:, 0:NT], words_f[:], ident[0:NT, 0:NT]).then_inc(s["wordsT_ps"], 1)

            pe.wait_ge(s["latent_in"], 32)
            pe.transpose(qo[0:RQ, 0:P], wdq[:], ident[:])
            pe.transpose(qo[:, P:2 * P], wdkv[:], ident[:]).then_inc(s["prep_pe"], 1)
            pe.wait_ge(s["rows_in"], 32)
            pe.transpose(sc[:, 0:E], wr_rows[:], ident[0:E, 0:E])
            pe.transpose(sc[:, P:P + E * FC], b1_rows[:], ident[0:E * FC, 0:E * FC]).then_inc(s["prep_pe"], 1)
            pe.wait_ge(s["prep_v"], PREP_LATENT)
            pe.matmul(pj[:, 0:H * HD], wdqT[:], wuq_s[:].rearrange("p h d -> p (h d)"), start=True, stop=True)
            pe.matmul(pj[:, H * HD:H * HD + KVH * (DN + HD)], wdkvT[:], wukv_s[:], start=True,
                      stop=True).then_inc(s["prep_pe"], 1)
            pe.wait_ge(s["wo_in"], 16 * 2 * KVH)
            for c in range(G):
                last = pe.transpose(pt[:, c * P:(c + 1) * P], wvr[:, c].rearrange("p g d -> p (g d)"), ident[:])
            last.then_inc(s["prep_pe"], 1)
            pe.wait_ge(s["prep_v"], PREP_WVR)
            for c in range(G):
                last = pe.matmul(ms[:, P:2 * P], wvrT[:, c, :], wo[:, c, :], start=(c == 0), stop=(c == G - 1))
            last.then_inc(s["prep_pe"], 1)
            pe.wait_ge(s["prep_v"], PREP_ALL)
            pe.wait_ge(s["consts"], 5)
            pe.wait_ge(s["cols_in"], 64)

            def step(st, u):
                if active(st, SCORE):
                    i, b = st - SCORE, (u - SCORE) % 2
                    pe.wait_ge(s["q_nope"], i + 1)
                    pe.wait_ge(s["q_rope"], i + 1)
                    if active(st, OUT + 1):
                        pe.wait_ge(s["oT"], st - OUT)
                    for c in range(G):
                        last = pe.transpose(qo[:, c * P:(c + 1) * P],
                                            qh[:, b, 2 * c:2 * c + 2, :].rearrange("p h d -> p (h d)"), ident[:])
                    last.then_inc(s["qT_ps"], 1)
                if active(st, PROJ):
                    i, b4 = st - PROJ, (u - PROJ) % U
                    pe.wait_ge(s["xn"], i + 1)
                    if active(st, FIN):
                        pe.wait_ge(s["h1"], st - FIN + 1)
                    if active(st, ROUTE):
                        pe.wait_ge(s["logits"], st - ROUTE + 1)
                    pe.transpose(ms[:, 0:P], xn[:, b4, :], ident[:]).then_inc(s["xnT_ps"], 1)
                if active(st, OUT):
                    i, b = st - OUT, (u - OUT) % 2
                    reused(pe, "pT", i, 1)
                    pe.wait_ge(s["probs_half"], i + 1)
                    for h in range(H):
                        if h == G:
                            pe.wait_ge(s["probs_n"], i + 1)
                        last = pe.transpose(pt[:, h * P:(h + 1) * P], probn[:, b, h * P:(h + 1) * P], ident[:])
                    last.then_inc(s["pT_ps"], 1)
                if active(st, SCORE):
                    i, b = st - SCORE, (u - SCORE) % 2
                    pe.wait_ge(s["q_nope"], i + 1)
                    if active(st, PROJ):
                        pe.wait_ge(s["xnT"], st - PROJ + 1)
                    else:
                        pe.wait_ge(s["logits"], st - ROUTE + 1)
                    pe.transpose(ms[:, P:2 * P], qh[:, b, H:HK, :].rearrange("p h d -> p (h d)"),
                                 ident[:]).then_inc(s["kT_ps"], 1)
                if active(st, PROJ):
                    i, b4 = st - PROJ, (u - PROJ) % U
                    pe.wait_ge(s["xnT"], i + 1)
                    reused(pe, "q_nope", i, 1)
                    reused(pe, "v", i, 1)
                    pe.matmul(pj[:, 0:512], xnT[:, b4, :], w_proj[:, 0:512], start=True, stop=True)
                    pe.matmul(pj[:, 512:C_END], xnT[:, b4, :], w_proj[:, 512:C_END], start=True,
                              stop=True).then_inc(s["proj"], 1)
                if active(st, SCORE):
                    i, b = st - SCORE, (u - SCORE) % 2
                    pe.wait_ge(s["qT"], i + 1)
                    pe.wait_ge(s["kT"], i + 1)
                    reused(pe, "probs", i, 1)
                    for g in range(KVH):
                        pe.matmul(sc[:, g * 512:(g + 1) * 512], ident_b[:], causal[:], start=True, stop=False,
                                  skip_group_check=True)
                    for c in range(G):
                        for g in range(KVH):
                            r = slice(g * HD, (g + 1) * HD)
                            at = g * 512 + c * P
                            last = pe.matmul(sc[:, at:at + P], qT[r, b, c, :], kT[r, b, :], start=False,
                                             stop=(c == G - 1), skip_group_check=True)
                    last.then_inc(s["scores"], 1)
                if active(st, OUT):
                    i, b, b4 = st - OUT, (u - OUT) % 2, (u - OUT) % U
                    pe.wait_ge(s["pT"], i + 1)
                    if active(st, SCORE):
                        pe.wait_ge(s["qT"], st - SCORE + 1)
                    else:
                        reused(pe, "oT", i, 1)
                    for g in range(KVH):
                        last = pe.matmul(qo[g * HD:(g + 1) * HD, :], vt[:, b4, g * HD:(g + 1) * HD],
                                         pT[:, b, g * 512:(g + 1) * 512], start=True, stop=True)
                    last.then_inc(s["oT_ps"], 1)
                if active(st, FIN):
                    i, b = st - FIN, (u - FIN) % 2
                    pe.wait_ge(s["hn_t"], i + 1)
                    if active(st, SCORE):
                        pe.wait_ge(s["kT"], st - SCORE + 1)
                    else:
                        pe.wait_ge(s["logits"], st - ROUTE + 1)
                    pe.transpose(ms[:, 2 * P:3 * P], hn_t[:, b, :], ident[:]).then_inc(s["hnT_ps"], 1)
                if active(st, OUT):
                    i, b, b4 = st - OUT, (u - OUT) % 2, (u - OUT) % U
                    pe.wait_ge(s["oT"], i + 1)
                    if active(st, FIN):
                        pe.wait_ge(s["hnT"], st - FIN + 1)
                    elif active(st, SCORE):
                        pe.wait_ge(s["kT"], st - SCORE + 1)
                    for c in range(G):
                        pe.matmul(ms[:, 3 * P:4 * P], oT[:, b, c, :], wo[:, c, :], start=(c == 0), stop=False)
                    pe.matmul(ms[:, 3 * P:4 * P], xnT[:, b4, :], w_res[:], start=False, stop=True).then_inc(s["attn"], 1)
                if active(st, FIN):
                    i, b = st - FIN, (u - FIN) % 2
                    pe.wait_ge(s["hnT"], i + 1)
                    pe.matmul(ms[:, 0:P], hnT[:, b, :], wr[:], start=True, stop=True).then_inc(s["logits_ps"], 1)

            def sort(part):
                n = E * PARTS[part]
                pe.wait_ge(s["route_pick"], part + 1)
                pe.wait_ge(s["oT"], (SORT0 - OUT, NT)[part])
                pe.matmul(qo[:, 0:n], before[:], r_pick[:, 0:n], start=True, stop=True)
                pe.matmul(qo[:, 256:256 + n], ones_b[:], r_pick[:, 0:n], start=True,
                          stop=True).then_inc(s["route_pe"], 1)
                pe.wait_ge(s["route_v"], part + 1)

            steps_a(pe, step, sort)

            def step_c(t, u):
                if within(t, 0):
                    pe.wait_ge(xs_in[u], turn(t, u) + 16)
                    reused(pe, "xsT", t)
                    tp = (qo, ms)[u % 2]
                    pe.transpose(tp[:, 0:P], xs[:, u, :], ident[:]).then_inc(s["xsT_ps"], 1)
                if within(t, FFN1):
                    n, b = t - FFN1, (u - FFN1) % 2
                    pe.wait_ge(s["xsT"], n + 1)
                    pe.wait_ge(s["w1_copy"], n + 1)
                    reused(pe, "hid", n)
                    for c in range(FC):
                        last = pe.matmul(pt[:, b * 512 + c * P:b * 512 + (c + 1) * P], w1s[:, b, c * P:(c + 1) * P],
                                         xsT[:, b, :], start=True, stop=True)
                    last.then_inc(s["hid_ps"], 1)
                if within(t, FFN2):
                    n, b = t - FFN2, (u - FFN2) % 2
                    e = pe.value_load(block_e[0:1, bass.ds(n, 1)], min_val=0, max_val=E - 1)
                    pe.wait_ge(s["hid"], n + 1)
                    reused(pe, "y", n)
                    for c in range(FC):
                        last = pe.matmul(pj[:, b * 512:b * 512 + P], hid[:, b, c, :],
                                         w2[:, bass.ds(e * (FC * P) + c * P, P)], start=(c == 0), stop=(c == FC - 1))
                    last.then_inc(s["y_ps"], 1)

            pe.wait_ge(s["w2_in"], 16)
            for done in ("logits", "q_nope", "v", "pT"):
                pe.wait_ge(s[done], NT)
            pe.wait_ge(s["pos"], 2)
            for t in range(U):
                step_c(t, t)
            with groups(pe, U, NB) as t:
                for u in range(U):
                    step_c(t + u, u)
            for t in range(NB, STEPS_C):
                step_c(t, t % U)

        @block.scalar
        def _(act):
            act.preload_act_table_set("natural_log_exp_and_others")
            act.dma_start(wr_rows[:], w_r).then_inc(s["rows_in"], 16)
            act.dma_start(b1_rows[:], b1.rearrange("e (c p) -> (e c) p", p=P)).then_inc(s["rows_in"], 16)

            def col(v):
                return v.rearrange("(p a) -> p a", a=1)

            act.dma_start(qln[:], col(q_ln_w)).then_inc(s["vec_in"], 16)
            act.dma_start(kvln[:], col(kv_ln_w)).then_inc(s["vec_in"], 16)
            for g in range(KVH):
                act.dma_start(hn_w[g * HD:(g + 1) * HD, 0:1], col(q_hn_w)).then_inc(s["vec_in"], 16)
                act.dma_start(hn_w[g * HD:(g + 1) * HD, 1:2], col(k_hn_w)).then_inc(s["vec_in"], 16)
            act.dma_start(rope_sb[:], rope_table).then_inc(s["vec2_in"], 16)
            act.dma_start(g_col[:], col(ln_g)).then_inc(s["vec2_in"], 16)
            act.dma_start(b_col[:], col(ln_b)).then_inc(s["vec2_in"], 16)
            act.dma_start(br_bc[:], b_r.partition_broadcast(P)).then_inc(s["vec2_in"], 16)

            def rsqrt_start(src, log, y, log_done, y_done, i):
                act.activation(log, src, ACT.Ln).then_inc(s[log_done], 1)
                act.wait_ge(s[log_done], i + 1)
                act.activation(y, log, ACT.Exp, scale=-0.5).then_inc(s[y_done], 1)

            def step(st, u):
                if active(st, SCORE):
                    i, b = st - SCORE, (u - SCORE) % 2
                    act.wait_ge(s["qT_ps"], i + 1)
                    reused(act, "scores", i)
                    act.copy(qT[:, b].rearrange("p c t -> p (c t)"), qo[:]).then_inc(s["qT"], 1)
                if active(st, PROJ):
                    i, b4 = st - PROJ, (u - PROJ) % U
                    act.wait_ge(s["xnT_ps"], i + 1)
                    reused(act, "attn", i, U)
                    act.copy(xnT[:, b4, :], ms[:, 0:P]).then_inc(s["xnT"], 1)
                if active(st, FIN):
                    i, b = st - FIN, (u - FIN) % 2
                    act.wait_ge(s["ln2_x"], i + 1)
                    rsqrt_start(x2[:, b, 0:2], rs2[:, b, 0, :], rs2[:, b, 1, :], "ln2_log", "ln2_exp", i)
                if active(st, SOFT):
                    i, b = st - SOFT, (u - SOFT) % 2
                    act.wait_ge(s["neg_max"], i + 1)
                    reused(act, "probs_n", i)
                    for h in range(H):
                        last = act.activation(prob[:, b, h * P:(h + 1) * P], sc[:, h * P:(h + 1) * P], ACT.Exp,
                                              bias=nmax[:, b, h:h + 1], accum_out=lsum[:, b, h:h + 1])
                    last.then_inc(s["probs"], 1)
                if active(st, OUT):
                    i, b = st - OUT, (u - OUT) % 2
                    act.wait_ge(s["pT_ps"], i + 1)
                    reused(act, "oT_ps", i)
                    act.copy(pT[:, b, :], pt[:]).then_inc(s["pT"], 1)
                if active(st, LN1):
                    i, b4 = st - LN1, (u - LN1) % U
                    act.wait_ge(s["ln1_x"], i + 1)
                    rsqrt_start(x1[:, b4, 0:1], rs1[:, b4, 0:1], rs1[:, b4, 1:2], "ln1_log", "ln1_exp", i)
                if active(st, PROJ):
                    i, b = st - PROJ, (u - PROJ) % 2
                    act.wait_ge(s["proj"], i + 1)
                    reused(act, "head_x", i)
                    act.activation(sq[:, b, :], pj[:, 0:C_V], ACT.Square)
                    act.activation(sq_latq[:, b, :], pj[:, C_CQ:C_CKV], ACT.Square, accum_out=ss_lat[:, b, 0:1])
                    act.activation(sq_lat[:, b, :], pj[:, C_CKV:C_END], ACT.Square,
                                   accum_out=ss_lat[:, b, 1:2]).then_inc(s["squares"], 1)
                if active(st, OUT):
                    i, b = st - OUT, (u - OUT) % 2
                    act.wait_ge(s["oT_ps"], i + 1)
                    reused(act, "attn", i)
                    act.copy(oT[:, b].rearrange("p c t -> p (c t)"), qo[:]).then_inc(s["oT"], 1)
                if active(st, FIN):
                    i, b = st - FIN, (u - FIN) % 2
                    act.wait_ge(s["hnT_ps"], i + 1)
                    act.activation(hnT[:, b, :], ms[:, 2 * P:3 * P], ACT.Identity, bias=b_col[:, 0:1],
                                   scale=g_col[:, 0:1]).then_inc(s["hnT"], 1)
                    act.copy(hn[:, bass.ds(i, 1), :], hn_t[:, b:b + 1, :]).then_inc(s["hn"], 1)
                if active(st, PROJ):
                    i, b, b4 = st - PROJ, (u - PROJ) % 2, (u - PROJ) % U
                    act.wait_ge(s["head_x"], i + 1)
                    rsqrt_start(hx[:, b, :], hw[:, b, 0, :], hw[:, b, 1, :], "head_log", "head_exp", i)
                    act.wait_ge(s["k_nope"], i + 1)
                    reused(act, "oT_ps", i, U)
                    act.activation(vt[:, b4, :], pj[:, C_V:C_CQ], ACT.Copy,
                                   scale=hw[:, b, 4, HK:HK + 1]).then_inc(s["v"], 1)

            act.wait_ge(s["vec2_in"], 64)
            steps_a(act, step, lambda part: None)

            for part in range(2):
                c = slice(FIRST_TILE[part], FIRST_TILE[part] + PARTS[part])
                act.wait_ge(s["route_pick"], part + 1)
                act.activation(gate_e[:, c], gap[:, c], ACT.Exp).then_inc(s["gate_exp"], 1)

            def step_c(t, u):
                if within(t, 0):
                    b = u % 2
                    act.wait_ge(s["xsT_ps"], t + 1)
                    reused(act, "hid_ps", t)
                    act.activation(xsT[:, b, :], (qo, ms)[b][:, 0:P], ACT.Identity, bias=b_col[:, 0:1],
                                   scale=g_col[:, 0:1]).then_inc(s["xsT"], 1)
                if within(t, FFN1):
                    n, b = t - FFN1, (u - FFN1) % 2
                    act.wait_ge(s["hid_ps"], n + 1)
                    reused(act, "y_ps", n)
                    for c in range(FC):
                        last = act.activation(hid[:, b, c, :], pt[:, b * 512 + c * P:b * 512 + (c + 1) * P], ACT.Gelu,
                                              bias=b1s[:, b, c:c + 1])
                    last.then_inc(s["hid"], 1)

            for t in range(U):
                step_c(t, t)
            with groups(act, U, NB) as t:
                for u in range(U):
                    step_c(t + u, u)
            for t in range(NB, STEPS_C):
                step_c(t, t % U)

        @block.vector
        def _(dve):
            def then(ins, sem, value):
                ins.then_inc(s[sem], 1)
                dve.wait_ge(s[sem], value)

            dve.wait_ge(s["words_in"], 16)
            dve.tensor_copy(words_f[:], words[:]).then_inc(s["words_f"], 1)
            dve.memset(zero[:], 0.0)
            dve.memset(ones_b[:], 1.0)
            dve.memset(ones_f[:], 1.0)
            dve.memset(wr[:], 0.0).then_inc(s["ones"], 1)
            dve.wait_ge(s["wordsT_ps"], 1)
            dve.tensor_copy(words_T[:], ms[:, 0:NT]).then_inc(s["words_i"], 1)

            dve.wait_ge(s["vec_in"], 16 * (2 + 2 * KVH))
            dve.wait_ge(s["up_in"], 64)
            for k in range(2):
                dve.tensor_scalar(wuq_s[:, :, k * DN:(k + 1) * DN].rearrange("k (c g) d -> k g c d", g=KVH),
                                  wuq[:, k, :].rearrange("k (g c d) -> k g c d", g=KVH, c=G), qln[:, 0:1], None,
                                  ALU.mult).then_inc(s["prep_v"], 1)
            dve.tensor_scalar(wukv_s[:], wukv[:], kvln[:, 0:1], None, ALU.mult).then_inc(s["prep_v"], 1)
            dve.tensor_scalar(qk_w[:], hn_w[:, 0:1], hn_w[:, 1:2], float(HD) ** -0.5, ALU.mult,
                              ALU.mult).then_inc(s["prep_v"], 1)
            dve.wait_ge(s["prep_pe"], 1)
            dve.tensor_copy(wdqT[:], qo[0:RQ, 0:P]).then_inc(s["prep_v"], 1)
            dve.tensor_copy(wdkvT[:], qo[:, P:2 * P]).then_inc(s["prep_v"], 1)
            dve.wait_ge(s["prep_pe"], 2)
            dve.wait_ge(s["ones"], 1)
            dve.tensor_copy(wr[:, 0:E], sc[:, 0:E]).then_inc(s["prep_v"], 1)
            dve.tensor_copy(b1c[:], sc[:, P:P + E * FC]).then_inc(s["prep_v"], 1)
            dve.wait_ge(s["prep_pe"], 4)
            dve.tensor_copy(wvrT[:].rearrange("p c n -> p (c n)"), pt[:, 0:512]).then_inc(s["prep_v"], 1)
            dve.tensor_copy(w_proj[:, 0:H * HD], pj[:, 0:H * HD]).then_inc(s["prep_v"], 1)
            dve.tensor_copy(heads(w_proj[:, H * HD:C_V])[:, :, 0:DN],
                            pj[:, H * HD:H * HD + KVH * DN].rearrange("p (g d) -> p g d", g=KVH)
                            ).then_inc(s["prep_v"], 1)
            dve.tensor_copy(w_proj[:, C_V:C_CQ], pj[:, H * HD + KVH * DN:H * HD + KVH * (DN + HD)]
                            ).then_inc(s["prep_v"], 1)
            dve.wait_ge(s["prep_pe"], 5)
            dve.tensor_copy(w_res[:], ms[:, P:2 * P]).then_inc(s["prep_v"], 1)
            dve.wait_ge(s["vec2_in"], 64)
            dve.wait_ge(s["consts"], 5)
            dve.wait_ge(s["prep_v"], PREP_ALL)

            def newton(x, y, work, out, n1, n2, done, i):
                w1_, w2_ = work
                then(dve.scalar_tensor_tensor(out=w1_, in0=y, scalar=-0.5, in1=y, op0=ALU.mult, op1=ALU.mult), n1, i + 1)
                then(dve.tensor_tensor(w2_, w1_, x, ALU.mult), n2, i + 1)
                dve.scalar_tensor_tensor(out=out, in0=w2_, scalar=1.5, in1=y, op0=ALU.add,
                                         op1=ALU.mult).then_inc(s[done], 1)

            def step(st, u):
                if active(st, FIN):
                    i, b = st - FIN, (u - FIN) % 2
                    dve.wait_ge(s["attn"], i + 1)
                    if active(st, ROUTE):
                        dve.wait_ge(s["logits_ps"], st - ROUTE + 1)
                    reused(dve, "res", i)
                    dve.wait_ge(s["h0_kept"], i + 1)
                    then(dve.tensor_tensor(h1[:, b:b + 1, :], res[:, bass.ds(i, 1), :],
                                           ms[:, 3 * P:4 * P].unsqueeze(1), ALU.add), "h1", i + 1)
                if active(st, ROUTE):
                    i, b = st - ROUTE, (u - ROUTE) % 2
                    dve.wait_ge(s["logits_ps"], i + 1)
                    dve.tensor_tensor(logit[:, b, :], ms[:, 0:E], br_bc[:], ALU.add).then_inc(s["logits"], 1)
                if active(st, FIN):
                    i, b = st - FIN, (u - FIN) % 2
                    dve.bn_stats(st2[:, b, :], h1[:, b, :]).then_inc(s["ln2_stats"], 1)
                    apart(dve)
                    dve.wait_ge(s["ln2_stats"], i + 1)
                    then(dve.bn_aggr(mv2[:, b, :], st2[:, b, :]), "ln2_mv", i + 1)
                    then(dve.tensor_scalar(x2[:, b, 0:1], mv2[:, b, 1:2], LN_EPS, None, ALU.add), "ln2_v", i + 1)
                    then(dve.reciprocal(x2[:, b, 2:3], x2[:, b, 0:1]), "ln2_inv", i + 1)
                    dve.tensor_scalar(x2[:, b, 1:2], mv2[:, b, 1:2], x2[:, b, 2:3], LN_EPS, ALU.mult,
                                      ALU.add).then_inc(s["ln2_x"], 1)
                if active(st, ROUTE):
                    i, b = st - ROUTE, (u - ROUTE) % 2
                    apart(dve)
                    dve.wait_ge(s["logits"], i + 1)
                    dve.max(top[:, b, :], logit[:, b, :]).then_inc(s["top"], 1)
                    apart(dve)
                    dve.wait_ge(s["top"], i + 1)
                    dve.max_index(top_i[:, b, :], top[:, b, :], logit[:, b, :]).then_inc(s["top_idx"], 1)
                    dve.tensor_scalar(gap[:, bass.ds(i, 1)], top[:, b, 1:2], top[:, b, 0:1], None,
                                      ALU.subtract).then_inc(s["gap"], 1)
                    dve.wait_ge(s["top_idx"], i + 1)
                    then(dve.tensor_copy(top_f[:, b, :], top_i[:, b, 0:2]), "top_f", i + 1)
                    for k in range(2):
                        dve.tensor_scalar(pick[:, k, :, bass.ds(i, 1)], iota_e[:].unsqueeze(2), top_f[:, b, k:k + 1],
                                          None, ALU.is_equal).then_inc(s["pick"], 1)
                if active(st, SCORE):
                    i, b = st - SCORE, (u - SCORE) % 2
                    dve.wait_ge(s["kT_ps"], i + 1)
                    reused(dve, "scores", i)
                    dve.tensor_scalar(kT[:, b, :], ms[:, P:2 * P], qk_w[:, 0:1], None, ALU.mult).then_inc(s["kT"], 1)
                if active(st, LN1):
                    i, b4 = st - LN1, (u - LN1) % U
                    dve.wait_ge(row_in[b4], turn(i, b4) + 16)
                    dve.wait_ge(u_in[b4], turn(i, b4) + 16)
                    then(dve.tensor_scalar(keep[:, b4:b4 + 1], uval[:, b4:b4 + 1], KEEP, 1.0 / KEEP, ALU.is_lt,
                                           ALU.mult), "keep", i + 1)
                    reused(dve, "xn", i, U)
                    then(dve.tensor_scalar(h0[:, b4, :], row[:, b4, :], keep[:, b4:b4 + 1], None, ALU.mult), "h0", i + 1)
                    dve.bn_stats(st1[:, b4, :], h0[:, b4, :]).then_inc(s["ln1_stats"], 1)
                    dve.tensor_copy(res[:, bass.ds(i, 1), :], h0[:, b4:b4 + 1, :]).then_inc(s["h0_kept"], 1)
                    apart(dve)
                    dve.wait_ge(s["ln1_stats"], i + 1)
                    then(dve.bn_aggr(mv1[:, b4, :], st1[:, b4, :]), "ln1_mv", i + 1)
                    dve.tensor_scalar(x1[:, b4, 0:1], mv1[:, b4, 1:2], LN_EPS, None, ALU.add).then_inc(s["ln1_x"], 1)
                if active(st, FIN):
                    i, b = st - FIN, (u - FIN) % 2
                    dve.wait_ge(s["ln2_exp"], i + 1)
                    newton(x2[:, b, 0:2], rs2[:, b, 1, :], (rs2[:, b, 2, :], rs2[:, b, 3, :]), rs2[:, b, 4, :],
                           "ln2_n1", "ln2_n2", "rstd2", i)
                    dve.wait_ge(s["rstd2"], i + 1)
                    then(dve.tensor_scalar(xn2[:, b, :], h1[:, b, :], mv2[:, b, 0:1], rs2[:, b, 4, 0:1], ALU.subtract,
                                           ALU.mult), "xn2", i + 1)
                    reused(dve, "hn", i)
                    dve.tensor_scalar(hn_t[:, b, :], xn2[:, b, :], rs2[:, b, 4, 1:2], None, ALU.mult).then_inc(s["hn_t"], 1)
                if active(st, LN1):
                    i, b4 = st - LN1, (u - LN1) % U
                    dve.wait_ge(s["ln1_exp"], i + 1)
                    newton(x1[:, b4, 0:1], rs1[:, b4, 1:2], (rs1[:, b4, 2:3], rs1[:, b4, 3:4]), rs1[:, b4, 4:5],
                           "ln1_n1", "ln1_n2", "rstd1", i)
                    dve.wait_ge(s["rstd1"], i + 1)
                    reused(dve, "xnT_ps", i, U)
                    dve.tensor_scalar(xn[:, b4, :], h0[:, b4, :], mv1[:, b4, 0:1], rs1[:, b4, 4:5], ALU.subtract,
                                      ALU.mult).then_inc(s["xn"], 1)
                if active(st, SOFT):
                    i, b = st - SOFT, (u - SOFT) % 2
                    dve.wait_ge(s["probs"], i + 1)
                    reused(dve, "probs_n", i)
                    dve.reciprocal(linv[:, b, :], lsum[:, b, :]).then_inc(s["inv_sum"], 1)
                if active(st, PROJ):
                    i, b = st - PROJ, (u - PROJ) % 2
                    sm = small[:, b, :]
                    x_kv = hx[:, b, HK:HK + 1]
                    dve.wait_ge(s["squares"], i + 1)
                    dve.tensor_reduce(ss[:, b, :], sq[:, b, :].rearrange("p (n d) -> p n d", d=DN), AX.X, ALU.add)
                    then(dve.tensor_scalar(x_kv, ss_lat[:, b, 1:2], 1.0 / P, RMS_EPS, ALU.mult, ALU.add), "kv_x", i + 1)
                    dve.reciprocal(sm[:, 0:1], x_kv)
                    dve.tensor_scalar(sm[:, 1:2], ss_lat[:, b, 0:1], RMS_EPS / RQ, RMS_EPS * RMS_EPS, ALU.mult, ALU.add)
                    then(dve.tensor_tensor(sm[:, 2:2 + H], ss[:, b, 0:2 * H:2], ss[:, b, 1:2 * H:2], ALU.add),
                         "q_sum", i + 1)
                    then(dve.scalar_tensor_tensor(out=sm[:, 2 + H:2 + HK], in0=ss[:, b, 2 * H::2], scalar=sm[:, 0:1],
                                                  in1=ss[:, b, 2 * H + 1::2], op0=ALU.mult, op1=ALU.add), "k_sum", i + 1)
                    dve.tensor_scalar(hx[:, b, 0:H], sm[:, 2:2 + H], 1.0 / HD, sm[:, 1:2], ALU.mult, ALU.add)
                    dve.tensor_scalar(hx[:, b, H:HK], sm[:, 2 + H:2 + HK], 1.0 / HD, RMS_EPS, ALU.mult,
                                      ALU.add).then_inc(s["head_x"], 1)
                if active(st, PROJ):
                    i, b = st - PROJ, (u - PROJ) % 2
                    rot = heads(pj[:, 0:C_V])[:, :, DN:HD]
                    half = DR // 2
                    dve.wait_ge(s["squares"], i + 1)
                    reused(dve, "rope", i)
                    dve.tensor_tensor(rope_a[:, b], rot, over_heads(cos, HK), ALU.mult)
                    dve.tensor_tensor(rope_b[:, b, :, 0:half], rot[:, :, half:DR], over_heads(sin[:, 0:half], HK), ALU.mult)
                    dve.tensor_tensor(rope_b[:, b, :, half:DR], rot[:, :, 0:half], over_heads(sin[:, half:DR], HK),
                                      ALU.mult).then_inc(s["rope_hi"], 1)
                if active(st, PROJ):
                    i, b = st - PROJ, (u - PROJ) % 2
                    rs = hw[:, b, 4, :]
                    dve.wait_ge(s["head_exp"], i + 1)
                    reused(dve, "q_rope", i)
                    reused(dve, "v", i)
                    newton(hx[:, b, :], hw[:, b, 1, :], (hw[:, b, 2, :], hw[:, b, 3, :]), rs, "head_n1", "head_n2",
                           "head_rs", i)
                    dve.wait_ge(s["head_rs"], i + 1)
                    then(dve.tensor_scalar(small[:, b, 14:16], rs[:, H:HK], rs[:, HK:HK + 1], None, ALU.mult),
                         "kn_scale", i + 1)
                    reused(dve, "kT_ps", i)
                    pr = heads(pj[:, 0:C_V])
                    dve.tensor_tensor(qh[:, b, H:HK, 0:DN], pr[:, H:HK, 0:DN], bc(small[:, b, 14:16], DN), ALU.mult
                                      ).then_inc(s["k_nope"], 1)
                    dve.tensor_tensor(qh[:, b, 0:H, 0:DN], pr[:, 0:H, 0:DN], bc(rs[:, 0:H], DN), ALU.mult
                                      ).then_inc(s["q_nope"], 1)
                if active(st, SCORE):
                    i, b = st - SCORE, (u - SCORE) % 2
                    dve.wait_ge(s["scores"], i + 1)
                    reused(dve, "probs", i)
                    dve.tensor_reduce(nmax[:, b, :], sc[:].rearrange("p (h k) -> p h k", k=P), AX.X, ALU.max,
                                      negate=True).then_inc(s["neg_max"], 1)

            def sort(part):
                nt = PARTS[part]
                n = E * nt
                t0 = FIRST_TILE[part]
                nb = BLOCKS[part]
                count = [0]

                def link(ins):
                    count[0] += 1
                    ins.then_inc(s[f"sort{part}"], 1)
                    dve.wait_ge(s[f"sort{part}"], count[0])

                sel = [pick[:, k, :, t0:t0 + nt] for k in range(2)]
                tiles = lambda ap: ap.rearrange("p (e t) -> p e t", e=E)
                dve.wait_ge(s["pick"], 2 * (t0 + nt))
                dve.wait_ge(s["gap"], t0 + nt)
                dve.tensor_tensor(tiles(r_pick[:, 0:n]), sel[0], sel[1], ALU.add).then_inc(s["route_pick"], 1)
                dve.wait_ge(s["route_pe"], part + 1)
                dve.tensor_copy(r_cnt[:, 0:n], qo[:, 256:256 + n])
                dve.tensor_copy(r_rank[:, 0:n], qo[:, 0:n]).then_inc(s["route_v"], 1)
                dve.wait_ge(s["route_v"], part + 1)
                link(dve.tensor_tensor_scan(r_run[:, 0:n], ones_f[:, 0:n], r_cnt[:, 0:n], 0.0, ALU.mult, ALU.add))
                ends = tiles(r_run[:, 0:n])[:, :, nt - 1:nt].rearrange("p e o -> p (e o)")
                start, cnt, blk, upto, off, tmp = (r_small[:, k, :] for k in range(6))
                dve.tensor_copy(start[:, 1:E], ends[:, 0:E - 1])
                link(dve.memset(start[:, 0:1], 0.0))
                link(dve.tensor_tensor(cnt, ends, start, ALU.subtract))
                link(dve.tensor_scalar(r_int[:, 0, :], cnt, float(P - 1), None, ALU.add))
                link(dve.tensor_scalar(r_int[:, 1, :], r_int[:, 0, :], P.bit_length() - 1, None, ALU.arith_shift_right))
                link(dve.tensor_copy(blk, r_int[:, 1, :]))
                link(dve.tensor_tensor_scan(upto, ones_f[:, 0:E], blk, 0.0, ALU.mult, ALU.add))
                link(dve.tensor_tensor(tmp, upto, blk, ALU.subtract))
                link(dve.tensor_scalar(tmp, tmp, float(P), None, ALU.mult))
                link(dve.tensor_tensor(off, tmp, start, ALU.subtract))
                link(dve.tensor_tensor(r_pos[:, 0:n], r_run[:, 0:n], r_cnt[:, 0:n], ALU.subtract))
                link(dve.tensor_tensor(r_pos[:, 0:n], r_pos[:, 0:n], r_rank[:, 0:n], ALU.add))
                link(dve.tensor_tensor(tiles(r_pos[:, 0:n]), tiles(r_pos[:, 0:n]),
                                       off.unsqueeze(2).to_broadcast([P, E, nt]), ALU.add))
                for k in range(2):
                    link(dve.tensor_tensor(tiles(r_sel[:, k, 0:n]), tiles(r_pos[:, 0:n]), sel[k], ALU.mult))
                    link(dve.tensor_reduce(r_posf[:, k, 0:nt], r_sel[:, k, 0:n].rearrange("p (e t) -> p t e", e=E),
                                           AX.X, ALU.add))
                    link(dve.tensor_copy(pos[:, k, t0:t0 + nt], r_posf[:, k, 0:nt]))
                link(dve.tensor_tensor(r_cmp[:, 0:nb, :], iota_b[:, 0:nb].unsqueeze(2).to_broadcast([P, nb, E]),
                                       upto.unsqueeze(1).to_broadcast([P, nb, E]), ALU.is_ge))
                link(dve.tensor_reduce(r_blk[:, 0, 0:nb], r_cmp[:, 0:nb, :], AX.X, ALU.add))
                link(dve.tensor_scalar(r_blk[:, 1, 0:nb], r_blk[:, 0, 0:nb], float(E - 1), None, ALU.min))
                dve.tensor_copy(block_e[0:1, FIRST_BLOCK[part]:FIRST_BLOCK[part] + nb],
                                r_blk[0:1, 1, 0:nb]).then_inc(s["pos"], 1)

            steps_a(dve, step, sort)

            dve.wait_ge(s["gate_exp"], 2)
            then(dve.tensor_scalar(gates[:, 0, :], gate_e[:], 1.0, None, ALU.add), "gate1", 1)
            then(dve.reciprocal(gates[:, 0, :], gates[:, 0, :]), "gate2", 1)
            dve.tensor_tensor(gates[:, 1, :], gates[:, 0, :], gate_e[:], ALU.mult).then_inc(s["gates"], 1)
            dve.wait_ge(s["gates"], 1)
            dve.wait_ge(s["w1_in"], 16)
            dve.wait_ge(s["b2_in"], 16)
            dve.wait_ge(s["pos"], 2)
            dve.wait_ge(s["res"], NT)

            def mix(i, u):
                dve.wait_ge(y1_in[u], turn(i, u) + 16)
                dve.wait_ge(y2_in[u], turn(i, u) + 16)
                at = res[:, bass.ds(i, 1), :]
                then(dve.scalar_tensor_tensor(out=at, in0=y1[:, u:u + 1, :], scalar=gates[:, 0, bass.ds(i, 1)], in1=at,
                                              op0=ALU.mult, op1=ALU.add), "mix1", i + 1)
                dve.scalar_tensor_tensor(out=at, in0=y2[:, u:u + 1, :], scalar=gates[:, 1, bass.ds(i, 1)], in1=at,
                                         op0=ALU.mult, op1=ALU.add).then_inc(s["mixed"], 1)

            def step_c(t, u):
                if within(t, 0):
                    b = u % 2
                    e = dve.value_load(block_e[0:1, bass.ds(t, 1)], min_val=0, max_val=E - 1)
                    reused(dve, "hid", t)
                    dve.tensor_copy(w1s[:, b, :], w1[:, bass.ds(e * F, F)])
                    dve.tensor_copy(b1s[:, b, :], b1c[:, bass.ds(e * FC, FC)]).then_inc(s["w1_copy"], 1)
                if within(t, FFN2):
                    n, b, b4 = t - FFN2, (u - FFN2) % 2, (u - FFN2) % U
                    e = dve.value_load(block_e[0:1, bass.ds(n, 1)], min_val=0, max_val=E - 1)
                    dve.wait_ge(s["y_ps"], n + 1)
                    if not (isinstance(n, int) and n < U):
                        dve.wait_ge(y_out[b4], turn(n, b4))
                    dve.tensor_tensor(ysb[:, b4, :], pj[:, b * 512:b * 512 + P], b2_bc[:, bass.ds(e * D, D)],
                                      ALU.add).then_inc(s["y"], 1)

            for t in range(U):
                step_c(t, t)
            with groups(dve, U, MIX0) as t:
                for u in range(U):
                    step_c(t + u, u)
            with groups(dve, MIX0, NB) as t:
                for u in range(U):
                    step_c(t + u, u)
                    mix(t - (MIX0 - u), u)
            for t in range(NB, STEPS_C):
                step_c(t, t % U)
            with groups(dve, NB - MIX0, NT) as i:
                for u in range(U):
                    mix(i + u, u)


_INS = ["x", "L0_tok_weight", "L0_tok_mask_u", "L0_attn_W_DQ", "L0_attn_W_UQ", "L0_attn_W_QR", "L0_attn_W_DKV",
        "L0_attn_W_UK", "L0_attn_W_UV", "L0_attn_W_KR", "L0_attn_W_VR", "L0_attn_W_O", "L0_attn_q_ln_w",
        "L0_attn_kv_ln_w", "L0_attn_q_head_norm_w", "L0_attn_k_head_norm_w", "L0_ffn_ln_g", "L0_ffn_ln_b",
        "L0_ffn_w_r", "L0_ffn_b_r", "L0_ffn_W1", "L0_ffn_b1", "L0_ffn_W2", "L0_ffn_b2"]


def rope_constants(tokens):
    inv_freq = 1.0 / 500000.0 ** (np.arange(0, DR, 2, dtype=np.float32) / DR)
    freqs = np.outer(np.arange(tokens, dtype=np.float32), inv_freq)
    return np.concatenate([np.cos(freqs), np.cos(freqs), -np.sin(freqs), np.sin(freqs)], axis=1).astype(np.float32)


def kernel(**inputs):
    import concourse.bacc as _bacc
    from concourse.bass_utils import run_bass_kernel_spmd as _run

    nc = _bacc.Bacc("TRN2", target_bir_lowering=False, num_devices=1)
    arrays, args = {}, []
    for name in _INS:
        a = np.ascontiguousarray(inputs[name])
        arrays[f"in_{name}"] = a
        args.append(nc.dram_tensor(f"in_{name}", a.shape, mybir.dt.from_np(a.dtype), kind="ExternalInput").ap())
    table = rope_constants(inputs["x"].shape[1])
    arrays["rope_table"] = table
    args.append(nc.dram_tensor("rope_table", table.shape, F32, kind="ExternalInput").ap())
    shape = (*inputs["x"].shape, inputs["L0_tok_weight"].shape[1])
    args.append(nc.dram_tensor("out", shape, F32, kind="ExternalOutput").ap())
    attention_and_experts_kernel(nc, *args)
    return _run(nc, [arrays], core_ids=[0]).results[0]["out"]
```

```python
from contextlib import ExitStack, contextmanager

import numpy as np

import concourse.bass as bass
from concourse import mybir

F32 = mybir.dt.float32
BF16 = mybir.dt.bfloat16
I32 = mybir.dt.int32
U32 = mybir.dt.uint32
ALU = mybir.AluOpType
ACT = mybir.ActivationFunctionType
AX = mybir.AxisListType

P = 128
H, KVH, HD, DN, DR = 8, 2, 64, 32, 32
HK = H + KVH
G = H // KVH
RMS_EPS = 1e-6
LN_EPS = 1e-5
KEEP = 0.9
MASKED = -1e30
E = 8
UNROLL = 4

TILE_SEMS = (
    "keep", "h0", "ln1_stats", "ln1_mv", "ln1_x", "xn", "xnT_ps", "xnT", "proj_q", "proj", "squares_q", "squares",
    "q_squares", "kv_x", "kv_inv", "q_sum", "k_sum", "head_x", "kn_scale", "q_nope", "k_nope", "rope_hi", "rope", "q_rope", "v",
    "qT_ps", "qT", "kT_ps", "kT", "scores", "neg_max", "probs_half", "probs", "inv_half", "inv_sum", "probn_half", "probn",
    "pT_half_ps", "pT_ps", "pT_half", "pT", "oT_ps", "oT", "attn", "h1", "ln2_stats", "ln2_mv", "ln2_v", "ln2_inv", "ln2_x",
    "xn2", "hn", "res", "hnT_ps", "hnT", "logits_ps", "logits", "top", "top_idx", "top_f", "pick", "gap",
    "mix1", "mixed", "out",
)
STEP_SEMS = ("norm_log", "norm_exp", "norm_n1", "norm_n2", "norm_rs")
BLOCK_SEMS = ("xsT_ps", "xsT", "w1_copy", "hid_ps", "hid", "y_ps", "y")
OTHER_SEMS = (
    "words_in", "latent_in", "up_in", "cols_in", "wo_in", "rows_in", "vec_in", "vec2_in", "w1_in", "w2_in", "b2_in",
    "ones", "ident0", "ident", "const0", "consts", "zeroed", "words_f", "wordsT_ps", "words_i", "prep_pe", "prep_v",
    "route_pick", "route_pe", "route_v", "sort0", "sort1", "pos", "scattered0", "scattered1", "gate_exp", "gate1", "gate2", "gates",
)
PREP_LATENT, PREP_WVR, PREP_ALL = 6, 9, 13


def attention_and_experts_kernel(nc, x, emb, mask_u, W_DQ, W_UQ, W_QR, W_DKV, W_UK, W_UV, W_KR, W_VR, W_O,
                                 q_ln_w, kv_ln_w, q_hn_w, k_hn_w, ln_g, ln_b, w_r, b_r, W1, b1, W2, b2,
                                 rope_table, out):
    NT, T = x.shape
    D = emb.shape[1]
    F = W1.shape[2]
    FC = F // P
    RQ = W_DQ.shape[1]
    assert T == P and D == P and RQ == HD and W_DKV.shape[1] == P
    PARTS = (20, NT - 20)
    FIRST_TILE = (0, PARTS[0])
    BLOCKS = tuple(-(-(2 * n + E - 1) // UNROLL) * UNROLL for n in PARTS)
    FIRST_BLOCK = (0, BLOCKS[0])
    NB = sum(BLOCKS)
    ZROWS = 8 * P
    ZEROING = NB * P // ZROWS
    assert all(n * P % ZROWS == 0 for n in BLOCKS)

    C_V = HK * HD
    C_CQ = C_V + P
    C_CKV = C_CQ + RQ
    C_END = C_CKV + P

    X_KV = HK
    X_LN1 = X_KV + 1
    X_LN2 = X_LN1 + 1
    NX = X_LN2 + 2

    sorted_x = [nc.dram_tensor(f"sorted_x{k}", (n * P, D), F32).ap() for k, n in enumerate(BLOCKS)]
    sorted_y = [nc.dram_tensor(f"sorted_y{k}", (n * P, D), F32).ap() for k, n in enumerate(BLOCKS)]

    with ExitStack() as ctx:
        def sb(name, shape, dt=F32):
            return ctx.enter_context(nc.sbuf_tensor(name, shape, dt))

        def ps(name, cols):
            return ctx.enter_context(nc.psum_tensor(name, [P, cols], F32))

        s = {name: ctx.enter_context(nc.semaphore(name)) for name in TILE_SEMS + STEP_SEMS + BLOCK_SEMS + OTHER_SEMS}
        row_in = [ctx.enter_context(nc.semaphore(f"row_in{k}")) for k in range(UNROLL)]
        u_in = [ctx.enter_context(nc.semaphore(f"u_in{k}")) for k in range(UNROLL)]
        hn_kept = [ctx.enter_context(nc.semaphore(f"hn_kept{k}")) for k in range(UNROLL)]
        xs_in = [ctx.enter_context(nc.semaphore(f"xs_in{k}")) for k in range(UNROLL)]
        y_out = [ctx.enter_context(nc.semaphore(f"y_out{k}")) for k in range(UNROLL)]
        y1_in = [ctx.enter_context(nc.semaphore(f"y1_in{k}")) for k in range(UNROLL)]
        y2_in = [ctx.enter_context(nc.semaphore(f"y2_in{k}")) for k in range(UNROLL)]

        pj = ps("pj", 1024)
        sc = ps("sc", 1024)
        pt = ps("pt", 1024)
        C_ATTN, C_LOGITS = 512, 512 + P
        qo = ps("qo", 512)
        ms = ps("ms", 512)

        ident = sb("ident_f", [P, P])
        ident_b = sb("ident_b", [P, P], BF16)
        causal = sb("causal", [P, G * P], BF16)
        before = sb("before", [P, P], BF16)
        ones_b = sb("ones_b", [P, P], BF16)
        iota_e = sb("iota_e", [P, E])
        iota_b = sb("iota_b", [P, BLOCKS[0]])
        ones_f = sb("ones_f", [P, E * PARTS[0]])
        zero = sb("zero", [P, ZROWS // P * D])
        rope_sb = sb("rope_sb", [P, 2 * DR])
        cos = rope_sb[:, 0:DR]
        sin = rope_sb[:, DR:2 * DR]
        w_proj = sb("w_proj", [P, C_END])
        w_res = sb("w_res", [P, P])
        wo = sb("wo", [P, G, P])
        wr = sb("wr", [P, P])
        qk_w = sb("qk_w", [P, 1])
        g_col = sb("g_col", [P, 1])
        b_col = sb("b_col", [P, 1])
        br_bc = sb("br_bc", [P, E])
        w1 = sb("w1", [P, E * F])
        w2 = sb("w2", [P, E * FC * P])
        b1c = sb("b1c", [P, E * FC])
        b2_bc = sb("b2_bc", [P, E * D])
        words = sb("words", [NT, P], I32)
        words_f = sb("words_f32", [NT, P])
        words_T = sb("words_T", [P, NT], U32)

        res = sb("res_all", [P, NT, D])
        hn = sb("hn_all", [P, NT, D])
        pick = sb("pick_all", [P, 2, E, NT])
        gap = sb("gap_all", [P, NT])
        gate_e = sb("gate_e", [P, NT])
        gates = sb("gates_all", [P, 2, NT])
        pos = sb("pos_all", [P, 2, NT], U32)
        block_e = sb("block_e", [1, NB], I32)

        U = UNROLL
        row = sb("row", [P, U, D])
        uval = sb("uval", [P, U])
        keep = sb("keep_b", [P, U])
        st1 = sb("st1", [P, U, 6])
        mv1 = sb("mv1", [P, U, 2])
        xn = sb("xn_b", [P, U, D])
        xnT = sb("xnT_b", [P, U, P])
        sq = sb("sq", [P, 2, C_V])
        sq_lat = sb("sq_lat", [P, 2, P])
        sq_latq = sb("sq_latq", [P, 2, RQ])
        ss_lat = sb("ss_lat", [P, 2, 2])
        ss = sb("ss", [P, 2, 2 * HK])
        norm_x = sb("norm_x", [P, 2, NX])
        norm_w = sb("norm_w", [P, 2, 5, NX])
        small = sb("small", [P, 2, 16])
        rope_a = sb("rope_a", [P, 2, HK, DR])
        rope_b = sb("rope_bb", [P, 2, HK, DR])
        rope_c = sb("rope_cc", [P, 2, HK, DR])
        qh = sb("qh", [P, 2, HK, HD])
        vt = sb("vt", [P, U, P])
        qT = sb("qT_b", [P, 2, G, P])
        kT = sb("kT_b", [P, 2, P])
        nmax = sb("nmax", [P, 2, H])
        lsum = sb("lsum", [P, 2, H])
        linv = sb("linv", [P, 2, H])
        prob = sb("prob", [P, 2, H * P])
        probn = sb("probn", [P, 2, H * P])
        pT = sb("pT_b", [P, 2, H * P])
        oT = sb("oT_b", [P, 2, G, P])
        h1 = sb("h1_b", [P, 2, D])
        st2 = sb("st2", [P, 2, 6])
        mv2 = sb("mv2", [P, 2, 2])
        inv2 = sb("inv2", [P, 2])
        xn2 = sb("xn2_b", [P, 2, D])
        hn_t = sb("hn_t", [P, U, D])
        hnT = sb("hnT_b", [P, 2, P])
        logit = sb("logit", [P, 2, E])
        top = sb("top_b", [P, 2, E])
        top_i = sb("top_i", [P, 2, E], U32)
        top_f = sb("top_fb", [P, 2, 2])

        xs = sb("xs", [P, U, D])
        xsT = sb("xsT_b", [P, 2, P])
        w1s = sb("w1s", [P, 2, F])
        b1s = sb("b1s", [P, 2, FC])
        b2s = sb("b2s", [P, U, D])
        hid = sb("hid_b", [P, 2, FC, P])
        ysb = sb("ysb", [P, U, D])
        y1 = sb("y1", [P, U, D])
        y2 = sb("y2", [P, U, D])

        wdq = sb("wdq", [P, RQ])
        wdkv = sb("wdkv", [P, P])
        wuq = sb("wuq", [RQ, 2, H * DN])
        wukv = sb("wukv", [P, KVH * DN + KVH * HD])
        wvr = sb("wvr", [P, G, KVH, HD])
        wvrT = sb("wvrT", [P, G, P])
        wdqT = sb("wdqT", [RQ, P])
        wdkvT = sb("wdkvT", [P, P])
        wuq_s = sb("wuq_s", [RQ, H, HD])
        wukv_s = sb("wukv_s", [P, KVH * DN + KVH * HD])
        qln = sb("qln", [RQ, 1])
        kvln = sb("kvln", [P, 1])
        hn_w = sb("hn_w", [P, 2])
        wr_rows = sb("wr_rows", [E, P])
        b1_rows = sb("b1_rows", [E * FC, P])

        NR = E * PARTS[0]
        r_pick = sb("r_pick", [P, NR], BF16)
        r_cnt = sb("r_cnt", [P, NR])
        r_run = sb("r_run", [P, NR])
        r_rank = sb("r_rank", [P, NR])
        r_pos = sb("r_pos", [P, NR])
        r_sel = sb("r_sel", [P, 2, NR])
        r_posf = sb("r_posf", [P, 2, PARTS[0]])
        r_small = sb("r_small", [P, 8, E])
        r_int = sb("r_int", [P, 2, E], I32)
        r_cmp = sb("r_cmp", [P, BLOCKS[0], E])
        r_blk = sb("r_blk", [P, 2, BLOCKS[0]])

        def heads(ap):
            return ap.rearrange("p (h d) -> p h d", d=HD)

        def bc(ap, n):
            k = ap.shape[-1]
            return ap.unsqueeze(2).to_broadcast([P, k, n])

        def over_heads(ap, n):
            k = ap.shape[-1]
            return ap.unsqueeze(1).to_broadcast([P, n, k])

        def reused(eng, sem, i, depth=2):
            if not (isinstance(i, int) and i < depth):
                eng.wait_ge(s[sem], i - (depth - 1))

        def apart(eng):
            eng.wait_ge(s["ident"], 1)

        LN1, PROJ, SCORE, SOFT, OUT, LN2, ROUTE = range(7)
        AHEAD = 2
        LOOP_A = (8, 24)
        STEPS_A = NT + ROUTE
        SORT0 = PARTS[0] + ROUTE

        def normed(st):
            return not isinstance(st, int) or 1 <= st < NT + LN2

        @contextmanager
        def groups(eng, first, end):
            with eng.Fori(0, (end - first) // U) as k:
                yield eng.snap(k * U + first)

        def active(st, lag):
            return not isinstance(st, int) or 0 <= st - lag < NT

        def steps_a(eng, body):
            for st in range(LOOP_A[0]):
                body(st, st % U)
            with groups(eng, LOOP_A[0], LOOP_A[1]) as st:
                for u in range(U):
                    body(st + u, u)
            for st in range(LOOP_A[1], STEPS_A):
                body(st, st % U)

        FFN1, FFN2 = 1, 2
        STEPS_C = NB + FFN2
        MIX0 = FIRST_BLOCK[1] + U
        MIX1 = min(MIX0 + PARTS[0] // U * U, NB)
        SORT_STAGES = 8

        def within(t, lag):
            return not isinstance(t, int) or 0 <= t - lag < NB

        def turn(t, u):
            return 16 * (t // U) if isinstance(t, int) else (t - u) * (16 // U)

        block = ctx.enter_context(nc.Block())

        @block.gpsimd
        def _(pool):
            pool.memset(ident[:], 0.0).then_inc(s["ident0"], 1)
            pool.wait_ge(s["ident0"], 1)
            pool.affine_select(out=ident[:], in_=ident[:], compare_op=ALU.not_equal, fill=1.0, base=0,
                               pattern=[[-1, P]], channel_multiplier=1).then_inc(s["ident"], 1)

            def gather(i, u):
                reused(pool, "h0", i, U)
                pool.indirect_dma_start(row[:, u, :], None, emb, bass.IndirectOffsetOnAxis(
                    ap=words_T[:, i:i + 1], axis=0)).then_inc(row_in[u], 16)
                pool.indirect_dma_start(uval[:, u:u + 1], None, mask_u, bass.IndirectOffsetOnAxis(
                    ap=words_T[:, i:i + 1], axis=0)).then_inc(u_in[u], 16)

            pool.wait_ge(s["words_i"], 1)
            for i in range(AHEAD):
                gather(i, i % U)

            pool.memset(ident_b[:], 0.0).then_inc(s["const0"], 1)
            pool.memset(causal[:], 0.0).then_inc(s["const0"], 1)
            pool.memset(before[:], 1.0).then_inc(s["const0"], 1)
            pool.wait_ge(s["const0"], 3)
            pool.affine_select(out=ident_b[:], in_=ident_b[:], compare_op=ALU.not_equal, fill=1.0, base=0,
                               pattern=[[-1, P]], channel_multiplier=1).then_inc(s["consts"], 1)
            pool.affine_select(out=causal[:].rearrange("p (g k) -> p g k", g=G),
                               in_=causal[:].rearrange("p (g k) -> p g k", g=G), compare_op=ALU.is_ge, fill=MASKED,
                               base=0, pattern=[[0, G], [-1, P]], channel_multiplier=1).then_inc(s["consts"], 1)
            pool.affine_select(out=before[:], in_=before[:], compare_op=ALU.is_gt, fill=0.0, base=0,
                               pattern=[[1, P]], channel_multiplier=-1).then_inc(s["consts"], 1)
            pool.iota(iota_e[:], pattern=[[1, E]], base=0, channel_multiplier=0,
                      allow_small_or_imprecise_dtypes=True).then_inc(s["consts"], 1)
            pool.iota(iota_b[:], pattern=[[1, BLOCKS[0]]], base=0, channel_multiplier=0,
                      allow_small_or_imprecise_dtypes=True).then_inc(s["consts"], 1)

            def ready_to_scatter(part):
                pool.wait_ge(s["pos"], part + 1)
                pool.wait_ge(s["zeroed"], 16 * ZEROING)
                for u in range(U):
                    pool.wait_ge(hn_kept[u], 16 * (FIRST_TILE[part] + PARTS[part]) // U)

            def scatter(part, lo, hi):
                for n in range(lo, min(hi, 2 * PARTS[part])):
                    i, k = FIRST_TILE[part] + n // 2, n % 2
                    pool.indirect_dma_start(sorted_x[part], bass.IndirectOffsetOnAxis(ap=pos[:, k, i:i + 1], axis=0),
                                            hn[:, i, :], None).then_inc(s[f"scattered{part}"], 16)

            scattered = [0]

            SCATTER0 = SORT0 + 3

            def scatter_some(st, n):
                if st >= SCATTER0:
                    scatter(0, scattered[0], scattered[0] + n)
                    scattered[0] += n

            def step(st, u):
                if st == SCATTER0:
                    ready_to_scatter(0)
                if active(st, SCORE):
                    i, b = st - SCORE, (u - SCORE) % 2
                    pool.wait_ge(s["rope"], i + 1)
                    pool.wait_ge(s["norm_rs"], st)
                    reused(pool, "kT_ps", i)
                    pool.tensor_tensor(qh[:, b, :, DN:HD], rope_c[:, b], bc(norm_w[:, (u - 1) % 2, 4, 0:HK], DR),
                                       ALU.mult).then_inc(s["q_rope"], 1)
                if active(st, SOFT):
                    i, b = st - SOFT, (u - SOFT) % 2
                    reused(pool, "pT_ps", i)
                    c = slice(0, G * P)
                    pool.wait_ge(s["inv_half"], i + 1)
                    pool.tensor_tensor(probn[:, b, c].rearrange("p (h k) -> p h k", k=P),
                                       prob[:, b, c].rearrange("p (h k) -> p h k", k=P),
                                       bc(linv[:, b, 0:G], P), ALU.mult).then_inc(s["probn_half"], 1)
                if st + AHEAD < NT:
                    gather(st + AHEAD, (u + AHEAD) % U)
                scatter_some(st, 1)
                if active(st, SOFT):
                    i, b = st - SOFT, (u - SOFT) % 2
                    c = slice(G * P, H * P)
                    pool.wait_ge(s["inv_sum"], i + 1)
                    pool.tensor_tensor(probn[:, b, c].rearrange("p (h k) -> p h k", k=P),
                                       prob[:, b, c].rearrange("p (h k) -> p h k", k=P),
                                       bc(linv[:, b, G:H], P), ALU.mult).then_inc(s["probn"], 1)
                if active(st, LN2):
                    i, b = st - LN2, (u - LN2) % 2
                    pool.wait_ge(s["xn2"], i + 1)
                    pool.tensor_tensor(res[:, bass.ds(i, 1), :], h1[:, b:b + 1, :], xn2[:, b:b + 1, :],
                                       ALU.add).then_inc(s["res"], 1)
                scatter_some(st, 2)
                if active(st, PROJ):
                    i, b = st - PROJ, (u - PROJ) % 2
                    pool.wait_ge(s["rope_hi"], i + 1)
                    pool.tensor_tensor(rope_c[:, b], rope_a[:, b], rope_b[:, b], ALU.add).then_inc(s["rope"], 1)
                scatter_some(st, 2)

            for st in range(STEPS_A):
                step(st, st % U)
            scatter(0, scattered[0], 2 * PARTS[0])
            ready_to_scatter(1)
            scatter(1, 0, 2 * PARTS[1])

            def fetch(part, i, u):
                reused(pool, "mixed", i, U)
                pool.indirect_dma_start(y1[:, u, :], None, sorted_y[part], bass.IndirectOffsetOnAxis(
                    ap=pos[:, 0, i:i + 1], axis=0)).then_inc(y1_in[u], 16)
                pool.indirect_dma_start(y2[:, u, :], None, sorted_y[part], bass.IndirectOffsetOnAxis(
                    ap=pos[:, 1, i:i + 1], axis=0)).then_inc(y2_in[u], 16)

            for part in range(2):
                for u in range(U):
                    pool.wait_ge(y_out[u], 16 * (FIRST_BLOCK[part] + BLOCKS[part]) // U)
                for i in range(FIRST_TILE[part], FIRST_TILE[part] + PARTS[part]):
                    fetch(part, i, i % U)

        @block.sync
        def _(sp):
            sp.dma_start(words[:], x).then_inc(s["words_in"], 16)
            sp.dma_start(wdq[:], W_DQ).then_inc(s["latent_in"], 16)
            sp.dma_start(wdkv[:], W_DKV).then_inc(s["latent_in"], 16)
            sp.dma_start(wuq[:, 0, :], W_UQ).then_inc(s["up_in"], 16)
            sp.dma_start(wuq[:, 1, :], W_QR).then_inc(s["up_in"], 16)
            sp.dma_start(wukv[:, 0:KVH * DN], W_UK).then_inc(s["up_in"], 16)
            sp.dma_start(wukv[:, KVH * DN:], W_UV).then_inc(s["up_in"], 16)
            for g in range(KVH):
                sp.dma_start(w_proj[:, (H + g) * HD + DN:(H + g + 1) * HD],
                             W_KR[:, g * DR:(g + 1) * DR]).then_inc(s["cols_in"], 16)
            sp.dma_start(w_proj[:, C_CQ:C_CKV], W_DQ).then_inc(s["cols_in"], 16)
            sp.dma_start(w_proj[:, C_CKV:C_END], W_DKV).then_inc(s["cols_in"], 16)
            for g in range(KVH):
                sp.dma_start(wvr[:, :, g, :],
                             W_VR[:, g * G * HD:(g + 1) * G * HD].rearrange("k (c d) -> k c d", c=G)
                             ).then_inc(s["wo_in"], 16)
                sp.dma_start(wo[g * HD:(g + 1) * HD],
                             W_O[g * G * HD:(g + 1) * G * HD, :].rearrange("(c d) n -> d c n", c=G)
                             ).then_inc(s["wo_in"], 16)
            sp.dma_start(w1[:].rearrange("p (e f) -> p e f", e=E), W1.rearrange("e d f -> d e f")).then_inc(s["w1_in"], 16)
            sp.dma_start(w2[:].rearrange("p (e c d) -> p e c d", e=E, c=FC),
                         W2.rearrange("e (c p) d -> p e c d", p=P)).then_inc(s["w2_in"], 16)
            sp.dma_start(b2_bc[:], b2.rearrange("e d -> (e d)").partition_broadcast(P)).then_inc(s["b2_in"], 16)

            sp.wait_ge(s["ones"], 1)
            for part in range(2):
                with sp.Fori(0, BLOCKS[part] * P // ZROWS) as z:
                    sp.dma_start(sorted_x[part][bass.ds(z * ZROWS, ZROWS), :].rearrange("(p r) d -> p (r d)", p=P),
                                 zero[:]).then_inc(s["zeroed"], 16)

            with sp.Fori(0, NT // U) as g:
                i = sp.snap(g * U)
                for u in range(U):
                    sp.wait_ge(s["hn"], i + u + 1)
                    sp.dma_start(hn[:, bass.ds(i + u, 1), :], hn_t[:, u:u + 1, :]).then_inc(hn_kept[u], 16)

            STORE = 6
            PUT = MIX0 + 2 * U
            PUT1 = min(PUT + PARTS[0] // U * U, NB)

            def put(i):
                sp.wait_ge(s["mixed"], i + 1)
                sp.dma_start(out[bass.ds(i, 1)].rearrange("a t d -> t a d"),
                             res[:, bass.ds(i, 1), :]).then_inc(s["out"], 16)

            def rows(buffers, part, n):
                return buffers[part][bass.ds((n - FIRST_BLOCK[part]) * P, P), :]

            def step(t, u, part=None):
                if within(t, 0):
                    reused(sp, "xsT_ps", t, U)
                    k = part if part is not None else int(t >= FIRST_BLOCK[1])
                    sp.dma_start(xs[:, u, :], rows(sorted_x, k, t)).then_inc(xs_in[u], 16)
                if within(t, STORE):
                    n, b4 = t - STORE, (u - STORE) % U
                    sp.wait_ge(s["y"], n + 1)
                    k = part if part is not None else int(n >= FIRST_BLOCK[1])
                    sp.dma_start(rows(sorted_y, k, n), ysb[:, b4, :]).then_inc(y_out[b4], 16)

            sp.wait_ge(s["scattered0"], 16 * 2 * PARTS[0])
            for t in range(2 * U):
                step(t, t % U)
            with groups(sp, 2 * U, FIRST_BLOCK[1]) as t:
                for u in range(U):
                    step(t + u, u, 0)
            sp.wait_ge(s["scattered1"], 16 * 2 * PARTS[1])
            for t in range(FIRST_BLOCK[1], PUT):
                step(t, t % U)
            with groups(sp, PUT, PUT1) as t:
                for u in range(U):
                    step(t + u, u, 1)
                    put(t + (u - PUT))
            if PUT1 < NB:
                with groups(sp, PUT1, NB) as t:
                    for u in range(U):
                        step(t + u, u, 1)
            for t in range(NB, NB + STORE):
                step(t, t % U)
            with sp.Fori(PUT1 - PUT, NT) as i:
                put(i)
            sp.wait_ge(s["out"], 16 * NT)

        @block.tensor
        def _(pe):
            pe.wait_ge(s["ident"], 1)
            pe.wait_ge(s["words_f"], 1)
            pe.transpose(ms[:, 0:NT], words_f[:], ident[0:NT, 0:NT]).then_inc(s["wordsT_ps"], 1)

            pe.wait_ge(s["latent_in"], 32)
            pe.transpose(qo[0:RQ, 0:P], wdq[:], ident[:])
            pe.transpose(qo[:, P:2 * P], wdkv[:], ident[:]).then_inc(s["prep_pe"], 1)
            pe.wait_ge(s["rows_in"], 32)
            pe.transpose(sc[:, 0:E], wr_rows[:], ident[0:E, 0:E])
            pe.transpose(sc[:, P:P + E * FC], b1_rows[:], ident[0:E * FC, 0:E * FC]).then_inc(s["prep_pe"], 1)
            pe.wait_ge(s["prep_v"], PREP_LATENT)
            pe.matmul(pj[:, 0:H * HD], wdqT[:], wuq_s[:].rearrange("p h d -> p (h d)"), start=True, stop=True)
            pe.matmul(pj[:, H * HD:H * HD + KVH * (DN + HD)], wdkvT[:], wukv_s[:], start=True,
                      stop=True).then_inc(s["prep_pe"], 1)
            pe.wait_ge(s["wo_in"], 16 * 2 * KVH)
            for c in range(G):
                last = pe.transpose(pt[:, c * P:(c + 1) * P], wvr[:, c].rearrange("p g d -> p (g d)"), ident[:])
            last.then_inc(s["prep_pe"], 1)
            pe.wait_ge(s["prep_v"], PREP_WVR)
            for c in range(G):
                last = pe.matmul(ms[:, P:2 * P], wvrT[:, c, :], wo[:, c, :], start=(c == 0), stop=(c == G - 1))
            last.then_inc(s["prep_pe"], 1)
            pe.wait_ge(s["prep_v"], PREP_ALL)
            pe.wait_ge(s["consts"], 5)
            pe.wait_ge(s["cols_in"], 64)

            def sort(part):
                n = E * PARTS[part]
                to = (qo, sc)[part]
                pe.wait_ge(s["route_pick"], part + 1)
                if part == 0:
                    pe.wait_ge(s["qT"], SORT0 - SCORE + 1)
                pe.matmul(to[:, 0:n], before[:], r_pick[:, 0:n], start=True, stop=True)
                pe.matmul(to[:, 256:256 + n], ones_b[:], r_pick[:, 0:n], start=True,
                          stop=True).then_inc(s["route_pe"], 1)

            def step(st, u):
                if active(st, OUT):
                    i, b, b4 = st - OUT, (u - OUT) % 2, (u - OUT) % U
                    pe.wait_ge(s["pT_half"], i + 1)
                    pe.wait_ge(s["pT"], i + 1)
                    pe.wait_ge(s["v"], i + 1)
                    reused(pe, "oT", i, 1)
                    for g in range(KVH):
                        last = pe.matmul(pt[g * HD:(g + 1) * HD, 0:512], vt[:, b4, g * HD:(g + 1) * HD],
                                         pT[:, b, g * 512:(g + 1) * 512], start=True, stop=True)
                    last.then_inc(s["oT_ps"], 1)
                if active(st, OUT) or active(st, ROUTE):
                    if active(st, SOFT + 1):
                        pe.wait_ge(s["pT"], st - SOFT)
                    if active(st, OUT + 1):
                        pe.wait_ge(s["h1"], st - OUT)
                    if active(st, ROUTE + 1):
                        pe.wait_ge(s["logits"], st - ROUTE)
                if active(st, ROUTE):
                    i, b = st - ROUTE, (u - ROUTE) % 2
                    pe.wait_ge(s["hnT"], i + 1)
                    pe.matmul(pt[:, C_LOGITS:C_LOGITS + P], hnT[:, b, :], wr[:], start=True, stop=True
                              ).then_inc(s["logits_ps"], 1)
                if active(st, PROJ):
                    i, b4 = st - PROJ, (u - PROJ) % U
                    pe.wait_ge(s["xn"], i + 1)
                    if active(st, LN2 + 1):
                        pe.wait_ge(s["hnT"], st - LN2)
                    pe.transpose(ms[:, 0:P], xn[:, b4, :], ident[:]).then_inc(s["xnT_ps"], 1)
                if active(st, OUT):
                    i, b, b4 = st - OUT, (u - OUT) % 2, (u - OUT) % U
                    pe.wait_ge(s["oT"], i + 1)
                    at = pt[:, C_ATTN:C_ATTN + P]
                    for c in range(G):
                        pe.matmul(at, oT[:, b, c, :], wo[:, c, :], start=(c == 0), stop=False)
                    pe.matmul(at, xnT[:, b4, :], w_res[:], start=False, stop=True).then_inc(s["attn"], 1)
                if active(st, SCORE):
                    i, b = st - SCORE, (u - SCORE) % 2
                    pe.wait_ge(s["q_nope"], i + 1)
                    pe.wait_ge(s["q_rope"], i + 1)
                    reused(pe, "qT", i, 1)
                    if isinstance(st, int) and st == SORT0 + 1:
                        pe.wait_ge(s["route_v"], 1)
                    for c in range(G):
                        last = pe.transpose(qo[:, c * P:(c + 1) * P],
                                            qh[:, b, 2 * c:2 * c + 2, :].rearrange("p h d -> p (h d)"), ident[:])
                    last.then_inc(s["qT_ps"], 1)
                    pe.wait_ge(s["k_nope"], i + 1)
                    if active(st, PROJ):
                        pe.wait_ge(s["xnT"], st - PROJ + 1)
                    else:
                        pe.wait_ge(s["hnT"], st - LN2)
                    pe.transpose(ms[:, P:2 * P], qh[:, b, H:HK, :].rearrange("p h d -> p (h d)"),
                                 ident[:]).then_inc(s["kT_ps"], 1)
                if active(st, PROJ):
                    i, b4 = st - PROJ, (u - PROJ) % U
                    pe.wait_ge(s["xnT"], i + 1)
                    reused(pe, "q_nope", i, 1)
                    pe.matmul(pj[:, 0:512], xnT[:, b4, :], w_proj[:, 0:512], start=True, stop=True
                              ).then_inc(s["proj_q"], 1)
                    reused(pe, "v", i, 1)
                    pe.matmul(pj[:, 512:C_END], xnT[:, b4, :], w_proj[:, 512:C_END], start=True,
                              stop=True).then_inc(s["proj"], 1)
                if active(st, LN2):
                    i = st - LN2
                    pe.wait_ge(s["hn"], i + 1)
                    if active(st, SCORE):
                        pe.wait_ge(s["kT"], st - SCORE + 1)
                    else:
                        pe.wait_ge(s["hnT"], i)
                    pe.transpose(ms[:, 2 * P:3 * P], hn_t[:, (u - LN2) % U, :], ident[:]).then_inc(s["hnT_ps"], 1)
                if active(st, SOFT):
                    i, b = st - SOFT, (u - SOFT) % 2
                    pe.wait_ge(s["probn_half"], i + 1)
                    reused(pe, "pT_half", i, 1)
                    if active(st, OUT):
                        pe.wait_ge(s["oT"], st - OUT + 1)
                    for h in range(G):
                        last = pe.transpose(pt[:, h * P:(h + 1) * P], probn[:, b, h * P:(h + 1) * P], ident[:])
                    last.then_inc(s["pT_half_ps"], 1)
                if active(st, SCORE):
                    i, b = st - SCORE, (u - SCORE) % 2
                    pe.wait_ge(s["qT"], i + 1)
                    pe.wait_ge(s["kT"], i + 1)
                    reused(pe, "probs", i, 1)
                    for g in range(KVH):
                        pe.matmul(sc[:, g * 512:(g + 1) * 512], ident_b[:], causal[:], start=True, stop=False,
                                  skip_group_check=True)
                    for c in range(G):
                        for g in range(KVH):
                            r = slice(g * HD, (g + 1) * HD)
                            at = g * 512 + c * P
                            last = pe.matmul(sc[:, at:at + P], qT[r, b, c, :], kT[r, b, :], start=False,
                                             stop=(c == G - 1), skip_group_check=True)
                    last.then_inc(s["scores"], 1)
                if active(st, SOFT):
                    i, b = st - SOFT, (u - SOFT) % 2
                    pe.wait_ge(s["probn"], i + 1)
                    reused(pe, "pT", i, 1)
                    if active(st, OUT):
                        pe.wait_ge(s["h1"], st - OUT + 1)
                    if active(st, ROUTE):
                        pe.wait_ge(s["logits"], st - ROUTE + 1)
                    for h in range(G, H):
                        last = pe.transpose(pt[:, h * P:(h + 1) * P], probn[:, b, h * P:(h + 1) * P], ident[:])
                    last.then_inc(s["pT_ps"], 1)
                if isinstance(st, int) and st == SORT0:
                    sort(0)

            steps_a(pe, step)

            def step_c(t, u):
                if within(t, FFN2):
                    e = pe.value_load(block_e[0:1, bass.ds(t - FFN2, 1)], min_val=0, max_val=E - 1)
                if within(t, 0):
                    pe.wait_ge(xs_in[u], turn(t, u) + 16)
                    reused(pe, "xsT", t)
                    tp = (qo, ms)[u % 2]
                    pe.transpose(tp[:, 0:P], xs[:, u, :], ident[:]).then_inc(s["xsT_ps"], 1)
                if within(t, FFN1):
                    n, b = t - FFN1, (u - FFN1) % 2
                    pe.wait_ge(s["xsT"], n + 1)
                    pe.wait_ge(s["w1_copy"], n + 1)
                    reused(pe, "hid", n)
                    for c in range(FC):
                        last = pe.matmul(pt[:, b * 512 + c * P:b * 512 + (c + 1) * P], w1s[:, b, c * P:(c + 1) * P],
                                         xsT[:, b, :], start=True, stop=True)
                    last.then_inc(s["hid_ps"], 1)
                if within(t, FFN2):
                    n, b = t - FFN2, (u - FFN2) % 2
                    pe.wait_ge(s["hid"], n + 1)
                    reused(pe, "y", n)
                    for c in range(FC):
                        last = pe.matmul(pj[:, b * 512:b * 512 + P], hid[:, b, c, :],
                                         w2[:, bass.ds(e * (FC * P) + c * P, P)], start=(c == 0), stop=(c == FC - 1))
                    last.then_inc(s["y_ps"], 1)

            pe.wait_ge(s["w2_in"], 16)
            for done in ("logits", "h1", "q_nope", "v", "probs", "pT_half", "pT", "hnT", "oT"):
                pe.wait_ge(s[done], NT)
            pe.wait_ge(s["pos"], 1)
            for t in range(U):
                step_c(t, t)
                if t == 0:
                    sort(1)
            with groups(pe, U, NB) as t:
                for u in range(U):
                    step_c(t + u, u)
            for t in range(NB, STEPS_C):
                step_c(t, t % U)

        @block.scalar
        def _(act):
            act.preload_act_table_set("natural_log_exp_and_others")
            act.dma_start(wr_rows[:], w_r).then_inc(s["rows_in"], 16)
            act.dma_start(b1_rows[:], b1.rearrange("e (c p) -> (e c) p", p=P)).then_inc(s["rows_in"], 16)

            def col(v):
                return v.rearrange("(p a) -> p a", a=1)

            act.dma_start(qln[:], col(q_ln_w)).then_inc(s["vec_in"], 16)
            act.dma_start(kvln[:], col(kv_ln_w)).then_inc(s["vec_in"], 16)
            for g in range(KVH):
                act.dma_start(hn_w[g * HD:(g + 1) * HD, 0:1], col(q_hn_w)).then_inc(s["vec_in"], 16)
                act.dma_start(hn_w[g * HD:(g + 1) * HD, 1:2], col(k_hn_w)).then_inc(s["vec_in"], 16)
            act.dma_start(rope_sb[:], rope_table).then_inc(s["vec2_in"], 16)
            act.dma_start(g_col[:], col(ln_g)).then_inc(s["vec2_in"], 16)
            act.dma_start(b_col[:], col(ln_b)).then_inc(s["vec2_in"], 16)
            act.dma_start(br_bc[:], b_r.partition_broadcast(P)).then_inc(s["vec2_in"], 16)

            def exps(st, u, heads, done):
                i, b = st - SOFT, (u - SOFT) % 2
                for h in heads:
                    last = act.activation(prob[:, b, h * P:(h + 1) * P], sc[:, h * P:(h + 1) * P], ACT.Exp,
                                          bias=nmax[:, b, h:h + 1], accum_out=lsum[:, b, h:h + 1])
                if done is not None:
                    last.then_inc(s[done], 1)

            def step(st, u):
                if active(st, SOFT):
                    act.wait_ge(s["neg_max"], st - SOFT + 1)
                    reused(act, "probn", st - SOFT)
                    exps(st, u, range(0, 2), None)
                if active(st, OUT):
                    i, b = st - OUT, (u - OUT) % 2
                    act.wait_ge(s["oT_ps"], i + 1)
                    reused(act, "attn", i)
                    act.copy(oT[:, b].rearrange("p c t -> p (c t)"), pt[:, 0:512]).then_inc(s["oT"], 1)
                if active(st, SOFT):
                    exps(st, u, range(2, G), "probs_half")
                if active(st, PROJ):
                    i, b4 = st - PROJ, (u - PROJ) % U
                    act.wait_ge(s["xnT_ps"], i + 1)
                    reused(act, "attn", i, U)
                    act.copy(xnT[:, b4, :], ms[:, 0:P]).then_inc(s["xnT"], 1)
                if active(st, SCORE):
                    i, b, b4 = st - SCORE, (u - SCORE) % 2, (u - SCORE) % U
                    act.wait_ge(s["k_nope"], i + 1)
                    reused(act, "oT_ps", i, U)
                    act.activation(vt[:, b4, :], pj[:, C_V:C_CQ], ACT.Copy,
                                   scale=norm_w[:, (u - 1) % 2, 4, X_KV:X_KV + 1]).then_inc(s["v"], 1)
                if active(st, SOFT):
                    exps(st, u, range(G, G + 2), None)
                if active(st, SCORE):
                    i, b = st - SCORE, (u - SCORE) % 2
                    act.wait_ge(s["qT_ps"], i + 1)
                    reused(act, "scores", i)
                    act.copy(qT[:, b].rearrange("p c t -> p (c t)"), qo[:]).then_inc(s["qT"], 1)
                    act.wait_ge(s["kT_ps"], i + 1)
                    act.activation(kT[:, b, :], ms[:, P:2 * P], ACT.Copy, scale=qk_w[:, 0:1]).then_inc(s["kT"], 1)
                if active(st, SOFT):
                    exps(st, u, range(G + 2, H), "probs")
                if active(st, PROJ):
                    i, b = st - PROJ, (u - PROJ) % 2
                    act.wait_ge(s["proj_q"], i + 1)
                    reused(act, "head_x", i)
                    act.activation(sq[:, b, 0:512], pj[:, 0:512], ACT.Square).then_inc(s["squares_q"], 1)
                if active(st, PROJ):
                    i, b = st - PROJ, (u - PROJ) % 2
                    act.wait_ge(s["proj"], i + 1)
                    act.activation(sq[:, b, 512:C_V], pj[:, 512:C_V], ACT.Square)
                    act.activation(sq_latq[:, b, :], pj[:, C_CQ:C_CKV], ACT.Square, accum_out=ss_lat[:, b, 0:1])
                    act.activation(sq_lat[:, b, :], pj[:, C_CKV:C_END], ACT.Square,
                                   accum_out=ss_lat[:, b, 1:2]).then_inc(s["squares"], 1)
                if active(st, LN2):
                    i, b = st - LN2, (u - LN2) % 2
                    act.wait_ge(s["hnT_ps"], i + 1)
                    reused(act, "logits_ps", i)
                    act.activation(hnT[:, b, :], ms[:, 2 * P:3 * P], ACT.Identity, bias=b_col[:, 0:1],
                                   scale=g_col[:, 0:1]).then_inc(s["hnT"], 1)
                if active(st, SOFT):
                    i, b = st - SOFT, (u - SOFT) % 2
                    act.wait_ge(s["pT_half_ps"], i + 1)
                    reused(act, "oT_ps", i)
                    act.copy(pT[:, b, 0:512], pt[:, 0:512]).then_inc(s["pT_half"], 1)
                if normed(st + 1):
                    for sem, lag in (("head_x", PROJ), ("ln1_x", LN1), ("ln2_x", OUT)):
                        if active(st, lag):
                            act.wait_ge(s[sem], st - lag + 1)
                    w = norm_w[:, u % 2]
                    act.activation(w[:, 0, :], norm_x[:, u % 2, :], ACT.Ln).then_inc(s["norm_log"], 1)
                    act.wait_ge(s["norm_log"], st + 1)
                    act.activation(w[:, 1, :], w[:, 0, :], ACT.Exp, scale=-0.5).then_inc(s["norm_exp"], 1)
                if active(st, SOFT):
                    i, b = st - SOFT, (u - SOFT) % 2
                    act.wait_ge(s["pT_ps"], i + 1)
                    act.copy(pT[:, b, 512:1024], pt[:, 512:1024]).then_inc(s["pT"], 1)

            act.wait_ge(s["vec2_in"], 64)
            steps_a(act, step)

            for part in range(2):
                c = slice(FIRST_TILE[part], FIRST_TILE[part] + PARTS[part])
                act.wait_ge(s["route_pick"], part + 1)
                act.activation(gate_e[:, c], gap[:, c], ACT.Exp).then_inc(s["gate_exp"], 1)

            def step_c(t, u):
                if within(t, 0):
                    b = u % 2
                    act.wait_ge(s["xsT_ps"], t + 1)
                    reused(act, "hid_ps", t)
                    act.activation(xsT[:, b, :], (qo, ms)[b][:, 0:P], ACT.Identity, bias=b_col[:, 0:1],
                                   scale=g_col[:, 0:1]).then_inc(s["xsT"], 1)
                if within(t, FFN1):
                    n, b = t - FFN1, (u - FFN1) % 2
                    act.wait_ge(s["hid_ps"], n + 1)
                    reused(act, "y_ps", n)
                    for c in range(FC):
                        last = act.activation(hid[:, b, c, :], pt[:, b * 512 + c * P:b * 512 + (c + 1) * P], ACT.Gelu,
                                              bias=b1s[:, b, c:c + 1])
                    last.then_inc(s["hid"], 1)

            for t in range(U):
                step_c(t, t)
            with groups(act, U, NB) as t:
                for u in range(U):
                    step_c(t + u, u)
            for t in range(NB, STEPS_C):
                step_c(t, t % U)

        @block.vector
        def _(dve):
            def then(ins, sem, value):
                ins.then_inc(s[sem], 1)
                dve.wait_ge(s[sem], value)

            dve.wait_ge(s["words_in"], 16)
            dve.tensor_copy(words_f[:], words[:]).then_inc(s["words_f"], 1)
            dve.memset(zero[:], 0.0)
            dve.memset(norm_x[:], 1.0)
            dve.memset(ones_b[:], 1.0)
            dve.memset(ones_f[:], 1.0)
            dve.memset(wr[:], 0.0).then_inc(s["ones"], 1)
            dve.wait_ge(s["wordsT_ps"], 1)
            dve.tensor_copy(words_T[:], ms[:, 0:NT]).then_inc(s["words_i"], 1)

            dve.wait_ge(s["vec_in"], 16 * (2 + 2 * KVH))
            dve.wait_ge(s["up_in"], 64)
            for k in range(2):
                dve.tensor_scalar(wuq_s[:, :, k * DN:(k + 1) * DN].rearrange("k (c g) d -> k g c d", g=KVH),
                                  wuq[:, k, :].rearrange("k (g c d) -> k g c d", g=KVH, c=G), qln[:, 0:1], None,
                                  ALU.mult).then_inc(s["prep_v"], 1)
            dve.tensor_scalar(wukv_s[:], wukv[:], kvln[:, 0:1], None, ALU.mult).then_inc(s["prep_v"], 1)
            dve.tensor_scalar(qk_w[:], hn_w[:, 0:1], hn_w[:, 1:2], float(HD) ** -0.5, ALU.mult,
                              ALU.mult).then_inc(s["prep_v"], 1)
            dve.wait_ge(s["prep_pe"], 1)
            dve.tensor_copy(wdqT[:], qo[0:RQ, 0:P]).then_inc(s["prep_v"], 1)
            dve.tensor_copy(wdkvT[:], qo[:, P:2 * P]).then_inc(s["prep_v"], 1)
            dve.wait_ge(s["prep_pe"], 2)
            dve.wait_ge(s["ones"], 1)
            dve.tensor_copy(wr[:, 0:E], sc[:, 0:E]).then_inc(s["prep_v"], 1)
            dve.tensor_copy(b1c[:], sc[:, P:P + E * FC]).then_inc(s["prep_v"], 1)
            dve.wait_ge(s["prep_pe"], 4)
            dve.tensor_copy(wvrT[:].rearrange("p c n -> p (c n)"), pt[:, 0:512]).then_inc(s["prep_v"], 1)
            dve.tensor_copy(w_proj[:, 0:H * HD], pj[:, 0:H * HD]).then_inc(s["prep_v"], 1)
            dve.tensor_copy(heads(w_proj[:, H * HD:C_V])[:, :, 0:DN],
                            pj[:, H * HD:H * HD + KVH * DN].rearrange("p (g d) -> p g d", g=KVH)
                            ).then_inc(s["prep_v"], 1)
            dve.tensor_copy(w_proj[:, C_V:C_CQ], pj[:, H * HD + KVH * DN:H * HD + KVH * (DN + HD)]
                            ).then_inc(s["prep_v"], 1)
            dve.wait_ge(s["prep_pe"], 5)
            dve.tensor_copy(w_res[:], ms[:, P:2 * P]).then_inc(s["prep_v"], 1)
            dve.wait_ge(s["vec2_in"], 64)
            dve.wait_ge(s["consts"], 5)
            dve.wait_ge(s["prep_v"], PREP_ALL)

            links = [0, 0]

            def sort(part, stages):
                nt = PARTS[part]
                n = E * nt
                t0 = FIRST_TILE[part]
                nb = BLOCKS[part]
                counted = (qo, sc)[part]

                def link(ins):
                    links[part] += 1
                    ins.then_inc(s[f"sort{part}"], 1)
                    dve.wait_ge(s[f"sort{part}"], links[part])

                sel = [pick[:, k, :, t0:t0 + nt] for k in range(2)]
                tiles = lambda ap: ap.rearrange("p (e t) -> p e t", e=E)
                ends = tiles(r_run[:, 0:n])[:, :, nt - 1:nt].rearrange("p e o -> p (e o)")
                start, cnt, blk, upto, off, tmp = (r_small[:, k, :] for k in range(6))
                if 0 in stages:
                    dve.wait_ge(s["pick"], 2 * (t0 + nt))
                    dve.wait_ge(s["gap"], t0 + nt)
                    dve.tensor_tensor(tiles(r_pick[:, 0:n]), sel[0], sel[1], ALU.add).then_inc(s["route_pick"], 1)
                if 1 in stages:
                    dve.wait_ge(s["route_pe"], part + 1)
                    dve.tensor_copy(r_cnt[:, 0:n], counted[:, 256:256 + n])
                    dve.tensor_copy(r_rank[:, 0:n], counted[:, 0:n]).then_inc(s["route_v"], 1)
                    dve.wait_ge(s["route_v"], part + 1)
                    link(dve.tensor_tensor_scan(r_run[:, 0:n], ones_f[:, 0:n], r_cnt[:, 0:n], 0.0, ALU.mult, ALU.add))
                if 2 in stages:
                    dve.tensor_copy(start[:, 1:E], ends[:, 0:E - 1])
                    link(dve.memset(start[:, 0:1], 0.0))
                    link(dve.tensor_tensor(cnt, ends, start, ALU.subtract))
                if 3 in stages:
                    link(dve.tensor_scalar(r_int[:, 0, :], cnt, float(P - 1), None, ALU.add))
                    link(dve.tensor_scalar(r_int[:, 1, :], r_int[:, 0, :], P.bit_length() - 1, None, ALU.arith_shift_right))
                    link(dve.tensor_copy(blk, r_int[:, 1, :]))
                    link(dve.tensor_tensor_scan(upto, ones_f[:, 0:E], blk, 0.0, ALU.mult, ALU.add))
                    link(dve.tensor_tensor(tmp, upto, blk, ALU.subtract))
                if 4 in stages:
                    link(dve.tensor_scalar(tmp, tmp, float(P), None, ALU.mult))
                    link(dve.tensor_tensor(off, tmp, start, ALU.subtract))
                if 5 in stages:
                    link(dve.tensor_tensor(r_pos[:, 0:n], r_run[:, 0:n], r_cnt[:, 0:n], ALU.subtract))
                    link(dve.tensor_tensor(r_pos[:, 0:n], r_pos[:, 0:n], r_rank[:, 0:n], ALU.add))
                    link(dve.tensor_tensor(tiles(r_pos[:, 0:n]), tiles(r_pos[:, 0:n]),
                                           off.unsqueeze(2).to_broadcast([P, E, nt]), ALU.add))
                if 6 in stages:
                    for k in range(2):
                        link(dve.tensor_tensor(tiles(r_sel[:, k, 0:n]), tiles(r_pos[:, 0:n]), sel[k], ALU.mult))
                        link(dve.tensor_reduce(r_posf[:, k, 0:nt], r_sel[:, k, 0:n].rearrange("p (e t) -> p t e", e=E),
                                               AX.X, ALU.add))
                        link(dve.tensor_copy(pos[:, k, t0:t0 + nt], r_posf[:, k, 0:nt]))
                if 7 in stages:
                    link(dve.tensor_tensor(r_cmp[:, 0:nb, :], iota_b[:, 0:nb].unsqueeze(2).to_broadcast([P, nb, E]),
                                           upto.unsqueeze(1).to_broadcast([P, nb, E]), ALU.is_ge))
                    link(dve.tensor_reduce(r_blk[:, 0, 0:nb], r_cmp[:, 0:nb, :], AX.X, ALU.add))
                    link(dve.tensor_scalar(r_blk[:, 1, 0:nb], r_blk[:, 0, 0:nb], float(E - 1), None, ALU.min))
                    dve.tensor_copy(block_e[0:1, FIRST_BLOCK[part]:FIRST_BLOCK[part] + nb],
                                    r_blk[0:1, 1, 0:nb]).then_inc(s["pos"], 1)

            def sort_in_step(st, place):
                if isinstance(st, int) and SORT0 <= st < SORT0 + 3:
                    sort(0, (((0,), (), (1,)), ((2,), (3,), (4,)), ((5,), (6,), (7,)))[st - SORT0][place])

            def step(st, u):
                sort_in_step(st, 0)
                x_b, r_b = u % 2, (u - 1) % 2
                rs = norm_w[:, r_b, 4, :]
                y, w1_, w2_ = (norm_w[:, r_b, k, :] for k in (1, 2, 3))
                t0_, t4 = st - LN1, (u - LN1) % U
                h0 = res[:, bass.ds(t0_, 1), :] if active(st, LN1) else None
                if active(st, LN1):
                    dve.wait_ge(row_in[t4], turn(t0_, t4) + 16)
                    dve.wait_ge(u_in[t4], turn(t0_, t4) + 16)
                    dve.tensor_scalar(keep[:, t4:t4 + 1], uval[:, t4:t4 + 1], KEEP, 1.0 / KEEP, ALU.is_lt,
                                      ALU.mult).then_inc(s["keep"], 1)
                if normed(st):
                    dve.wait_ge(s["norm_exp"], st)
                    if active(st, SCORE):
                        reused(dve, "q_rope", st - SCORE)
                        reused(dve, "v", st - SCORE)
                    dve.scalar_tensor_tensor(out=w1_, in0=y, scalar=-0.5, in1=y, op0=ALU.mult, op1=ALU.mult
                                             ).then_inc(s["norm_n1"], 1)
                if active(st, LN1):
                    dve.wait_ge(s["keep"], t0_ + 1)
                    dve.tensor_scalar(h0, row[:, t4:t4 + 1, :], keep[:, t4:t4 + 1], None, ALU.mult).then_inc(s["h0"], 1)
                if normed(st):
                    dve.wait_ge(s["norm_n1"], st)
                    dve.tensor_tensor(w2_, w1_, norm_x[:, r_b, :], ALU.mult).then_inc(s["norm_n2"], 1)
                if active(st, LN1):
                    apart(dve)
                    dve.wait_ge(s["h0"], t0_ + 1)
                    dve.bn_stats(st1[:, t4, :], h0.rearrange("p a d -> p (a d)")).then_inc(s["ln1_stats"], 1)
                if normed(st):
                    dve.wait_ge(s["norm_n2"], st)
                    dve.scalar_tensor_tensor(out=rs, in0=w2_, scalar=1.5, in1=y, op0=ALU.add,
                                             op1=ALU.mult).then_inc(s["norm_rs"], 1)
                if active(st, LN1):
                    apart(dve)
                    dve.wait_ge(s["ln1_stats"], t0_ + 1)
                    dve.bn_aggr(mv1[:, t4, :], st1[:, t4, :]).then_inc(s["ln1_mv"], 1)
                if normed(st):
                    dve.wait_ge(s["norm_rs"], st)
                if active(st, PROJ):
                    i, b4 = st - PROJ, (u - PROJ) % U
                    reused(dve, "xnT_ps", i, U)
                    dve.tensor_scalar(xn[:, b4:b4 + 1, :], res[:, bass.ds(i, 1), :], mv1[:, b4, 0:1],
                                      rs[:, X_LN1:X_LN1 + 1], ALU.subtract, ALU.mult).then_inc(s["xn"], 1)
                if active(st, SCORE):
                    i, b = st - SCORE, (u - SCORE) % 2
                    pr = heads(pj[:, 0:C_V])
                    dve.tensor_scalar(small[:, b, 14:16], rs[:, H:HK], rs[:, X_KV:X_KV + 1], None,
                                      ALU.mult).then_inc(s["kn_scale"], 1)
                    reused(dve, "kT_ps", i)
                    dve.tensor_tensor(qh[:, b, 0:H, 0:DN], pr[:, 0:H, 0:DN], bc(rs[:, 0:H], DN), ALU.mult
                                      ).then_inc(s["q_nope"], 1)
                    dve.wait_ge(s["kn_scale"], i + 1)
                    dve.tensor_tensor(qh[:, b, H:HK, 0:DN], pr[:, H:HK, 0:DN], bc(small[:, b, 14:16], DN), ALU.mult
                                      ).then_inc(s["k_nope"], 1)
                if active(st, LN1):
                    dve.wait_ge(s["ln1_mv"], t0_ + 1)
                    dve.tensor_scalar(norm_x[:, x_b, X_LN1:X_LN1 + 1], mv1[:, t4, 1:2], LN_EPS, None,
                                      ALU.add).then_inc(s["ln1_x"], 1)
                if active(st, SOFT):
                    i, b = st - SOFT, (u - SOFT) % 2
                    dve.wait_ge(s["probs_half"], i + 1)
                    reused(dve, "probn", i)
                    dve.reciprocal(linv[:, b, 0:G], lsum[:, b, 0:G]).then_inc(s["inv_half"], 1)
                if active(st, LN2):
                    i, b = st - LN2, (u - LN2) % 2
                    reused(dve, "res", i)
                    dve.tensor_scalar(xn2[:, b, :], h1[:, b, :], mv2[:, b, 0:1], rs[:, X_LN2:X_LN2 + 1],
                                      ALU.subtract, ALU.mult).then_inc(s["xn2"], 1)
                sort_in_step(st, 1)
                if active(st, OUT):
                    i, b = st - OUT, (u - OUT) % 2
                    dve.wait_ge(s["attn"], i + 1)
                    if active(st, ROUTE):
                        dve.wait_ge(s["logits_ps"], st - ROUTE + 1)
                    reused(dve, "res", i)
                    dve.tensor_tensor(h1[:, b:b + 1, :], res[:, bass.ds(i, 1), :],
                                      pt[:, C_ATTN:C_ATTN + P].unsqueeze(1), ALU.add).then_inc(s["h1"], 1)
                if active(st, ROUTE):
                    i, b = st - ROUTE, (u - ROUTE) % 2
                    dve.wait_ge(s["logits_ps"], i + 1)
                    dve.tensor_tensor(logit[:, b, :], pt[:, C_LOGITS:C_LOGITS + E], br_bc[:],
                                      ALU.add).then_inc(s["logits"], 1)
                if active(st, LN2):
                    i, b = st - LN2, (u - LN2) % 2
                    dve.wait_ge(s["xn2"], i + 1)
                    reused(dve, "hnT_ps", i, U)
                    b4 = (u - LN2) % U
                    if not (isinstance(i, int) and i < U):
                        dve.wait_ge(hn_kept[b4], turn(i, b4))
                    dve.tensor_scalar(hn_t[:, b4, :], xn2[:, b, :], rs[:, X_LN2 + 1:X_LN2 + 2], None,
                                      ALU.mult).then_inc(s["hn"], 1)
                if active(st, OUT):
                    i, b = st - OUT, (u - OUT) % 2
                    dve.wait_ge(s["h1"], i + 1)
                    dve.bn_stats(st2[:, b, :], h1[:, b, :]).then_inc(s["ln2_stats"], 1)
                if active(st, ROUTE):
                    i, b = st - ROUTE, (u - ROUTE) % 2
                    apart(dve)
                    dve.wait_ge(s["logits"], i + 1)
                    dve.max(top[:, b, :], logit[:, b, :]).then_inc(s["top"], 1)
                if active(st, OUT):
                    i, b = st - OUT, (u - OUT) % 2
                    apart(dve)
                    dve.wait_ge(s["ln2_stats"], i + 1)
                    dve.bn_aggr(mv2[:, b, :], st2[:, b, :]).then_inc(s["ln2_mv"], 1)
                if active(st, ROUTE):
                    i, b = st - ROUTE, (u - ROUTE) % 2
                    apart(dve)
                    dve.wait_ge(s["top"], i + 1)
                    dve.max_index(top_i[:, b, :], top[:, b, :], logit[:, b, :]).then_inc(s["top_idx"], 1)
                x2 = norm_x[:, x_b, X_LN2:X_LN2 + 2]
                if active(st, OUT):
                    i, b = st - OUT, (u - OUT) % 2
                    dve.wait_ge(s["ln2_mv"], i + 1)
                    dve.tensor_scalar(x2[:, 0:1], mv2[:, b, 1:2], LN_EPS, None, ALU.add).then_inc(s["ln2_v"], 1)
                if active(st, ROUTE):
                    i, b = st - ROUTE, (u - ROUTE) % 2
                    dve.wait_ge(s["top_idx"], i + 1)
                    dve.tensor_copy(top_f[:, b, :], top_i[:, b, 0:2]).then_inc(s["top_f"], 1)
                    dve.tensor_scalar(gap[:, bass.ds(i, 1)], top[:, b, 1:2], top[:, b, 0:1], None,
                                      ALU.subtract).then_inc(s["gap"], 1)
                if active(st, OUT):
                    i, b = st - OUT, (u - OUT) % 2
                    dve.wait_ge(s["ln2_v"], i + 1)
                    dve.reciprocal(inv2[:, b:b + 1], x2[:, 0:1]).then_inc(s["ln2_inv"], 1)
                if active(st, ROUTE):
                    i, b = st - ROUTE, (u - ROUTE) % 2
                    dve.wait_ge(s["top_f"], i + 1)
                    for k in range(2):
                        dve.tensor_scalar(pick[:, k, :, bass.ds(i, 1)], iota_e[:].unsqueeze(2), top_f[:, b, k:k + 1],
                                          None, ALU.is_equal).then_inc(s["pick"], 1)
                if active(st, OUT):
                    i, b = st - OUT, (u - OUT) % 2
                    dve.wait_ge(s["ln2_inv"], i + 1)
                    dve.tensor_scalar(x2[:, 1:2], mv2[:, b, 1:2], inv2[:, b:b + 1], LN_EPS, ALU.mult,
                                      ALU.add).then_inc(s["ln2_x"], 1)
                if active(st, SOFT):
                    i, b = st - SOFT, (u - SOFT) % 2
                    dve.wait_ge(s["probs"], i + 1)
                    dve.reciprocal(linv[:, b, G:H], lsum[:, b, G:H]).then_inc(s["inv_sum"], 1)
                if active(st, PROJ):
                    i, b = st - PROJ, (u - PROJ) % 2
                    sm = small[:, b, :]
                    x = norm_x[:, x_b, :]
                    rot = heads(pj[:, 0:C_V])[:, :, DN:HD]
                    half = DR // 2
                    dve.wait_ge(s["squares_q"], i + 1)
                    dve.tensor_reduce(ss[:, b, 0:2 * H], sq[:, b, 0:512].rearrange("p (n d) -> p n d", d=DN), AX.X,
                                      ALU.add).then_inc(s["q_squares"], 1)
                    dve.wait_ge(s["squares"], i + 1)
                    dve.tensor_reduce(ss[:, b, 2 * H:2 * HK], sq[:, b, 512:C_V].rearrange("p (n d) -> p n d", d=DN),
                                      AX.X, ALU.add)
                    dve.tensor_scalar(x[:, X_KV:X_KV + 1], ss_lat[:, b, 1:2], 1.0 / P, RMS_EPS, ALU.mult,
                                      ALU.add).then_inc(s["kv_x"], 1)
                    dve.tensor_scalar(sm[:, 1:2], ss_lat[:, b, 0:1], RMS_EPS / RQ, RMS_EPS * RMS_EPS, ALU.mult, ALU.add)
                    dve.wait_ge(s["q_squares"], i + 1)
                    dve.tensor_tensor(sm[:, 2:2 + H], ss[:, b, 0:2 * H:2], ss[:, b, 1:2 * H:2],
                                      ALU.add).then_inc(s["q_sum"], 1)
                    dve.wait_ge(s["kv_x"], i + 1)
                    dve.reciprocal(sm[:, 0:1], x[:, X_KV:X_KV + 1]).then_inc(s["kv_inv"], 1)
                    reused(dve, "rope", i)
                    dve.tensor_tensor(rope_a[:, b], rot, over_heads(cos, HK), ALU.mult)
                    dve.wait_ge(s["kv_inv"], i + 1)
                    dve.scalar_tensor_tensor(out=sm[:, 2 + H:2 + HK], in0=ss[:, b, 2 * H::2], scalar=sm[:, 0:1],
                                             in1=ss[:, b, 2 * H + 1::2], op0=ALU.mult, op1=ALU.add
                                             ).then_inc(s["k_sum"], 1)
                    dve.tensor_tensor(rope_b[:, b, :, 0:half], rot[:, :, half:DR], over_heads(sin[:, 0:half], HK), ALU.mult)
                    dve.wait_ge(s["q_sum"], i + 1)
                    dve.wait_ge(s["k_sum"], i + 1)
                    dve.tensor_scalar(x[:, 0:H], sm[:, 2:2 + H], 1.0 / HD, sm[:, 1:2], ALU.mult, ALU.add)
                    dve.tensor_scalar(x[:, H:HK], sm[:, 2 + H:2 + HK], 1.0 / HD, RMS_EPS, ALU.mult,
                                      ALU.add).then_inc(s["head_x"], 1)
                    dve.tensor_tensor(rope_b[:, b, :, half:DR], rot[:, :, 0:half], over_heads(sin[:, half:DR], HK),
                                      ALU.mult).then_inc(s["rope_hi"], 1)
                if active(st, SCORE):
                    i, b = st - SCORE, (u - SCORE) % 2
                    dve.wait_ge(s["scores"], i + 1)
                    reused(dve, "probs", i)
                    dve.tensor_reduce(nmax[:, b, :], sc[:].rearrange("p (h k) -> p h k", k=P), AX.X, ALU.max,
                                      negate=True).then_inc(s["neg_max"], 1)
                sort_in_step(st, 2)

            steps_a(dve, step)

            dve.wait_ge(s["w1_in"], 16)
            dve.wait_ge(s["b2_in"], 16)

            def mix1(i, u):
                dve.wait_ge(y1_in[u], turn(i, u) + 16)
                at = res[:, bass.ds(i, 1), :]
                dve.scalar_tensor_tensor(out=at, in0=y1[:, u:u + 1, :], scalar=gates[:, 0, bass.ds(i, 1)], in1=at,
                                         op0=ALU.mult, op1=ALU.add).then_inc(s["mix1"], 1)

            def mix2(i, u):
                dve.wait_ge(y2_in[u], turn(i, u) + 16)
                dve.wait_ge(s["mix1"], i + 1)
                at = res[:, bass.ds(i, 1), :]
                dve.scalar_tensor_tensor(out=at, in0=y2[:, u:u + 1, :], scalar=gates[:, 1, bass.ds(i, 1)], in1=at,
                                         op0=ALU.mult, op1=ALU.add).then_inc(s["mixed"], 1)

            def step_c(t, u):
                if within(t, 0):
                    b = u % 2
                    e = dve.value_load(block_e[0:1, bass.ds(t, 1)], min_val=0, max_val=E - 1)
                    reused(dve, "hid", t)
                    reused(dve, "y", t, U)
                    dve.tensor_copy(b2s[:, u % U, :], b2_bc[:, bass.ds(e * D, D)])
                    dve.tensor_copy(w1s[:, b, :], w1[:, bass.ds(e * F, F)])
                    dve.tensor_copy(b1s[:, b, :], b1c[:, bass.ds(e * FC, FC)]).then_inc(s["w1_copy"], 1)
                if within(t, FFN2):
                    n, b, b4 = t - FFN2, (u - FFN2) % 2, (u - FFN2) % U
                    dve.wait_ge(s["y_ps"], n + 1)
                    if not (isinstance(n, int) and n < U):
                        dve.wait_ge(y_out[b4], turn(n, b4))
                    dve.tensor_tensor(ysb[:, b4, :], pj[:, b * 512:b * 512 + P], b2s[:, b4, :],
                                      ALU.add).then_inc(s["y"], 1)

            for t in range(SORT_STAGES):
                sort(1, [t])
                step_c(t, t % U)
            dve.wait_ge(s["gate_exp"], 2)
            then(dve.tensor_scalar(gates[:, 0, :], gate_e[:], 1.0, None, ALU.add), "gate1", 1)
            then(dve.reciprocal(gates[:, 0, :], gates[:, 0, :]), "gate2", 1)
            dve.tensor_tensor(gates[:, 1, :], gates[:, 0, :], gate_e[:], ALU.mult).then_inc(s["gates"], 1)
            dve.wait_ge(s["gates"], 1)
            dve.wait_ge(s["res"], NT)
            with groups(dve, SORT_STAGES, MIX0) as t:
                for u in range(U):
                    step_c(t + u, u)
            with groups(dve, MIX0, MIX1) as t:
                for u in range(U):
                    mix1(t - (MIX0 - u), u)
                    step_c(t + u, u)
                    mix2(t - (MIX0 - u), u)
            if MIX1 < NB:
                with groups(dve, MIX1, NB) as t:
                    for u in range(U):
                        step_c(t + u, u)
            for t in range(NB, STEPS_C):
                step_c(t, t % U)
            with groups(dve, MIX1 - MIX0, NT) as i:
                for u in range(U):
                    mix1(i + u, u)
                    mix2(i + u, u)


_INS = ["x", "L0_tok_weight", "L0_tok_mask_u", "L0_attn_W_DQ", "L0_attn_W_UQ", "L0_attn_W_QR", "L0_attn_W_DKV",
        "L0_attn_W_UK", "L0_attn_W_UV", "L0_attn_W_KR", "L0_attn_W_VR", "L0_attn_W_O", "L0_attn_q_ln_w",
        "L0_attn_kv_ln_w", "L0_attn_q_head_norm_w", "L0_attn_k_head_norm_w", "L0_ffn_ln_g", "L0_ffn_ln_b",
        "L0_ffn_w_r", "L0_ffn_b_r", "L0_ffn_W1", "L0_ffn_b1", "L0_ffn_W2", "L0_ffn_b2"]


def rope_constants(tokens):
    inv_freq = 1.0 / 500000.0 ** (np.arange(0, DR, 2, dtype=np.float32) / DR)
    freqs = np.outer(np.arange(tokens, dtype=np.float32), inv_freq)
    return np.concatenate([np.cos(freqs), np.cos(freqs), -np.sin(freqs), np.sin(freqs)], axis=1).astype(np.float32)


def kernel(**inputs):
    import concourse.bacc as _bacc
    from concourse.bass_utils import run_bass_kernel_spmd as _run

    nc = _bacc.Bacc("TRN2", target_bir_lowering=False, num_devices=1)
    arrays, args = {}, []
    for name in _INS:
        a = np.ascontiguousarray(inputs[name])
        arrays[f"in_{name}"] = a
        args.append(nc.dram_tensor(f"in_{name}", a.shape, mybir.dt.from_np(a.dtype), kind="ExternalInput").ap())
    table = rope_constants(inputs["x"].shape[1])
    arrays["rope_table"] = table
    args.append(nc.dram_tensor("rope_table", table.shape, F32, kind="ExternalInput").ap())
    shape = (*inputs["x"].shape, inputs["L0_tok_weight"].shape[1])
    args.append(nc.dram_tensor("out", shape, F32, kind="ExternalOutput").ap())
    attention_and_experts_kernel(nc, *args)
    return _run(nc, [arrays], core_ids=[0]).results[0]["out"]
```

```python
from contextlib import ExitStack, contextmanager

import numpy as np

import concourse.bass as bass
from concourse import mybir

F32 = mybir.dt.float32
BF16 = mybir.dt.bfloat16
I32 = mybir.dt.int32
U32 = mybir.dt.uint32
ALU = mybir.AluOpType
ACT = mybir.ActivationFunctionType
AX = mybir.AxisListType

P = 128
H, KVH, HD, DN, DR = 8, 2, 64, 32, 32
HK = H + KVH
G = H // KVH
RMS_EPS = 1e-6
LN_EPS = 1e-5
KEEP = 0.9
MASKED = -1e30
E = 8
UNROLL = 4

TILE_SEMS = (
    "keep", "h0", "ln1_stats", "ln1_mv", "ln1_x", "xn", "xnT_ps", "xnT", "proj_q", "proj", "squares_q", "squares",
    "q_squares", "kv_x", "kv_inv", "q_sum", "k_sum", "head_x", "kn_scale", "q_nope", "k_nope", "rope_hi", "rope",
    "q_rope", "v", "qT_ps", "qT", "kT_ps", "kT", "scores", "neg_max", "probs_half", "probs", "inv_half", "inv_sum",
    "probn_half", "probn", "pT_half_ps", "pT_ps", "pT_half", "pT", "oT_ps", "oT", "attn", "h1", "ln2_stats",
    "ln2_mv", "ln2_v", "ln2_inv", "ln2_x", "xn2", "hn", "res", "hnT_ps", "hnT", "logits_ps", "logits", "top",
    "top_idx", "top_f", "pick", "gap",
    "mix1", "mixed", "out",
)
STEP_SEMS = ("norm_log", "norm_exp", "norm_n1", "norm_n2", "norm_rs")
BLOCK_SEMS = ("xsT_ps", "xsT", "w1_copy", "hid_ps", "hid", "y_ps", "y")
OTHER_SEMS = (
    "words_in", "latent_in", "up_in", "cols_in", "wo_in", "rows_in", "vec_in", "vec2_in", "w1_in", "w2_in", "b2_in",
    "ones", "ident0", "ident", "const0", "consts", "zeroed", "words_f", "wordsT_ps", "words_i", "prep_pe", "prep_v",
    "route_pick", "route_pe", "route_v", "sort0", "sort1", "pos", "block_e", "scattered0",
    "scattered1", "gate_exp", "gate1", "gate2", "gates",
)
PREP_LATENT, PREP_PROJ, PREP_ROWS, PREP_WVR, PREP_ALL = 6, 9, 11, 12, 13
WVR_STEP, WRES_STEP = 2, 3


def attention_and_experts_kernel(nc, x, emb, mask_u, W_DQ, W_UQ, W_QR, W_DKV, W_UK, W_UV, W_KR, W_VR, W_O,
                                 q_ln_w, kv_ln_w, q_hn_w, k_hn_w, ln_g, ln_b, w_r, b_r, W1, b1, W2, b2,
                                 rope_table, out):
    NT, T = x.shape
    D = emb.shape[1]
    F = W1.shape[2]
    FC = F // P
    RQ = W_DQ.shape[1]
    assert T == P and D == P and RQ == HD and W_DKV.shape[1] == P
    PARTS = (20, NT - 20)
    FIRST_TILE = (0, PARTS[0])
    BLOCKS = tuple(2 * n + E - 1 for n in PARTS)
    FIRST_BLOCK = (0, BLOCKS[0])
    NB = sum(BLOCKS)
    ZROWS = 8 * P
    ZEROINGS = tuple(-(-n * P // ZROWS) for n in BLOCKS)

    C_V = HK * HD
    C_CQ = C_V + P
    C_CKV = C_CQ + RQ
    C_END = C_CKV + P

    X_KV = HK
    X_LN1 = X_KV + 1
    X_LN2 = X_LN1 + 1
    NX = X_LN2 + 2

    sorted_x = [nc.dram_tensor(f"sorted_x{k}", (n * ZROWS, D), F32).ap() for k, n in enumerate(ZEROINGS)]
    sorted_y = [nc.dram_tensor(f"sorted_y{k}", (n * P, D), F32).ap() for k, n in enumerate(BLOCKS)]

    with ExitStack() as ctx:
        def sb(name, shape, dt=F32):
            return ctx.enter_context(nc.sbuf_tensor(name, shape, dt))

        def ps(name, cols):
            return ctx.enter_context(nc.psum_tensor(name, [P, cols], F32))

        s = {name: ctx.enter_context(nc.semaphore(name)) for name in TILE_SEMS + STEP_SEMS + BLOCK_SEMS + OTHER_SEMS}
        row_in = [ctx.enter_context(nc.semaphore(f"row_in{k}")) for k in range(UNROLL)]
        u_in = [ctx.enter_context(nc.semaphore(f"u_in{k}")) for k in range(UNROLL)]
        hn_kept = [ctx.enter_context(nc.semaphore(f"hn_kept{k}")) for k in range(UNROLL)]
        xs_in = [ctx.enter_context(nc.semaphore(f"xs_in{k}")) for k in range(UNROLL)]
        y_out = [ctx.enter_context(nc.semaphore(f"y_out{k}")) for k in range(UNROLL)]
        y1_in = [ctx.enter_context(nc.semaphore(f"y1_in{k}")) for k in range(UNROLL)]
        y2_in = [ctx.enter_context(nc.semaphore(f"y2_in{k}")) for k in range(UNROLL)]

        pj = ps("pj", 1024)
        sc = ps("sc", 1024)
        pt = ps("pt", 1024)
        C_ATTN, C_LOGITS = 512, 512 + P
        qo = ps("qo", 512)
        ms = ps("ms", 512)

        ident = sb("ident_f", [P, P])
        ident_b = sb("ident_b", [P, P], BF16)
        causal = sb("causal", [P, G * P], BF16)
        before = sb("before", [P, P], BF16)
        ones_b = sb("ones_b", [P, P], BF16)
        iota_e = sb("iota_e", [P, E])
        iota_b = sb("iota_b", [P, BLOCKS[0]])
        ones_f = sb("ones_f", [P, E * PARTS[0]])
        zero = sb("zero", [P, ZROWS // P * D])
        rope_sb = sb("rope_sb", [P, 2 * DR])
        cos = rope_sb[:, 0:DR]
        sin = rope_sb[:, DR:2 * DR]
        w_proj = sb("w_proj", [P, C_END])
        w_res = sb("w_res", [P, P])
        wo = sb("wo", [P, G, P])
        wr = sb("wr", [P, P])
        qk_w = sb("qk_w", [P, 1])
        g_col = sb("g_col", [P, 1])
        b_col = sb("b_col", [P, 1])
        br_bc = sb("br_bc", [P, E])
        w1 = sb("w1", [P, E * F])
        w2 = sb("w2", [P, E * FC * P])
        b1c = sb("b1c", [P, E * FC])
        b2_bc = sb("b2_bc", [P, E * D])
        words = sb("words", [NT, P], I32)
        words_f = sb("words_f32", [NT, P])
        words_T = sb("words_T", [P, NT], U32)

        res = sb("res_all", [P, NT, D])
        hn = sb("hn_all", [P, NT, D])
        pick = sb("pick_all", [P, 2, E, NT])
        gap = sb("gap_all", [P, NT])
        gate_e = sb("gate_e", [P, NT])
        gates = sb("gates_all", [P, 2, NT])
        pos = sb("pos_all", [P, 2, NT], U32)
        block_e = sb("block_e", [1, NB], I32)

        U = UNROLL
        row = sb("row", [P, U, D])
        uval = sb("uval", [P, U])
        keep = sb("keep_b", [P, U])
        st1 = sb("st1", [P, U, 6])
        mv1 = sb("mv1", [P, U, 2])
        xn = sb("xn_b", [P, U, D])
        xnT = sb("xnT_b", [P, U, P])
        sq = sb("sq", [P, 2, C_V])
        sq_lat = sb("sq_lat", [P, 2, P])
        sq_latq = sb("sq_latq", [P, 2, RQ])
        ss_lat = sb("ss_lat", [P, 2, 2])
        ss = sb("ss", [P, 2, 2 * HK])
        norm_x = sb("norm_x", [P, 2, NX])
        norm_w = sb("norm_w", [P, 2, 5, NX])
        small = sb("small", [P, 2, 16])
        rope_a = sb("rope_a", [P, 2, HK, DR])
        rope_b = sb("rope_bb", [P, 2, HK, DR])
        rope_c = sb("rope_cc", [P, 2, HK, DR])
        qh = sb("qh", [P, 2, HK, HD])
        vt = sb("vt", [P, U, P])
        qT = sb("qT_b", [P, 2, G, P])
        kT = sb("kT_b", [P, 2, P])
        nmax = sb("nmax", [P, 2, H])
        lsum = sb("lsum", [P, 2, H])
        linv = sb("linv", [P, 2, H])
        prob = sb("prob", [P, 2, H * P])
        probn = sb("probn", [P, 2, H * P])
        pT = sb("pT_b", [P, 2, H * P])
        oT = sb("oT_b", [P, 2, G, P])
        h1 = sb("h1_b", [P, 2, D])
        st2 = sb("st2", [P, 2, 6])
        mv2 = sb("mv2", [P, 2, 2])
        inv2 = sb("inv2", [P, 2])
        xn2 = sb("xn2_b", [P, 2, D])
        hn_t = sb("hn_t", [P, U, D])
        hnT = sb("hnT_b", [P, 2, P])
        logit = sb("logit", [P, 2, E])
        top = sb("top_b", [P, 2, E])
        top_i = sb("top_i", [P, 2, E], U32)
        top_f = sb("top_fb", [P, 2, 2])

        xs = sb("xs", [P, U, D])
        xsT = sb("xsT_b", [P, 2, P])
        w1s = sb("w1s", [P, 2, F])
        b1s = sb("b1s", [P, 2, FC])
        b2s = sb("b2s", [P, U, D])
        hid = sb("hid_b", [P, 2, FC, P])
        ysb = sb("ysb", [P, U, D])
        y1 = sb("y1", [P, U, D])
        y2 = sb("y2", [P, U, D])

        wdq = sb("wdq", [P, RQ])
        wdkv = sb("wdkv", [P, P])
        wuq = sb("wuq", [RQ, 2, H * DN])
        wukv = sb("wukv", [P, KVH * DN + KVH * HD])
        wvr = sb("wvr", [P, G, KVH, HD])
        wvrT = sb("wvrT", [P, G, P])
        wdqT = sb("wdqT", [RQ, P])
        wdkvT = sb("wdkvT", [P, P])
        wuq_s = sb("wuq_s", [RQ, H, HD])
        wukv_s = sb("wukv_s", [P, KVH * DN + KVH * HD])
        qln = sb("qln", [RQ, 1])
        kvln = sb("kvln", [P, 1])
        hn_w = sb("hn_w", [P, 2])
        wr_rows = sb("wr_rows", [E, P])
        b1_rows = sb("b1_rows", [E * FC, P])

        NR = E * PARTS[0]
        r_pick = sb("r_pick", [P, NR], BF16)
        r_cnt = sb("r_cnt", [P, NR])
        r_run = sb("r_run", [P, NR])
        r_rank = sb("r_rank", [P, NR])
        r_pos = sb("r_pos", [P, NR])
        r_sel = sb("r_sel", [P, 2, NR])
        r_posf = sb("r_posf", [P, 2, PARTS[0]])
        r_small = sb("r_small", [P, 8, E])
        r_int = sb("r_int", [P, 2, E], I32)
        r_cmp = sb("r_cmp", [P, BLOCKS[0], E])
        r_blk = sb("r_blk", [P, 2, BLOCKS[0]])

        def heads(ap):
            return ap.rearrange("p (h d) -> p h d", d=HD)

        def bc(ap, n):
            k = ap.shape[-1]
            return ap.unsqueeze(2).to_broadcast([P, k, n])

        def over_heads(ap, n):
            k = ap.shape[-1]
            return ap.unsqueeze(1).to_broadcast([P, n, k])

        def reused(eng, sem, i, depth=2):
            if not (isinstance(i, int) and i < depth):
                eng.wait_ge(s[sem], i - (depth - 1))

        def apart(eng):
            eng.wait_ge(s["ident"], 1)

        LN1, PROJ, SCORE, SOFT, OUT, LN2, ROUTE = range(7)
        AHEAD = 2
        LOOP_A = (8, 24)
        STEPS_A = NT + ROUTE
        SORT0 = PARTS[0] + ROUTE
        assert LOOP_A[1] <= SORT0

        def normed(st):
            return not isinstance(st, int) or 1 <= st < NT + LN2

        @contextmanager
        def groups(eng, first, end, n=UNROLL):
            with eng.Fori(0, (end - first) // n) as k:
                yield eng.snap(k * n + first)

        def active(st, lag):
            return not isinstance(st, int) or 0 <= st - lag < NT

        def steps_a(eng, body, first=0):
            for st in range(first, LOOP_A[0]):
                body(st, st % U)
            with groups(eng, LOOP_A[0], LOOP_A[1]) as st:
                for u in range(U):
                    body(st + u, u)
            for st in range(LOOP_A[1], STEPS_A):
                body(st, st % U)

        FFN1, FFN2 = 1, 2
        STEPS_C = NB + FFN2
        UC = 2 * U
        LOOP_C = (UC, NB // UC * UC)
        STORE = 6
        MIX0 = -(-(FIRST_BLOCK[1] + STORE) // UC) * UC
        MIX1 = MIX0 + min(PARTS[0], NB - MIX0) // U * U
        SORT_STAGES = 7

        def within(t, lag):
            return not isinstance(t, int) or 0 <= t - lag < NB

        def turn(t, u):
            return 16 * (t // U) if isinstance(t, int) else (t - u) * (16 // U)

        block = ctx.enter_context(nc.Block())

        @block.gpsimd
        def _(pool):
            pool.memset(ident[:], 0.0).then_inc(s["ident0"], 1)
            pool.wait_ge(s["ident0"], 1)
            pool.affine_select(out=ident[:], in_=ident[:], compare_op=ALU.not_equal, fill=1.0, base=0,
                               pattern=[[-1, P]], channel_multiplier=1).then_inc(s["ident"], 1)

            def gather(i, u):
                reused(pool, "h0", i, U)
                pool.indirect_dma_start(row[:, u, :], None, emb, bass.IndirectOffsetOnAxis(
                    ap=words_T[:, i:i + 1], axis=0)).then_inc(row_in[u], 16)
                pool.indirect_dma_start(uval[:, u:u + 1], None, mask_u, bass.IndirectOffsetOnAxis(
                    ap=words_T[:, i:i + 1], axis=0)).then_inc(u_in[u], 16)

            pool.wait_ge(s["words_i"], 1)
            for i in range(AHEAD):
                gather(i, i % U)

            pool.memset(ident_b[:], 0.0).then_inc(s["const0"], 1)
            pool.memset(causal[:], 0.0).then_inc(s["const0"], 1)
            pool.memset(before[:], 1.0).then_inc(s["const0"], 1)
            pool.wait_ge(s["const0"], 3)
            pool.affine_select(out=ident_b[:], in_=ident_b[:], compare_op=ALU.not_equal, fill=1.0, base=0,
                               pattern=[[-1, P]], channel_multiplier=1).then_inc(s["consts"], 1)
            pool.affine_select(out=causal[:].rearrange("p (g k) -> p g k", g=G),
                               in_=causal[:].rearrange("p (g k) -> p g k", g=G), compare_op=ALU.is_ge, fill=MASKED,
                               base=0, pattern=[[0, G], [-1, P]], channel_multiplier=1).then_inc(s["consts"], 1)
            pool.affine_select(out=before[:], in_=before[:], compare_op=ALU.is_gt, fill=0.0, base=0,
                               pattern=[[1, P]], channel_multiplier=-1).then_inc(s["consts"], 1)
            pool.iota(iota_e[:], pattern=[[1, E]], base=0, channel_multiplier=0,
                      allow_small_or_imprecise_dtypes=True).then_inc(s["consts"], 1)
            pool.iota(iota_b[:], pattern=[[1, BLOCKS[0]]], base=0, channel_multiplier=0,
                      allow_small_or_imprecise_dtypes=True).then_inc(s["consts"], 1)

            def ready_to_scatter(part):
                pool.wait_ge(s["pos"], 2 * (part + 1))
                pool.wait_ge(s["zeroed"], 16 * sum(ZEROINGS))
                for u in range(U):
                    pool.wait_ge(hn_kept[u], 16 * len(range(u, FIRST_TILE[part] + PARTS[part], U)))

            def scatter(part, lo, hi):
                for n in range(lo, min(hi, 2 * PARTS[part])):
                    i, k = FIRST_TILE[part] + n // 2, n % 2
                    pool.indirect_dma_start(sorted_x[part], bass.IndirectOffsetOnAxis(ap=pos[:, k, i:i + 1], axis=0),
                                            hn[:, i, :], None).then_inc(s[f"scattered{part}"], 16)

            SCATTER0 = SORT0 + 2
            scattered = [0]

            def scatter_some(st, n):
                if st >= SCATTER0:
                    if scattered[0] == 0:
                        ready_to_scatter(0)
                    n = n if st < NT + SOFT else 2 * n
                    scatter(0, scattered[0], scattered[0] + n)
                    scattered[0] += n

            def step(st, u):
                if active(st, SCORE):
                    i, b = st - SCORE, (u - SCORE) % 2
                    pool.wait_ge(s["rope"], i + 1)
                    pool.wait_ge(s["norm_rs"], st)
                    reused(pool, "kT_ps", i)
                    pool.tensor_tensor(qh[:, b, :, DN:HD], rope_c[:, b], bc(norm_w[:, (u - 1) % 2, 4, 0:HK], DR),
                                       ALU.mult).then_inc(s["q_rope"], 1)
                if active(st, SOFT):
                    i, b = st - SOFT, (u - SOFT) % 2
                    reused(pool, "pT_ps", i)
                    c = slice(0, G * P)
                    pool.wait_ge(s["inv_half"], i + 1)
                    pool.tensor_tensor(probn[:, b, c].rearrange("p (h k) -> p h k", k=P),
                                       prob[:, b, c].rearrange("p (h k) -> p h k", k=P),
                                       bc(linv[:, b, 0:G], P), ALU.mult).then_inc(s["probn_half"], 1)
                if st + AHEAD < NT:
                    gather(st + AHEAD, (u + AHEAD) % U)
                else:
                    scatter_some(st, 2)
                if active(st, SOFT):
                    i, b = st - SOFT, (u - SOFT) % 2
                    c = slice(G * P, H * P)
                    pool.wait_ge(s["inv_sum"], i + 1)
                    pool.tensor_tensor(probn[:, b, c].rearrange("p (h k) -> p h k", k=P),
                                       prob[:, b, c].rearrange("p (h k) -> p h k", k=P),
                                       bc(linv[:, b, G:H], P), ALU.mult).then_inc(s["probn"], 1)
                if active(st, LN2):
                    i, b = st - LN2, (u - LN2) % 2
                    pool.wait_ge(s["xn2"], i + 1)
                    pool.tensor_tensor(res[:, bass.ds(i, 1), :], h1[:, b:b + 1, :], xn2[:, b:b + 1, :],
                                       ALU.add).then_inc(s["res"], 1)
                scatter_some(st, 2)
                if active(st, PROJ):
                    i, b = st - PROJ, (u - PROJ) % 2
                    pool.wait_ge(s["rope_hi"], i + 1)
                    pool.tensor_tensor(rope_c[:, b], rope_a[:, b], rope_b[:, b], ALU.add).then_inc(s["rope"], 1)
                scatter_some(st, 1)

            for st in range(STEPS_A):
                step(st, st % U)
            scatter(0, scattered[0], 2 * PARTS[0])
            ready_to_scatter(1)
            scatter(1, 0, 2 * PARTS[1])

            def fetch(part, i, u):
                reused(pool, "mixed", i, U)
                pool.indirect_dma_start(y1[:, u, :], None, sorted_y[part], bass.IndirectOffsetOnAxis(
                    ap=pos[:, 0, i:i + 1], axis=0)).then_inc(y1_in[u], 16)
                pool.indirect_dma_start(y2[:, u, :], None, sorted_y[part], bass.IndirectOffsetOnAxis(
                    ap=pos[:, 1, i:i + 1], axis=0)).then_inc(y2_in[u], 16)

            for part in range(2):
                for u in range(U):
                    pool.wait_ge(y_out[u], 16 * len(range(u, FIRST_BLOCK[part] + BLOCKS[part], U)))
                for i in range(FIRST_TILE[part], FIRST_TILE[part] + PARTS[part]):
                    fetch(part, i, i % U)

        @block.sync
        def _(sp):
            sp.dma_start(words[:], x).then_inc(s["words_in"], 16)
            sp.dma_start(wdq[:], W_DQ).then_inc(s["latent_in"], 16)
            sp.dma_start(wdkv[:], W_DKV).then_inc(s["latent_in"], 16)
            sp.dma_start(wuq[:, 0, :], W_UQ).then_inc(s["up_in"], 16)
            sp.dma_start(wuq[:, 1, :], W_QR).then_inc(s["up_in"], 16)
            sp.dma_start(wukv[:, 0:KVH * DN], W_UK).then_inc(s["up_in"], 16)
            sp.dma_start(wukv[:, KVH * DN:], W_UV).then_inc(s["up_in"], 16)
            for g in range(KVH):
                sp.dma_start(w_proj[:, (H + g) * HD + DN:(H + g + 1) * HD],
                             W_KR[:, g * DR:(g + 1) * DR]).then_inc(s["cols_in"], 16)
            sp.dma_start(w_proj[:, C_CQ:C_CKV], W_DQ).then_inc(s["cols_in"], 16)
            sp.dma_start(w_proj[:, C_CKV:C_END], W_DKV).then_inc(s["cols_in"], 16)
            for g in range(KVH):
                sp.dma_start(wvr[:, :, g, :],
                             W_VR[:, g * G * HD:(g + 1) * G * HD].rearrange("k (c d) -> k c d", c=G)
                             ).then_inc(s["wo_in"], 16)
                sp.dma_start(wo[g * HD:(g + 1) * HD],
                             W_O[g * G * HD:(g + 1) * G * HD, :].rearrange("(c d) n -> d c n", c=G)
                             ).then_inc(s["wo_in"], 16)
            sp.dma_start(w1[:].rearrange("p (e f) -> p e f", e=E),
                         W1.rearrange("e d f -> d e f")).then_inc(s["w1_in"], 16)
            sp.dma_start(w2[:].rearrange("p (e c d) -> p e c d", e=E, c=FC),
                         W2.rearrange("e (c p) d -> p e c d", p=P)).then_inc(s["w2_in"], 16)
            sp.dma_start(b2_bc[:], b2.rearrange("e d -> (e d)").partition_broadcast(P)).then_inc(s["b2_in"], 16)

            sp.wait_ge(s["ones"], 1)
            for part in range(2):
                with sp.Fori(0, ZEROINGS[part]) as z:
                    sp.dma_start(sorted_x[part][bass.ds(z * ZROWS, ZROWS), :].rearrange("(p r) d -> p (r d)", p=P),
                                 zero[:]).then_inc(s["zeroed"], 16)

            with sp.Fori(0, NT // U) as g:
                i = sp.snap(g * U)
                for u in range(U):
                    sp.wait_ge(s["hn"], i + u + 1)
                    sp.dma_start(hn[:, bass.ds(i + u, 1), :], hn_t[:, u:u + 1, :]).then_inc(hn_kept[u], 16)

            PUT = MIX0 + UC
            PUT1 = PUT + min(PARTS[0], NB - PUT) // U * U

            def put(i):
                sp.wait_ge(s["mixed"], i + 1)
                sp.dma_start(out[bass.ds(i, 1)].rearrange("a t d -> t a d"),
                             res[:, bass.ds(i, 1), :]).then_inc(s["out"], 16)

            def rows(buffers, part, n):
                return buffers[part][bass.ds((n - FIRST_BLOCK[part]) * P, P), :]

            def step(t, u, part=None):
                if within(t, 0):
                    reused(sp, "xsT_ps", t, U)
                    k = part if part is not None else int(t >= FIRST_BLOCK[1])
                    sp.dma_start(xs[:, u, :], rows(sorted_x, k, t)).then_inc(xs_in[u], 16)
                if within(t, STORE):
                    n, b4 = t - STORE, (u - STORE) % U
                    sp.wait_ge(s["y"], n + 1)
                    k = part if part is not None else int(n >= FIRST_BLOCK[1])
                    sp.dma_start(rows(sorted_y, k, n), ysb[:, b4, :]).then_inc(y_out[b4], 16)

            sp.wait_ge(s["scattered0"], 16 * 2 * PARTS[0])
            for t in range(2 * U):
                step(t, t % U)
            LOOP_END = FIRST_BLOCK[1] // U * U
            with groups(sp, 2 * U, LOOP_END) as t:
                for u in range(U):
                    step(t + u, u, 0)
            for t in range(LOOP_END, PUT):
                if t == FIRST_BLOCK[1]:
                    sp.wait_ge(s["scattered1"], 16 * 2 * PARTS[1])
                    sp.wait_ge(s["block_e"], 2)
                step(t, t % U)
            with groups(sp, PUT, PUT1) as t:
                for u in range(U):
                    step(t + u, u, 1)
                    put(t + (u - PUT))
            for t in range(PUT1, NB + STORE):
                step(t, t % U)
            with sp.Fori(PUT1 - PUT, NT) as i:
                put(i)
            sp.wait_ge(s["out"], 16 * NT)

        @block.tensor
        def _(pe):
            pe.wait_ge(s["ident"], 1)
            pe.wait_ge(s["words_f"], 1)
            pe.transpose(ms[:, 0:NT], words_f[:], ident[0:NT, 0:NT]).then_inc(s["wordsT_ps"], 1)

            pe.wait_ge(s["latent_in"], 32)
            pe.transpose(qo[0:RQ, 0:P], wdq[:], ident[:])
            pe.transpose(qo[:, P:2 * P], wdkv[:], ident[:]).then_inc(s["prep_pe"], 1)
            pe.wait_ge(s["prep_v"], PREP_LATENT)
            pe.matmul(pj[:, 0:H * HD], wdqT[:], wuq_s[:].rearrange("p h d -> p (h d)"), start=True, stop=True)
            pe.matmul(pj[:, H * HD:H * HD + KVH * (DN + HD)], wdkvT[:], wukv_s[:], start=True,
                      stop=True).then_inc(s["prep_pe"], 1)
            pe.wait_ge(s["rows_in"], 32)
            pe.transpose(sc[:, 0:E], wr_rows[:], ident[0:E, 0:E])
            pe.transpose(sc[:, P:P + E * FC], b1_rows[:], ident[0:E * FC, 0:E * FC]).then_inc(s["prep_pe"], 1)
            pe.wait_ge(s["prep_v"], PREP_PROJ)
            pe.wait_ge(s["consts"], 5)
            pe.wait_ge(s["cols_in"], 64)

            def sort(part):
                n = E * PARTS[part]
                to = (qo, sc)[part]
                pe.wait_ge(s["route_pick"], part + 1)
                if part == 0:
                    pe.wait_ge(s["qT"], SORT0 - SCORE + 1)
                pe.matmul(to[:, 0:n], before[:], r_pick[:, 0:n], start=True, stop=True)
                pe.matmul(to[:, 256:256 + n], ones_b[:], r_pick[:, 0:n], start=True,
                          stop=True).then_inc(s["route_pe"], 1)

            def fold_values(st):
                if isinstance(st, int) and st == WVR_STEP:
                    pe.wait_ge(s["prep_v"], PREP_ROWS)
                    pe.wait_ge(s["wo_in"], 16 * 2 * KVH)
                    for c in range(G):
                        last = pe.transpose(pt[:, c * P:(c + 1) * P], wvr[:, c].rearrange("p g d -> p (g d)"), ident[:])
                    last.then_inc(s["prep_pe"], 1)
                if isinstance(st, int) and st == WRES_STEP:
                    pe.wait_ge(s["prep_v"], PREP_WVR)
                    for c in range(G):
                        last = pe.matmul(pt[:, C_ATTN:C_ATTN + P], wvrT[:, c, :], wo[:, c, :], start=(c == 0),
                                         stop=(c == G - 1))
                    last.then_inc(s["prep_pe"], 1)

            def step(st, u):
                fold_values(st)
                if active(st, OUT):
                    i, b, b4 = st - OUT, (u - OUT) % 2, (u - OUT) % U
                    pe.wait_ge(s["pT_half"], i + 1)
                    pe.wait_ge(s["pT"], i + 1)
                    pe.wait_ge(s["v"], i + 1)
                    reused(pe, "oT", i, 1)
                    for g in range(KVH):
                        last = pe.matmul(pt[g * HD:(g + 1) * HD, 0:512], vt[:, b4, g * HD:(g + 1) * HD],
                                         pT[:, b, g * 512:(g + 1) * 512], start=True, stop=True)
                    last.then_inc(s["oT_ps"], 1)
                if active(st, OUT) or active(st, ROUTE):
                    if active(st, SOFT + 1):
                        pe.wait_ge(s["pT"], st - SOFT)
                    if active(st, OUT + 1):
                        pe.wait_ge(s["h1"], st - OUT)
                    if active(st, ROUTE + 1):
                        pe.wait_ge(s["logits"], st - ROUTE)
                if active(st, ROUTE):
                    i, b = st - ROUTE, (u - ROUTE) % 2
                    pe.wait_ge(s["hnT"], i + 1)
                    pe.matmul(pt[:, C_LOGITS:C_LOGITS + P], hnT[:, b, :], wr[:], start=True, stop=True
                              ).then_inc(s["logits_ps"], 1)
                if active(st, PROJ):
                    i, b4 = st - PROJ, (u - PROJ) % U
                    pe.wait_ge(s["xn"], i + 1)
                    if active(st, LN2 + 1):
                        pe.wait_ge(s["hnT"], st - LN2)
                    pe.transpose(ms[:, 0:P], xn[:, b4, :], ident[:]).then_inc(s["xnT_ps"], 1)
                if active(st, OUT):
                    i, b, b4 = st - OUT, (u - OUT) % 2, (u - OUT) % U
                    pe.wait_ge(s["oT"], i + 1)
                    at = pt[:, C_ATTN:C_ATTN + P]
                    for c in range(G):
                        pe.matmul(at, oT[:, b, c, :], wo[:, c, :], start=(c == 0), stop=False)
                    pe.matmul(at, xnT[:, b4, :], w_res[:], start=False, stop=True).then_inc(s["attn"], 1)
                if active(st, SCORE):
                    i, b = st - SCORE, (u - SCORE) % 2
                    pe.wait_ge(s["q_nope"], i + 1)
                    pe.wait_ge(s["q_rope"], i + 1)
                    reused(pe, "qT", i, 1)
                    if isinstance(st, int) and st == SORT0 + 1:
                        pe.wait_ge(s["route_v"], 1)
                    for c in range(G):
                        last = pe.transpose(qo[:, c * P:(c + 1) * P],
                                            qh[:, b, 2 * c:2 * c + 2, :].rearrange("p h d -> p (h d)"), ident[:])
                    last.then_inc(s["qT_ps"], 1)
                    pe.wait_ge(s["k_nope"], i + 1)
                    if active(st, PROJ):
                        pe.wait_ge(s["xnT"], st - PROJ + 1)
                    else:
                        pe.wait_ge(s["hnT"], st - LN2)
                    pe.transpose(ms[:, P:2 * P], qh[:, b, H:HK, :].rearrange("p h d -> p (h d)"),
                                 ident[:]).then_inc(s["kT_ps"], 1)
                if active(st, PROJ):
                    i, b4 = st - PROJ, (u - PROJ) % U
                    pe.wait_ge(s["xnT"], i + 1)
                    reused(pe, "q_nope", i, 1)
                    pe.matmul(pj[:, 0:512], xnT[:, b4, :], w_proj[:, 0:512], start=True, stop=True
                              ).then_inc(s["proj_q"], 1)
                    reused(pe, "v", i, 1)
                    pe.matmul(pj[:, 512:C_END], xnT[:, b4, :], w_proj[:, 512:C_END], start=True,
                              stop=True).then_inc(s["proj"], 1)
                if active(st, SOFT):
                    i, b = st - SOFT, (u - SOFT) % 2
                    pe.wait_ge(s["probn_half"], i + 1)
                    reused(pe, "pT_half", i, 1)
                    if active(st, OUT):
                        pe.wait_ge(s["oT"], st - OUT + 1)
                    for h in range(G):
                        last = pe.transpose(pt[:, h * P:(h + 1) * P], probn[:, b, h * P:(h + 1) * P], ident[:])
                    last.then_inc(s["pT_half_ps"], 1)
                if isinstance(st, int) and st == SORT0:
                    sort(0)
                if active(st, SCORE):
                    i, b = st - SCORE, (u - SCORE) % 2
                    pe.wait_ge(s["qT"], i + 1)
                    pe.wait_ge(s["kT"], i + 1)
                    reused(pe, "probs", i, 1)
                    for g in range(KVH):
                        pe.matmul(sc[:, g * 512:(g + 1) * 512], ident_b[:], causal[:], start=True, stop=False,
                                  skip_group_check=True)
                    for c in range(G):
                        for g in range(KVH):
                            r = slice(g * HD, (g + 1) * HD)
                            at = g * 512 + c * P
                            last = pe.matmul(sc[:, at:at + P], qT[r, b, c, :], kT[r, b, :], start=False,
                                             stop=(c == G - 1), skip_group_check=True)
                    last.then_inc(s["scores"], 1)
                if active(st, SOFT):
                    i, b = st - SOFT, (u - SOFT) % 2
                    pe.wait_ge(s["probn"], i + 1)
                    reused(pe, "pT", i, 1)
                    if isinstance(st, int) and st == WRES_STEP:
                        pe.wait_ge(s["prep_v"], PREP_ALL)
                    if active(st, OUT):
                        pe.wait_ge(s["h1"], st - OUT + 1)
                    if active(st, ROUTE):
                        pe.wait_ge(s["logits"], st - ROUTE + 1)
                    for h in range(G, H):
                        last = pe.transpose(pt[:, h * P:(h + 1) * P], probn[:, b, h * P:(h + 1) * P], ident[:])
                    last.then_inc(s["pT_ps"], 1)
                if active(st, LN2):
                    i = st - LN2
                    pe.wait_ge(s["hn"], i + 1)
                    if active(st, SCORE):
                        pe.wait_ge(s["kT"], st - SCORE + 1)
                    else:
                        pe.wait_ge(s["hnT"], i)
                    pe.transpose(ms[:, 2 * P:3 * P], hn_t[:, (u - LN2) % U, :], ident[:]).then_inc(s["hnT_ps"], 1)

            steps_a(pe, step)

            def step_c(t, u):
                if within(t, FFN2):
                    e = pe.value_load(block_e[0:1, bass.ds(t - FFN2, 1)], min_val=0, max_val=E - 1)
                if within(t, 0):
                    pe.wait_ge(xs_in[u % U], turn(t, u % U) + 16)
                    reused(pe, "xsT", t)
                    tp = (qo, ms)[u % 2]
                    pe.transpose(tp[:, 0:P], xs[:, u % U, :], ident[:]).then_inc(s["xsT_ps"], 1)
                if within(t, FFN1):
                    n, b = t - FFN1, (u - FFN1) % 2
                    pe.wait_ge(s["xsT"], n + 1)
                    pe.wait_ge(s["w1_copy"], n + 1)
                    reused(pe, "hid", n)
                    for c in range(FC):
                        last = pe.matmul(pt[:, b * 512 + c * P:b * 512 + (c + 1) * P], w1s[:, b, c * P:(c + 1) * P],
                                         xsT[:, b, :], start=True, stop=True)
                    last.then_inc(s["hid_ps"], 1)
                if within(t, FFN2):
                    n, b = t - FFN2, (u - FFN2) % 2
                    pe.wait_ge(s["hid"], n + 1)
                    reused(pe, "y", n)
                    for c in range(FC):
                        last = pe.matmul(pj[:, b * 512:b * 512 + P], hid[:, b, c, :],
                                         w2[:, bass.ds(e * (FC * P) + c * P, P)], start=(c == 0), stop=(c == FC - 1))
                    last.then_inc(s["y_ps"], 1)

            pe.wait_ge(s["w2_in"], 16)
            for done in ("logits", "h1", "q_nope", "v", "probs", "pT_half", "pT", "hnT", "oT"):
                pe.wait_ge(s[done], NT)
            pe.wait_ge(s["block_e"], 1)
            for t in range(UC):
                step_c(t, t)
                if t == 0:
                    sort(1)
            with groups(pe, *LOOP_C, UC) as t:
                for u in range(UC):
                    step_c(t + u, u)
            for t in range(LOOP_C[1], STEPS_C):
                step_c(t, t % UC)

        @block.scalar
        def _(act):
            act.preload_act_table_set("natural_log_exp_and_others")
            def col(v):
                return v.rearrange("(p a) -> p a", a=1)

            act.dma_start(qln[:], col(q_ln_w)).then_inc(s["vec_in"], 16)
            act.dma_start(kvln[:], col(kv_ln_w)).then_inc(s["vec_in"], 16)
            for g in range(KVH):
                act.dma_start(hn_w[g * HD:(g + 1) * HD, 0:1], col(q_hn_w)).then_inc(s["vec_in"], 16)
                act.dma_start(hn_w[g * HD:(g + 1) * HD, 1:2], col(k_hn_w)).then_inc(s["vec_in"], 16)
            act.dma_start(wr_rows[:], w_r).then_inc(s["rows_in"], 16)
            act.dma_start(b1_rows[:], b1.rearrange("e (c p) -> (e c) p", p=P)).then_inc(s["rows_in"], 16)
            act.dma_start(rope_sb[:], rope_table).then_inc(s["vec2_in"], 16)
            act.dma_start(g_col[:], col(ln_g)).then_inc(s["vec2_in"], 16)
            act.dma_start(b_col[:], col(ln_b)).then_inc(s["vec2_in"], 16)
            act.dma_start(br_bc[:], b_r.partition_broadcast(P)).then_inc(s["vec2_in"], 16)

            def exps(st, u, heads, done):
                i, b = st - SOFT, (u - SOFT) % 2
                for h in heads:
                    last = act.activation(prob[:, b, h * P:(h + 1) * P], sc[:, h * P:(h + 1) * P], ACT.Exp,
                                          bias=nmax[:, b, h:h + 1], accum_out=lsum[:, b, h:h + 1])
                if done is not None:
                    last.then_inc(s[done], 1)

            def step(st, u):
                if active(st, SOFT):
                    act.wait_ge(s["neg_max"], st - SOFT + 1)
                    reused(act, "probn", st - SOFT)
                    exps(st, u, range(0, 2), None)
                if active(st, OUT):
                    i, b = st - OUT, (u - OUT) % 2
                    act.wait_ge(s["oT_ps"], i + 1)
                    reused(act, "attn", i)
                    act.copy(oT[:, b].rearrange("p c t -> p (c t)"), pt[:, 0:512]).then_inc(s["oT"], 1)
                if active(st, SOFT):
                    exps(st, u, range(2, G), "probs_half")
                if active(st, PROJ):
                    i, b4 = st - PROJ, (u - PROJ) % U
                    act.wait_ge(s["xnT_ps"], i + 1)
                    reused(act, "attn", i, U)
                    act.copy(xnT[:, b4, :], ms[:, 0:P]).then_inc(s["xnT"], 1)
                if active(st, SCORE):
                    i, b, b4 = st - SCORE, (u - SCORE) % 2, (u - SCORE) % U
                    act.wait_ge(s["k_nope"], i + 1)
                    reused(act, "oT_ps", i, U)
                    act.activation(vt[:, b4, :], pj[:, C_V:C_CQ], ACT.Copy,
                                   scale=norm_w[:, (u - 1) % 2, 4, X_KV:X_KV + 1]).then_inc(s["v"], 1)
                if active(st, SOFT):
                    exps(st, u, range(G, G + 2), None)
                if active(st, SCORE):
                    i, b = st - SCORE, (u - SCORE) % 2
                    act.wait_ge(s["qT_ps"], i + 1)
                    reused(act, "scores", i)
                    act.copy(qT[:, b].rearrange("p c t -> p (c t)"), qo[:]).then_inc(s["qT"], 1)
                    act.wait_ge(s["kT_ps"], i + 1)
                    act.activation(kT[:, b, :], ms[:, P:2 * P], ACT.Copy, scale=qk_w[:, 0:1]).then_inc(s["kT"], 1)
                if active(st, SOFT):
                    exps(st, u, range(G + 2, H), "probs")
                if active(st, PROJ):
                    i, b = st - PROJ, (u - PROJ) % 2
                    act.wait_ge(s["proj_q"], i + 1)
                    reused(act, "head_x", i)
                    act.activation(sq[:, b, 0:512], pj[:, 0:512], ACT.Square).then_inc(s["squares_q"], 1)
                if active(st, PROJ):
                    i, b = st - PROJ, (u - PROJ) % 2
                    act.wait_ge(s["proj"], i + 1)
                    act.activation(sq[:, b, 512:C_V], pj[:, 512:C_V], ACT.Square)
                    act.activation(sq_latq[:, b, :], pj[:, C_CQ:C_CKV], ACT.Square, accum_out=ss_lat[:, b, 0:1])
                    act.activation(sq_lat[:, b, :], pj[:, C_CKV:C_END], ACT.Square,
                                   accum_out=ss_lat[:, b, 1:2]).then_inc(s["squares"], 1)
                if active(st, SOFT):
                    i, b = st - SOFT, (u - SOFT) % 2
                    act.wait_ge(s["pT_half_ps"], i + 1)
                    reused(act, "oT_ps", i)
                    act.copy(pT[:, b, 0:512], pt[:, 0:512]).then_inc(s["pT_half"], 1)
                if normed(st + 1):
                    for sem, lag in (("head_x", PROJ), ("ln1_x", LN1), ("ln2_x", OUT)):
                        if active(st, lag):
                            act.wait_ge(s[sem], st - lag + 1)
                    w = norm_w[:, u % 2]
                    act.activation(w[:, 0, :], norm_x[:, u % 2, :], ACT.Ln).then_inc(s["norm_log"], 1)
                    act.wait_ge(s["norm_log"], st + 1)
                    act.activation(w[:, 1, :], w[:, 0, :], ACT.Exp, scale=-0.5).then_inc(s["norm_exp"], 1)
                if active(st, SOFT):
                    i, b = st - SOFT, (u - SOFT) % 2
                    act.wait_ge(s["pT_ps"], i + 1)
                    act.copy(pT[:, b, 512:1024], pt[:, 512:1024]).then_inc(s["pT"], 1)
                if active(st, LN2):
                    i, b = st - LN2, (u - LN2) % 2
                    act.wait_ge(s["hnT_ps"], i + 1)
                    reused(act, "logits_ps", i)
                    act.activation(hnT[:, b, :], ms[:, 2 * P:3 * P], ACT.Identity, bias=b_col[:, 0:1],
                                   scale=g_col[:, 0:1]).then_inc(s["hnT"], 1)

            step(0, 0)
            act.wait_ge(s["vec2_in"], 64)
            act.wait_ge(s["prep_v"], PREP_PROJ)
            steps_a(act, step, 1)

            for part in range(2):
                c = slice(FIRST_TILE[part], FIRST_TILE[part] + PARTS[part])
                act.wait_ge(s["route_pick"], part + 1)
                act.activation(gate_e[:, c], gap[:, c], ACT.Exp).then_inc(s["gate_exp"], 1)

            def step_c(t, u):
                if within(t, 0):
                    b = u % 2
                    act.wait_ge(s["xsT_ps"], t + 1)
                    reused(act, "hid_ps", t)
                    act.activation(xsT[:, b, :], (qo, ms)[b][:, 0:P], ACT.Identity, bias=b_col[:, 0:1],
                                   scale=g_col[:, 0:1]).then_inc(s["xsT"], 1)
                if within(t, FFN1):
                    n, b = t - FFN1, (u - FFN1) % 2
                    act.wait_ge(s["hid_ps"], n + 1)
                    reused(act, "y_ps", n)
                    for c in range(FC):
                        last = act.activation(hid[:, b, c, :], pt[:, b * 512 + c * P:b * 512 + (c + 1) * P], ACT.Gelu,
                                              bias=b1s[:, b, c:c + 1])
                    last.then_inc(s["hid"], 1)

            for t in range(UC):
                step_c(t, t)
            with groups(act, *LOOP_C, UC) as t:
                for u in range(UC):
                    step_c(t + u, u)
            for t in range(LOOP_C[1], STEPS_C):
                step_c(t, t % UC)

        @block.vector
        def _(dve):
            def then(ins, sem, value):
                ins.then_inc(s[sem], 1)
                dve.wait_ge(s[sem], value)

            dve.wait_ge(s["words_in"], 16)
            dve.tensor_copy(words_f[:], words[:]).then_inc(s["words_f"], 1)
            dve.memset(zero[:], 0.0)
            dve.memset(norm_x[:], 1.0)
            dve.memset(ones_b[:], 1.0)
            dve.memset(ones_f[:], 1.0)
            dve.memset(wr[:], 0.0).then_inc(s["ones"], 1)
            dve.wait_ge(s["wordsT_ps"], 1)
            dve.tensor_copy(words_T[:], ms[:, 0:NT]).then_inc(s["words_i"], 1)

            links = [0, 0]

            def sort(part, stages):
                nt = PARTS[part]
                n = E * nt
                t0 = FIRST_TILE[part]
                nb = BLOCKS[part]
                counted = (qo, sc)[part]

                def signal(ins):
                    links[part] += 1
                    ins.then_inc(s[f"sort{part}"], 1)
                    return links[part]

                def wait(value):
                    dve.wait_ge(s[f"sort{part}"], value)

                def link(ins):
                    wait(signal(ins))

                sel = [pick[:, k, :, t0:t0 + nt] for k in range(2)]
                tiles = lambda ap: ap.rearrange("p (e t) -> p e t", e=E)
                ends = tiles(r_run[:, 0:n])[:, :, nt - 1:nt].rearrange("p e o -> p (e o)")
                start, blk, upto, off, tmp = (r_small[:, k, :] for k in range(5))
                if 0 in stages:
                    dve.wait_ge(s["pick"], 2 * (t0 + nt))
                    dve.wait_ge(s["gap"], t0 + nt)
                    dve.tensor_tensor(tiles(r_pick[:, 0:n]), sel[0], sel[1], ALU.add).then_inc(s["route_pick"], 1)
                if 1 in stages:
                    dve.wait_ge(s["route_pe"], part + 1)
                    dve.tensor_copy(r_cnt[:, 0:n], counted[:, 256:256 + n])
                    dve.tensor_copy(r_rank[:, 0:n], counted[:, 0:n]).then_inc(s["route_v"], 1)
                if 2 in stages:
                    dve.memset(start[:, 0:1], 0.0)
                    dve.wait_ge(s["route_v"], part + 1)
                    link(dve.tensor_tensor_scan(r_run[:, 0:n], ones_f[:, 0:n], r_cnt[:, 0:n], 0.0, ALU.mult, ALU.add))
                    signal(dve.tensor_copy(start[:, 1:E], ends[:, 0:E - 1]))
                    wait(links[part])
                    counts = signal(dve.scalar_tensor_tensor(
                        out=r_int[:, 0, :], in0=ends, scalar=float(P - 1), in1=start, op0=ALU.add, op1=ALU.subtract))
                    signal(dve.tensor_tensor(r_pos[:, 0:n], r_run[:, 0:n], r_cnt[:, 0:n], ALU.subtract))
                    wait(counts)
                    blocks = signal(dve.tensor_scalar(r_int[:, 1, :], r_int[:, 0, :], P.bit_length() - 1, None,
                                                      ALU.arith_shift_right))
                    wait(blocks)
                    blocks = signal(dve.tensor_copy(blk, r_int[:, 1, :]))
                    signal(dve.tensor_tensor(r_pos[:, 0:n], r_pos[:, 0:n], r_rank[:, 0:n], ALU.add))
                    wait(blocks)
                    signal(dve.tensor_tensor_scan(upto, ones_f[:, 0:E], blk, 0.0, ALU.mult, ALU.add))
                if 3 in stages:
                    wait(links[part])
                    link(dve.tensor_tensor(tmp, upto, blk, ALU.subtract))
                    link(dve.scalar_tensor_tensor(out=off, in0=tmp, scalar=float(P), in1=start, op0=ALU.mult,
                                                  op1=ALU.subtract))
                    signal(dve.tensor_tensor(tiles(r_pos[:, 0:n]), tiles(r_pos[:, 0:n]),
                                             off.unsqueeze(2).to_broadcast([P, E, nt]), ALU.add))
                if 4 in stages:
                    wait(links[part])
                    chosen = [signal(dve.tensor_tensor(tiles(r_sel[:, k, 0:n]), tiles(r_pos[:, 0:n]), sel[k], ALU.mult))
                              for k in range(2)]
                    for k in range(2):
                        wait(chosen[k])
                        chosen[k] = signal(dve.tensor_reduce(
                            r_posf[:, k, 0:nt], r_sel[:, k, 0:n].rearrange("p (e t) -> p t e", e=E), AX.X, ALU.add))
                    for k in range(2):
                        wait(chosen[k])
                        dve.tensor_copy(pos[:, k, t0:t0 + nt], r_posf[:, k, 0:nt]).then_inc(s["pos"], 1)
                if 5 in stages:
                    link(dve.tensor_tensor(r_cmp[:, 0:nb, :], iota_b[:, 0:nb].unsqueeze(2).to_broadcast([P, nb, E]),
                                           upto.unsqueeze(1).to_broadcast([P, nb, E]), ALU.is_ge))
                    signal(dve.tensor_reduce(r_blk[:, 0, 0:nb], r_cmp[:, 0:nb, :], AX.X, ALU.add))
                if 6 in stages:
                    wait(links[part])
                    link(dve.tensor_scalar(r_blk[:, 1, 0:nb], r_blk[:, 0, 0:nb], float(E - 1), None, ALU.min))
                    dve.tensor_copy(block_e[0:1, FIRST_BLOCK[part]:FIRST_BLOCK[part] + nb],
                                    r_blk[0:1, 1, 0:nb]).then_inc(s["block_e"], 1)

            SORT_PLACES = (((0,), (), (1,)), ((), (2,), (3,)), ((), (4,), (5,)), ((), (6,), ()))

            def sort_in_step(st, place):
                if isinstance(st, int) and SORT0 <= st < SORT0 + len(SORT_PLACES):
                    sort(0, SORT_PLACES[st - SORT0][place])

            def fold_values(st):
                if isinstance(st, int) and st == WVR_STEP:
                    dve.wait_ge(s["prep_pe"], 4)
                    dve.tensor_copy(wvrT[:].rearrange("p c n -> p (c n)"), pt[:, 0:512]).then_inc(s["prep_v"], 1)
                if isinstance(st, int) and st == WRES_STEP:
                    dve.wait_ge(s["prep_pe"], 5)
                    dve.tensor_copy(w_res[:], pt[:, C_ATTN:C_ATTN + P]).then_inc(s["prep_v"], 1)

            def step(st, u):
                sort_in_step(st, 0)
                fold_values(st)
                x_b, r_b = u % 2, (u - 1) % 2
                rs = norm_w[:, r_b, 4, :]
                y, w1_, w2_ = (norm_w[:, r_b, k, :] for k in (1, 2, 3))
                t0_, t4 = st - LN1, (u - LN1) % U
                h0 = res[:, bass.ds(t0_, 1), :] if active(st, LN1) else None
                if active(st, LN1):
                    dve.wait_ge(row_in[t4], turn(t0_, t4) + 16)
                    dve.wait_ge(u_in[t4], turn(t0_, t4) + 16)
                    dve.tensor_scalar(keep[:, t4:t4 + 1], uval[:, t4:t4 + 1], KEEP, 1.0 / KEEP, ALU.is_lt,
                                      ALU.mult).then_inc(s["keep"], 1)
                if normed(st):
                    dve.wait_ge(s["norm_exp"], st)
                    if active(st, SCORE):
                        reused(dve, "q_rope", st - SCORE)
                        reused(dve, "v", st - SCORE)
                    dve.scalar_tensor_tensor(out=w1_, in0=y, scalar=-0.5, in1=y, op0=ALU.mult, op1=ALU.mult
                                             ).then_inc(s["norm_n1"], 1)
                if active(st, LN1):
                    dve.wait_ge(s["keep"], t0_ + 1)
                    dve.tensor_scalar(h0, row[:, t4:t4 + 1, :], keep[:, t4:t4 + 1], None, ALU.mult).then_inc(s["h0"], 1)
                if normed(st):
                    dve.wait_ge(s["norm_n1"], st)
                    dve.tensor_tensor(w2_, w1_, norm_x[:, r_b, :], ALU.mult).then_inc(s["norm_n2"], 1)
                if active(st, LN1):
                    apart(dve)
                    dve.wait_ge(s["h0"], t0_ + 1)
                    dve.bn_stats(st1[:, t4, :], h0.rearrange("p a d -> p (a d)")).then_inc(s["ln1_stats"], 1)
                if normed(st):
                    dve.wait_ge(s["norm_n2"], st)
                    dve.scalar_tensor_tensor(out=rs, in0=w2_, scalar=1.5, in1=y, op0=ALU.add,
                                             op1=ALU.mult).then_inc(s["norm_rs"], 1)
                if normed(st):
                    dve.wait_ge(s["norm_rs"], st)
                if active(st, PROJ):
                    i, b4 = st - PROJ, (u - PROJ) % U
                    reused(dve, "xnT_ps", i, U)
                    dve.tensor_scalar(xn[:, b4:b4 + 1, :], res[:, bass.ds(i, 1), :], mv1[:, b4, 0:1],
                                      rs[:, X_LN1:X_LN1 + 1], ALU.subtract, ALU.mult).then_inc(s["xn"], 1)
                if active(st, SCORE):
                    i, b = st - SCORE, (u - SCORE) % 2
                    pr = heads(pj[:, 0:C_V])
                    reused(dve, "kT_ps", i)
                    dve.tensor_tensor(qh[:, b, 0:H, 0:DN], pr[:, 0:H, 0:DN], bc(rs[:, 0:H], DN), ALU.mult
                                      ).then_inc(s["q_nope"], 1)
                    dve.tensor_scalar(small[:, b, 14:16], rs[:, H:HK], rs[:, X_KV:X_KV + 1], None,
                                      ALU.mult).then_inc(s["kn_scale"], 1)
                if active(st, LN1):
                    apart(dve)
                    dve.wait_ge(s["ln1_stats"], t0_ + 1)
                    dve.bn_aggr(mv1[:, t4, :], st1[:, t4, :]).then_inc(s["ln1_mv"], 1)
                if active(st, SCORE):
                    i, b = st - SCORE, (u - SCORE) % 2
                    dve.wait_ge(s["kn_scale"], i + 1)
                    dve.tensor_tensor(qh[:, b, H:HK, 0:DN], pr[:, H:HK, 0:DN], bc(small[:, b, 14:16], DN), ALU.mult
                                      ).then_inc(s["k_nope"], 1)
                if active(st, LN1):
                    dve.wait_ge(s["ln1_mv"], t0_ + 1)
                    dve.tensor_scalar(norm_x[:, x_b, X_LN1:X_LN1 + 1], mv1[:, t4, 1:2], LN_EPS, None,
                                      ALU.add).then_inc(s["ln1_x"], 1)
                if active(st, SOFT):
                    i, b = st - SOFT, (u - SOFT) % 2
                    dve.wait_ge(s["probs_half"], i + 1)
                    reused(dve, "probn", i)
                    dve.reciprocal(linv[:, b, 0:G], lsum[:, b, 0:G]).then_inc(s["inv_half"], 1)
                if active(st, LN2):
                    i, b = st - LN2, (u - LN2) % 2
                    reused(dve, "res", i)
                    dve.tensor_scalar(xn2[:, b, :], h1[:, b, :], mv2[:, b, 0:1], rs[:, X_LN2:X_LN2 + 1],
                                      ALU.subtract, ALU.mult).then_inc(s["xn2"], 1)
                sort_in_step(st, 1)
                if active(st, OUT):
                    i, b = st - OUT, (u - OUT) % 2
                    dve.wait_ge(s["attn"], i + 1)
                    if active(st, ROUTE):
                        dve.wait_ge(s["logits_ps"], st - ROUTE + 1)
                    reused(dve, "res", i)
                    dve.tensor_tensor(h1[:, b:b + 1, :], res[:, bass.ds(i, 1), :],
                                      pt[:, C_ATTN:C_ATTN + P].unsqueeze(1), ALU.add).then_inc(s["h1"], 1)
                if active(st, ROUTE):
                    i, b = st - ROUTE, (u - ROUTE) % 2
                    dve.wait_ge(s["logits_ps"], i + 1)
                    dve.tensor_tensor(logit[:, b, :], pt[:, C_LOGITS:C_LOGITS + E], br_bc[:],
                                      ALU.add).then_inc(s["logits"], 1)
                if active(st, LN2):
                    i, b = st - LN2, (u - LN2) % 2
                    dve.wait_ge(s["xn2"], i + 1)
                    reused(dve, "hnT_ps", i, U)
                    b4 = (u - LN2) % U
                    if not (isinstance(i, int) and i < U):
                        dve.wait_ge(hn_kept[b4], turn(i, b4))
                    dve.tensor_scalar(hn_t[:, b4, :], xn2[:, b, :], rs[:, X_LN2 + 1:X_LN2 + 2], None,
                                      ALU.mult).then_inc(s["hn"], 1)
                if active(st, OUT):
                    i, b = st - OUT, (u - OUT) % 2
                    dve.wait_ge(s["h1"], i + 1)
                    dve.bn_stats(st2[:, b, :], h1[:, b, :]).then_inc(s["ln2_stats"], 1)
                if active(st, ROUTE):
                    i, b = st - ROUTE, (u - ROUTE) % 2
                    apart(dve)
                    dve.wait_ge(s["logits"], i + 1)
                    dve.max(top[:, b, :], logit[:, b, :]).then_inc(s["top"], 1)
                if active(st, OUT):
                    i, b = st - OUT, (u - OUT) % 2
                    apart(dve)
                    dve.wait_ge(s["ln2_stats"], i + 1)
                    dve.bn_aggr(mv2[:, b, :], st2[:, b, :]).then_inc(s["ln2_mv"], 1)
                if active(st, ROUTE):
                    i, b = st - ROUTE, (u - ROUTE) % 2
                    apart(dve)
                    dve.wait_ge(s["top"], i + 1)
                    dve.max_index(top_i[:, b, :], top[:, b, :], logit[:, b, :]).then_inc(s["top_idx"], 1)
                x2 = norm_x[:, x_b, X_LN2:X_LN2 + 2]
                if active(st, OUT):
                    i, b = st - OUT, (u - OUT) % 2
                    dve.wait_ge(s["ln2_mv"], i + 1)
                    dve.tensor_scalar(x2[:, 0:1], mv2[:, b, 1:2], LN_EPS, None, ALU.add).then_inc(s["ln2_v"], 1)
                if active(st, ROUTE):
                    i, b = st - ROUTE, (u - ROUTE) % 2
                    dve.wait_ge(s["top_idx"], i + 1)
                    dve.tensor_copy(top_f[:, b, :], top_i[:, b, 0:2]).then_inc(s["top_f"], 1)
                    dve.tensor_scalar(gap[:, bass.ds(i, 1)], top[:, b, 1:2], top[:, b, 0:1], None,
                                      ALU.subtract).then_inc(s["gap"], 1)
                if active(st, OUT):
                    i, b = st - OUT, (u - OUT) % 2
                    dve.wait_ge(s["ln2_v"], i + 1)
                    dve.reciprocal(inv2[:, b:b + 1], x2[:, 0:1]).then_inc(s["ln2_inv"], 1)
                if active(st, ROUTE):
                    i, b = st - ROUTE, (u - ROUTE) % 2
                    dve.wait_ge(s["top_f"], i + 1)
                    for k in range(2):
                        dve.tensor_scalar(pick[:, k, :, bass.ds(i, 1)], iota_e[:].unsqueeze(2), top_f[:, b, k:k + 1],
                                          None, ALU.is_equal).then_inc(s["pick"], 1)
                if active(st, OUT):
                    i, b = st - OUT, (u - OUT) % 2
                    dve.wait_ge(s["ln2_inv"], i + 1)
                    dve.tensor_scalar(x2[:, 1:2], mv2[:, b, 1:2], inv2[:, b:b + 1], LN_EPS, ALU.mult,
                                      ALU.add).then_inc(s["ln2_x"], 1)
                if active(st, SOFT):
                    i, b = st - SOFT, (u - SOFT) % 2
                    dve.wait_ge(s["probs"], i + 1)
                    dve.reciprocal(linv[:, b, G:H], lsum[:, b, G:H]).then_inc(s["inv_sum"], 1)
                sort_in_step(st, 2)
                if active(st, PROJ):
                    i, b = st - PROJ, (u - PROJ) % 2
                    sm = small[:, b, :]
                    x = norm_x[:, x_b, :]
                    rot = heads(pj[:, 0:C_V])[:, :, DN:HD]
                    half = DR // 2
                    dve.wait_ge(s["squares_q"], i + 1)
                    dve.tensor_reduce(ss[:, b, 0:2 * H], sq[:, b, 0:512].rearrange("p (n d) -> p n d", d=DN), AX.X,
                                      ALU.add).then_inc(s["q_squares"], 1)
                    dve.wait_ge(s["squares"], i + 1)
                    dve.tensor_reduce(ss[:, b, 2 * H:2 * HK], sq[:, b, 512:C_V].rearrange("p (n d) -> p n d", d=DN),
                                      AX.X, ALU.add)
                    dve.tensor_scalar(x[:, X_KV:X_KV + 1], ss_lat[:, b, 1:2], 1.0 / P, RMS_EPS, ALU.mult,
                                      ALU.add).then_inc(s["kv_x"], 1)
                    dve.tensor_scalar(sm[:, 1:2], ss_lat[:, b, 0:1], RMS_EPS / RQ, RMS_EPS * RMS_EPS, ALU.mult, ALU.add)
                    dve.wait_ge(s["q_squares"], i + 1)
                    dve.tensor_tensor(sm[:, 2:2 + H], ss[:, b, 0:2 * H:2], ss[:, b, 1:2 * H:2],
                                      ALU.add).then_inc(s["q_sum"], 1)
                    dve.wait_ge(s["kv_x"], i + 1)
                    dve.reciprocal(sm[:, 0:1], x[:, X_KV:X_KV + 1]).then_inc(s["kv_inv"], 1)
                    reused(dve, "rope", i)
                    dve.tensor_tensor(rope_a[:, b], rot, over_heads(cos, HK), ALU.mult)
                    dve.wait_ge(s["kv_inv"], i + 1)
                    dve.scalar_tensor_tensor(out=sm[:, 2 + H:2 + HK], in0=ss[:, b, 2 * H::2], scalar=sm[:, 0:1],
                                             in1=ss[:, b, 2 * H + 1::2], op0=ALU.mult, op1=ALU.add
                                             ).then_inc(s["k_sum"], 1)
                    dve.tensor_tensor(rope_b[:, b, :, 0:half], rot[:, :, half:DR], over_heads(sin[:, 0:half], HK),
                                      ALU.mult)
                    dve.wait_ge(s["q_sum"], i + 1)
                    dve.wait_ge(s["k_sum"], i + 1)
                    dve.tensor_scalar(x[:, 0:H], sm[:, 2:2 + H], 1.0 / HD, sm[:, 1:2], ALU.mult, ALU.add)
                    dve.tensor_scalar(x[:, H:HK], sm[:, 2 + H:2 + HK], 1.0 / HD, RMS_EPS, ALU.mult,
                                      ALU.add).then_inc(s["head_x"], 1)
                    dve.tensor_tensor(rope_b[:, b, :, half:DR], rot[:, :, 0:half], over_heads(sin[:, half:DR], HK),
                                      ALU.mult).then_inc(s["rope_hi"], 1)
                if active(st, SCORE):
                    i, b = st - SCORE, (u - SCORE) % 2
                    dve.wait_ge(s["scores"], i + 1)
                    reused(dve, "probs", i)
                    dve.tensor_reduce(nmax[:, b, :], sc[:].rearrange("p (h k) -> p h k", k=P), AX.X, ALU.max,
                                      negate=True).then_inc(s["neg_max"], 1)

            step(0, 0)
            dve.wait_ge(s["vec_in"], 16 * (2 + 2 * KVH))
            dve.wait_ge(s["up_in"], 64)
            for k in range(2):
                dve.tensor_scalar(wuq_s[:, :, k * DN:(k + 1) * DN].rearrange("k (c g) d -> k g c d", g=KVH),
                                  wuq[:, k, :].rearrange("k (g c d) -> k g c d", g=KVH, c=G), qln[:, 0:1], None,
                                  ALU.mult).then_inc(s["prep_v"], 1)
            dve.tensor_scalar(wukv_s[:], wukv[:], kvln[:, 0:1], None, ALU.mult).then_inc(s["prep_v"], 1)
            dve.tensor_scalar(qk_w[:], hn_w[:, 0:1], hn_w[:, 1:2], float(HD) ** -0.5, ALU.mult,
                              ALU.mult).then_inc(s["prep_v"], 1)
            dve.wait_ge(s["prep_pe"], 1)
            dve.tensor_copy(wdqT[:], qo[0:RQ, 0:P]).then_inc(s["prep_v"], 1)
            dve.tensor_copy(wdkvT[:], qo[:, P:2 * P]).then_inc(s["prep_v"], 1)
            dve.wait_ge(s["prep_pe"], 2)
            dve.tensor_copy(w_proj[:, 0:H * HD], pj[:, 0:H * HD]).then_inc(s["prep_v"], 1)
            dve.tensor_copy(heads(w_proj[:, H * HD:C_V])[:, :, 0:DN],
                            pj[:, H * HD:H * HD + KVH * DN].rearrange("p (g d) -> p g d", g=KVH)
                            ).then_inc(s["prep_v"], 1)
            dve.tensor_copy(w_proj[:, C_V:C_CQ], pj[:, H * HD + KVH * DN:H * HD + KVH * (DN + HD)]
                            ).then_inc(s["prep_v"], 1)
            dve.wait_ge(s["prep_pe"], 3)
            dve.wait_ge(s["ones"], 1)
            dve.tensor_copy(wr[:, 0:E], sc[:, 0:E]).then_inc(s["prep_v"], 1)
            dve.tensor_copy(b1c[:], sc[:, P:P + E * FC]).then_inc(s["prep_v"], 1)
            dve.wait_ge(s["vec2_in"], 64)
            dve.wait_ge(s["consts"], 5)
            dve.wait_ge(s["prep_v"], PREP_PROJ)
            steps_a(dve, step, 1)

            dve.wait_ge(s["w1_in"], 16)
            dve.wait_ge(s["b2_in"], 16)

            def mix1(i, u):
                dve.wait_ge(y1_in[u], turn(i, u) + 16)
                at = res[:, bass.ds(i, 1), :]
                dve.scalar_tensor_tensor(out=at, in0=y1[:, u:u + 1, :], scalar=gates[:, 0, bass.ds(i, 1)], in1=at,
                                         op0=ALU.mult, op1=ALU.add).then_inc(s["mix1"], 1)

            def mix2(i, u):
                dve.wait_ge(y2_in[u], turn(i, u) + 16)
                dve.wait_ge(s["mix1"], i + 1)
                at = res[:, bass.ds(i, 1), :]
                dve.scalar_tensor_tensor(out=at, in0=y2[:, u:u + 1, :], scalar=gates[:, 1, bass.ds(i, 1)], in1=at,
                                         op0=ALU.mult, op1=ALU.add).then_inc(s["mixed"], 1)

            def step_c(t, u):
                if within(t, 0):
                    b = u % 2
                    e = dve.value_load(block_e[0:1, bass.ds(t, 1)], min_val=0, max_val=E - 1)
                    reused(dve, "hid", t)
                    reused(dve, "y", t, U)
                    dve.tensor_copy(b2s[:, u % U, :], b2_bc[:, bass.ds(e * D, D)])
                    dve.tensor_copy(w1s[:, b, :], w1[:, bass.ds(e * F, F)])
                    dve.tensor_copy(b1s[:, b, :], b1c[:, bass.ds(e * FC, FC)]).then_inc(s["w1_copy"], 1)
                if within(t, FFN2):
                    n, b, b4 = t - FFN2, (u - FFN2) % 2, (u - FFN2) % U
                    dve.wait_ge(s["y_ps"], n + 1)
                    if not (isinstance(n, int) and n < U):
                        dve.wait_ge(y_out[b4], turn(n, b4))
                    dve.tensor_tensor(ysb[:, b4, :], pj[:, b * 512:b * 512 + P], b2s[:, b4, :],
                                      ALU.add).then_inc(s["y"], 1)

            for t in range(UC):
                if t < SORT_STAGES:
                    sort(1, [t])
                step_c(t, t)
            with groups(dve, UC, MIX0, UC) as t:
                for u in range(UC):
                    step_c(t + u, u)
            dve.wait_ge(s["gate_exp"], 2)
            then(dve.tensor_scalar(gates[:, 0, :], gate_e[:], 1.0, None, ALU.add), "gate1", 1)
            then(dve.reciprocal(gates[:, 0, :], gates[:, 0, :]), "gate2", 1)
            dve.tensor_tensor(gates[:, 1, :], gates[:, 0, :], gate_e[:], ALU.mult).then_inc(s["gates"], 1)
            dve.wait_ge(s["gates"], 1)
            dve.wait_ge(s["res"], NT)
            LAST = MIX0 + (MIX1 - MIX0) // UC * UC
            with groups(dve, MIX0, LAST, UC) as t:
                for u in range(UC):
                    mix1(t - (MIX0 - u), u % U)
                    step_c(t + u, u)
                    mix2(t - (MIX0 - u), u % U)
            for t in range(LAST, STEPS_C):
                if t < MIX1:
                    mix1(t - MIX0, t % U)
                step_c(t, t % UC)
                if t < MIX1:
                    mix2(t - MIX0, t % U)
            with groups(dve, MIX1 - MIX0, NT) as i:
                for u in range(U):
                    mix1(i + u, u)
                    mix2(i + u, u)


_INS = ["x", "L0_tok_weight", "L0_tok_mask_u", "L0_attn_W_DQ", "L0_attn_W_UQ", "L0_attn_W_QR", "L0_attn_W_DKV",
        "L0_attn_W_UK", "L0_attn_W_UV", "L0_attn_W_KR", "L0_attn_W_VR", "L0_attn_W_O", "L0_attn_q_ln_w",
        "L0_attn_kv_ln_w", "L0_attn_q_head_norm_w", "L0_attn_k_head_norm_w", "L0_ffn_ln_g", "L0_ffn_ln_b",
        "L0_ffn_w_r", "L0_ffn_b_r", "L0_ffn_W1", "L0_ffn_b1", "L0_ffn_W2", "L0_ffn_b2"]


def rope_constants(tokens):
    inv_freq = 1.0 / 500000.0 ** (np.arange(0, DR, 2, dtype=np.float32) / DR)
    freqs = np.outer(np.arange(tokens, dtype=np.float32), inv_freq)
    return np.concatenate([np.cos(freqs), np.cos(freqs), -np.sin(freqs), np.sin(freqs)], axis=1).astype(np.float32)


def kernel(**inputs):
    import concourse.bacc as _bacc
    from concourse.bass_utils import run_bass_kernel_spmd as _run

    nc = _bacc.Bacc("TRN2", target_bir_lowering=False, num_devices=1)
    arrays, args = {}, []
    for name in _INS:
        a = np.ascontiguousarray(inputs[name])
        arrays[f"in_{name}"] = a
        args.append(nc.dram_tensor(f"in_{name}", a.shape, mybir.dt.from_np(a.dtype), kind="ExternalInput").ap())
    table = rope_constants(inputs["x"].shape[1])
    arrays["rope_table"] = table
    args.append(nc.dram_tensor("rope_table", table.shape, F32, kind="ExternalInput").ap())
    shape = (*inputs["x"].shape, inputs["L0_tok_weight"].shape[1])
    args.append(nc.dram_tensor("out", shape, F32, kind="ExternalOutput").ap())
    attention_and_experts_kernel(nc, *args)
    return _run(nc, [arrays], core_ids=[0]).results[0]["out"]
```
